# Optimizing a Trainium2 kernel written in Bass

```python
import numpy as np
import jax
import jax.numpy as jnp

def _softmax(x, axis=-1):
    return jax.nn.softmax(x, axis=axis)

def _gelu(x):
    return jax.nn.gelu(x, approximate=True)

def _silu(x):
    return jax.nn.silu(x)

def _sigmoid(x):
    return jax.nn.sigmoid(x)

def _layernorm(x, axis=-1, eps=1e-05):
    m = jnp.mean(x, axis=axis, keepdims=True)
    v = jnp.var(x, axis=axis, keepdims=True)
    return (x - m) / jnp.sqrt(v + eps)

def _scatter_add(tgt, idx, src, axis=0):
    return tgt.at[idx].add(src)

def _segment_sum(src, seg, n):
    return jax.ops.segment_sum(src, seg, n)
kernel_name = 'mk_gnn_resnorm_d2_gnn_r32_02edcc'

def setup_inputs(seed: int=0):
    np.random.seed(seed)
    _w = jnp.asarray

    def _rec_inputs():
        import jax
        import jax.numpy as jnp
        _gk = jax.random.key(seed)
        x = -0.0006008 + 1.001 * jax.random.normal(jax.random.fold_in(_gk, 1), (50000, 256), jnp.float32)
        src = jax.random.randint(jax.random.fold_in(_gk, 2), (25000,), 0, 50000, jnp.int32)
        dst = jnp.minimum((50000 * jax.random.uniform(jax.random.fold_in(_gk, 3), (25000,)) ** 2.0).astype(jnp.int32), 49999)
        _o = jnp.argsort(dst, stable=True)
        src = src[_o]
        dst = dst[_o]
        edge_attr_20 = jax.random.uniform(jax.random.fold_in(_gk, 12), (25000, 20), jnp.float32, 0.0, 1)
        return (x, src, dst, edge_attr_20)
    x, src, dst, edge_attr_20 = _rec_inputs()

    def _L0_gnn_setup():
        import jax, jax.numpy as jnp
        import numpy as np
        N, E, HDIM, NG = (10000, 10000, 256, 20)
        BN_EPS = 1e-05
        key = jax.random.key(seed)
        ks = jax.random.split(key, 12)
        inp = {'x': jax.random.normal(ks[0], (N, HDIM), dtype=jnp.float32), 'rbf': jax.random.uniform(ks[1], (E, NG), dtype=jnp.float32), 'ei': jax.random.randint(ks[2], (2, E), 0, N, dtype=jnp.int64), 'Wf1': jax.random.normal(ks[3], (NG, HDIM), dtype=jnp.float32) / np.sqrt(NG), 'bf1': jnp.zeros((HDIM,), dtype=jnp.float32), 'Wf2': jax.random.normal(ks[4], (HDIM, HDIM), dtype=jnp.float32) / np.sqrt(HDIM), 'bf2': jnp.zeros((HDIM,), dtype=jnp.float32), 'Wu1': jax.random.normal(ks[5], (HDIM, HDIM), dtype=jnp.float32) / np.sqrt(HDIM), 'bu1': jnp.zeros((HDIM,), dtype=jnp.float32), 'Wu2': jax.random.normal(ks[6], (HDIM, HDIM), dtype=jnp.float32) / np.sqrt(HDIM), 'bu2': jnp.zeros((HDIM,), dtype=jnp.float32), 'gamma': jnp.ones((HDIM,), dtype=jnp.float32), 'beta': jnp.zeros((HDIM,), dtype=jnp.float32)}
        return inp
    _L0_gnn_all = _L0_gnn_setup()
    _L0_gnn_in = {k: v for k, v in _L0_gnn_all.items() if k in ('Wf1', 'bf1', 'Wf2', 'bf2', 'Wu1', 'bu1', 'Wu2', 'bu2', 'gamma', 'beta')}
    del _L0_gnn_all

    def _L1_gnn_setup():
        import jax, jax.numpy as jnp
        import numpy as np
        N_NODES = 10000
        N_EDGES = 10000
        D = 256
        key = jax.random.key(seed)
        k1, k2, k3, k4, k5 = jax.random.split(key, 5)
        x = jax.random.normal(k1, (N_NODES, D), dtype=jnp.float32)
        src = jax.random.randint(k2, (N_EDGES,), 0, N_NODES, dtype=jnp.int32)
        dst = jax.random.randint(k3, (N_EDGES,), 0, N_NODES, dtype=jnp.int32)
        s = 1.0 / np.sqrt(D)
        theta_w = jax.random.uniform(k4, (D, D), jnp.float32, -s, s)
        theta_b = jnp.zeros((D,), jnp.float32)
        phi_w = jax.random.uniform(k5, (D, D), jnp.float32, -s, s)
        phi_b = jnp.zeros((D,), jnp.float32)
        return {'x': x, 'src': src, 'dst': dst, 'theta_w': theta_w, 'theta_b': theta_b, 'phi_w': phi_w, 'phi_b': phi_b}
    _L1_gnn_all = _L1_gnn_setup()
    _L1_gnn_in = {k: v for k, v in _L1_gnn_all.items() if k in ('theta_w', 'theta_b', 'phi_w', 'phi_b')}
    del _L1_gnn_all
    return {'x': x, 'src': src, 'dst': dst, 'edge_attr_20': edge_attr_20, 'L0_gnn_Wf1': _L0_gnn_in['Wf1'], 'L0_gnn_bf1': _L0_gnn_in['bf1'], 'L0_gnn_Wf2': _L0_gnn_in['Wf2'], 'L0_gnn_bf2': _L0_gnn_in['bf2'], 'L0_gnn_Wu1': _L0_gnn_in['Wu1'], 'L0_gnn_bu1': _L0_gnn_in['bu1'], 'L0_gnn_Wu2': _L0_gnn_in['Wu2'], 'L0_gnn_bu2': _L0_gnn_in['bu2'], 'L0_gnn_gamma': _L0_gnn_in['gamma'], 'L0_gnn_beta': _L0_gnn_in['beta'], 'L1_gnn_theta_w': _L1_gnn_in['theta_w'], 'L1_gnn_theta_b': _L1_gnn_in['theta_b'], 'L1_gnn_phi_w': _L1_gnn_in['phi_w'], 'L1_gnn_phi_b': _L1_gnn_in['phi_b']}

def reference(x, src, dst, edge_attr_20, L0_gnn_Wf1, L0_gnn_bf1, L0_gnn_Wf2, L0_gnn_bf2, L0_gnn_Wu1, L0_gnn_bu1, L0_gnn_Wu2, L0_gnn_bu2, L0_gnn_gamma, L0_gnn_beta, L1_gnn_theta_w, L1_gnn_theta_b, L1_gnn_phi_w, L1_gnn_phi_b):
    import jax
    import jax.numpy as jnp

    def _L0_gnn_ref(x, rbf, Wf1, bf1, Wf2, bf2, Wu1, bu1, Wu2, bu2, gamma, beta, ei):
        import jax, jax.numpy as jnp
        import numpy as np
        N, E, HDIM, NG = (10000, 10000, 256, 20)
        BN_EPS = 1e-05
        row, col = (ei[0], ei[1])
        filt = jax.nn.silu(rbf @ Wf1 + bf1) @ Wf2 + bf2
        msg = x[col] * filt
        agg = jax.ops.segment_sum(msg, row, num_segments=x.shape[0])
        h = jax.nn.silu(agg @ Wu1 + bu1) @ Wu2 + bu2
        mean = jnp.mean(h, axis=0)
        var = jnp.mean(jnp.square(h - mean), axis=0)
        bn = gamma * (h - mean) * jax.lax.rsqrt(var + BN_EPS) + beta
        return x + bn

    def _L1_gnn_ref(x, src, dst, theta_w, theta_b, phi_w, phi_b):
        import jax, jax.numpy as jnp
        import numpy as np
        N_NODES = 10000
        N_EDGES = 10000
        D = 256
        x_src = x[src]
        x_dst = x[dst]
        theta_x = (x_dst - x_src) @ theta_w.T + theta_b
        phi_x = x_src @ phi_w.T + phi_b
        e = jax.nn.relu(theta_x + phi_x)
        out = jax.ops.segment_max(e, dst, num_segments=x.shape[0])
        return jnp.where(jnp.isfinite(out), out, 0.0)
    edge_index = jnp.stack([src, dst])
    x = _layernorm(x + _L0_gnn_ref(x, edge_attr_20, L0_gnn_Wf1, L0_gnn_bf1, L0_gnn_Wf2, L0_gnn_bf2, L0_gnn_Wu1, L0_gnn_bu1, L0_gnn_Wu2, L0_gnn_bu2, L0_gnn_gamma, L0_gnn_beta, edge_index), axis=-1)
    x = _layernorm(x + _L1_gnn_ref(x, src, dst, L1_gnn_theta_w, L1_gnn_theta_b, L1_gnn_phi_w, L1_gnn_phi_b), axis=-1)
    return x

_drawn_inputs = setup_inputs


def setup_inputs(seed=0):
    import zlib

    import numpy as np

    out = dict(_drawn_inputs(seed))
    spreads = {'L0_gnn_bf1': (0.0, 0.1),
     'L0_gnn_bf2': (0.0, 0.1),
     'L0_gnn_bu1': (0.0, 0.1),
     'L0_gnn_bu2': (0.0, 0.1),
     'L0_gnn_gamma': (1.0, 0.2),
     'L0_gnn_beta': (0.0, 0.1),
     'L1_gnn_theta_b': (0.0, 0.1),
     'L1_gnn_phi_b': (0.0, 0.1)}
    factors = {}
    for name, (base, spread) in spreads.items():
        noise = np.random.default_rng([zlib.crc32(name.encode()), seed]).standard_normal(out[name].shape)
        drawn = base * np.exp(spread * noise) if base else spread * noise
        out[name] = jnp.asarray(drawn.astype(out[name].dtype))
    for name, factor in factors.items():
        out[name] = (out[name] * factor).astype(out[name].dtype)
    return out
```

```python
from contextlib import ExitStack

import concourse.bass as bass
from concourse import mybir

F32 = mybir.dt.float32
BF16 = mybir.dt.bfloat16
I32 = mybir.dt.int32
U32 = mybir.dt.uint32
ALU = mybir.AluOpType
ACT = mybir.ActivationFunctionType

P = 128
SUB = 4
TE = SUB * P
LO = 256
ROUND = 1.5 * 2.0 ** 31
SKIP = 65536.0
EPS = 1e-5


class Tile:

    def __init__(self, c, unroll=1, k=None):
        self.c, self.unroll, self.k = c, unroll, k
        self.n = c if k is None else k * unroll + c

    def slot(self, m):
        return self.c % m

    def turn(self, m):
        return self.c // m if self.k is None else self.k * (self.unroll // m) + self.c // m


def pipeline(eng, count, unroll, stages):
    lags = max(lag for lag, _ in stages)

    def step(c, k=None):
        for lag, body in stages:
            if k is not None or 0 <= c - lag < count:
                body(Tile(c - lag, unroll, k))

    first = lags + max(unroll, 2)
    rounds = (count - first) // unroll
    for c in range(first):
        step(c)
    with eng.Fori(0, rounds) as k:
        for j in range(unroll):
            step(first + j, k)
    for c in range(first + rounds * unroll, count + lags):
        step(c)


def wait(eng, sem, value, most=None):
    if isinstance(value, int):
        if most is not None:
            value = min(value, most)
        if value <= 0:
            return
    eng.wait_ge(sem, value)


def build(nc, x, src, dst, attr, wf1, bf1, wf2, bf2, wu1, bu1, wu2, bu2, gamma, beta,
          theta_w, theta_b, phi_w, phi_b, out):
    N, D = x.shape
    E, G = attr.shape
    KC = D // P
    NT = -(-E // TE)
    COLS = NT * SUB
    EP = NT * TE
    PAD_KEY = N + 47
    assert N <= PAD_KEY < LO * LO and KC == 2 and D == LO
    W0 = 24
    OTHER0, KEY0 = G, G + 2
    W1 = 4
    OTHER1, KEY1 = 0, 2
    R = 10
    NN = N // (P * R)
    TAIL = N - NN * P * R
    assert TAIL <= P

    ctx = ExitStack()
    with ctx:
        def sb(name, shape, dt=F32):
            return ctx.enter_context(nc.sbuf_tensor(name, shape, dt))

        def ps(name, shape, dt=F32):
            return ctx.enter_context(nc.psum_tensor(name, shape, dt))

        def sem(name):
            return ctx.enter_context(nc.semaphore(name))

        sorted0 = nc.dram_tensor("sorted0", (EP + 1, W0), F32).ap()
        sorted1 = nc.dram_tensor("sorted1", (EP + 1, W1), F32).ap()
        d_tab = nc.dram_tensor("d_tab", (N, D), F32).ap()
        x1_tab = nc.dram_tensor("x1_tab", (N, D), F32).ap()

        iota_f = sb("iota_f", [P, LO])
        iota_b = sb("iota_b", [P, LO], BF16)
        row_id = sb("row_id", [P, 2])
        ident = sb("ident", [P, P])
        ident_b = sb("ident_b", [P, P], BF16)
        before = sb("before", [P, P])
        before_b = sb("before_b", [P, P], BF16)
        ones = sb("ones", [P, LO])
        zeros_b = sb("zeros_b", [P, TE], BF16)
        pad_row = sb("pad_row", [1, W0])

        wf1_s = sb("wf1_s", [G, D])
        wf2_s = sb("wf2_s", [P, KC, D])
        wu1_s = sb("wu1_s", [P, KC, D])
        wu2_s = sb("wu2_s", [P, KC, D])
        theta_n = sb("theta_n", [P, KC, D])
        phi_n = sb("phi_n", [P, KC, D])
        w_dst = sb("w_dst", [P, KC, D])
        w_src = sb("w_src", [P, KC, D])
        cols = sb("cols", [P, 6, KC])
        rows_b = sb("rows_b", [P, 3, D])
        z0_wide = sb("z0_wide", [P, KC, P])
        h0 = sb("h0", [P, D])
        shift = sb("shift", [P, D])
        bn_scale = sb("bn_scale", [P, D])
        bn_shift = sb("bn_shift", [P, D])
        bn_mean = sb("bn_mean", [P, D])
        bn_tmp = sb("bn_tmp", [P, D])
        bn_sum = sb("bn_sum", [P, 2, D])

        key_i = sb("key_i", [P, 2, COLS], I32)
        other_i = sb("other_i", [P, 2, COLS], I32)
        part_i = sb("part_i", [P, 2, COLS], I32)
        part_f = sb("part_f", [P, NT, 2, SUB])
        high_b = sb("high_b", [P, COLS], BF16)
        pay1 = sb("pay1", [P, COLS, W1])
        parts = sb("parts", [P, 2, 2, SUB])
        hot_hi = sb("hot_hi", [P, 2, SUB, LO], BF16)
        hot_lo = sb("hot_lo", [P, 2, SUB, LO], BF16)
        high_row = sb("high_row", [P, 2, TE], BF16)
        hot_hi_t = sb("hot_hi_t", [P, 2, 2, TE], BF16)
        earlier = sb("earlier", [P, 2, SUB, TE], BF16)
        tab_hi = sb("tab_hi", [P, 2, 2 * LO], BF16)
        tab_lo = sb("tab_lo", [P, 2, 2 * LO], BF16)
        cnt_s = sb("cnt_s", [P, 2, LO])
        incl = sb("incl", [P, 2, LO])
        tot = sb("tot", [P, 2])
        off = sb("off", [P, 2])
        base = sb("base", [P, 2, LO])
        place_f = sb("place_f", [P, 2, SUB])
        place_i = sb("place_i", [P, 2, SUB], I32)
        picked = sb("picked", [P, SUB, LO], BF16)
        pay_t = sb("pay_t", [P, 2, SUB, W0])

        edge = sb("edge", [P, 4, SUB, W0])
        ends_i = sb("ends_i", [P, 4, 2, SUB], I32)
        next_key = sb("next_key", [P, 4, SUB])
        tail_f = sb("tail_f", [P, 4, SUB])
        tail_i = sb("tail_i", [P, 4, SUB], I32)
        is_last = sb("is_last", [P, 4, SUB])
        goes_on = sb("goes_on", [P, SUB])
        key_row = sb("key_row", [P, 2, TE + 1])
        same = sb("same", [P, 2, TE])
        attr_t = sb("attr_t", [G, TE])
        gathered = sb("gathered", [P, 2, SUB, D])
        h1_xt = sb("h1_xt", [P, 4 * KC * TE])
        h1 = h1_xt[:, 0:2 * KC * TE].rearrange("p (s c e) -> p s c e", s=2, c=KC)
        xt = h1_xt[:, 2 * KC * TE:4 * KC * TE].rearrange("p (s c e) -> p s c e", s=2, c=KC)
        xt2 = h1
        attr_s = h1_xt[:, 0:COLS * G].rearrange("p (t g) -> p t g", g=G)
        msg = sb("msg", [P, KC, TE])
        agg = sb("agg", [P, 2, KC, TE])
        zt = sb("zt", [P, 2, KC, TE])
        d_rows = sb("d_rows", [P, 2, SUB, D])
        sq = sb("sq", [P, 2, SUB, D])
        acc_d = sb("acc_d", [P, SUB, D])
        acc_q = sb("acc_q", [P, SUB, D])
        node_x_all = sb("node_x_all", [P, 2 * R * D])
        node_d_all = sb("node_d_all", [P, 2 * R * D])
        node_x = node_x_all[:, :].rearrange("p (s r d) -> p s r d", s=2, r=R)
        node_d = node_d_all[:, :].rearrange("p (s r d) -> p s r d", s=2, r=R)
        pay0 = node_x_all[:, 0:COLS * W0].rearrange("p (t w) -> p t w", w=W0)
        gathered2 = node_d_all[:, 0:4 * SUB * D].rearrange("p (s g d) -> p s g d", s=4, g=SUB)
        stats = sb("stats", [P, 2, R, 6])
        moment = sb("moment", [P, 2, 5, R])
        spread = sb("spread", [P, 2, 2, R])
        sd = sb("sd", [P, 2, 2, R])
        inv = sb("inv", [P, 2, 2, R])
        neg = sb("neg", [P, 2, 2, R])

        bank = [ps(f"bank{i}", [P, TE]) for i in range(8)]

        s_pad = sem("padding_set")
        s_const = sem("constants_made")
        s_const_v = sem("constants_cast")
        s_key_in = sem("keys_loaded")
        s_attr_in = sem("attributes_loaded")
        s_w_in = sem("weights_loaded")
        s_zero = sem("zeros_made")
        s_fill = sem("d_tab_filled")
        s_prep = sem("vector_setup_step")
        s_w2 = sem("phi_minus_theta")
        s_wt = sem("weights_transposed")
        s_wt_used = sem("weights_copied")
        s_z0 = sem("z0_ready")
        s_h0 = sem("h0_in_psum")
        s_h0_v = sem("h0_step")
        s_pay = sem("payload_step")

        def sort_sems(a):
            return {k: sem(f"{k}{a}") for k in (
                "split", "parts_c", "hot_c", "counted", "prefix", "offset", "base_in", "parts_s", "hot_s",
                "high_bank", "high_ready", "ready", "tab_hi_ready", "tab_ready", "added", "looked_up",
                "place_found", "place_ready", "pay_ready", "pay_all")} | {
                    "scattered": [sem(f"scattered{a}_{i}") for i in range(2)]}

        sort_s = [sort_sems(0), sort_sems(1)]

        def layer_sems(a, names):
            return {k: sem(f"{k}{a}") for k in names} | {
                "edges_in": [sem(f"edges_in{a}_{i}") for i in range(4)],
                "gathered": [sem(f"gathered{a}_{i}") for i in range(2)],
                "scattered": [sem(f"rows_scattered{a}_{i}") for i in range(2)]}

        l0 = layer_sems(0, ("key_bank", "key_row", "attr_bank", "attr_t", "h1_bank", "h1", "xt_bank", "xt",
                            "filt_bank", "msg", "same", "agg", "z_bank", "z", "h_bank", "d", "sq", "stats",
                            "tails", "tail_step", "ends"))
        l1 = layer_sems(1, ("key_bank", "key_row", "xt_bank", "xt", "xt2_bank", "xt2", "e_bank", "e", "same",
                            "best", "best_bank", "sum", "stats", "mv", "spread", "sd", "inv", "neg", "rows",
                            "tails", "tail_step", "ends"))
        s_sum = sem("column_sums")
        s_bn = sem("batch_norm_step")
        s_bn_sd = sem("batch_norm_sd")
        s_bn_v = sem("batch_norm_variance")
        nd = {k: sem(f"node_{k}") for k in ("step", "stats", "mv", "spread", "sd", "inv", "neg", "rows")}
        nd_in = [sem(f"node_in_{i}") for i in range(2)]
        nd_out = [sem(f"node_out_{i}") for i in range(2)]
        s_pad_row = sem("pad_rows_written")

        sorted_rows = [t[0:EP, :].rearrange("(t s p) w -> t p s w", s=SUB, p=P) for t in (sorted0, sorted1)]
        next_rows = [t[1:EP + 1, :].rearrange("(t s p) w -> t p s w", s=SUB, p=P) for t in (sorted0, sorted1)]

        def node_tiles(t):
            return t[0:NN * P * R, :].rearrange("(t p r) d -> t p r d", p=P, r=R)

        WT = [W0, W1]
        KEY = [KEY0, KEY1]
        OTHER = [OTHER0, OTHER1]
        FULL = E // COLS
        REST = E - FULL * COLS

        def halves(a):
            return part_i[:, a, :].rearrange("p (t s) -> p t s", s=SUB)

        block = ctx.enter_context(nc.Block())

        @block.sync
        def _(sp):
            sp.wait_ge(s_pad, 1)
            for tile, slot, arr in ((key_i, 0, src), (key_i, 1, dst), (other_i, 0, dst), (other_i, 1, src)):
                sp.dma_start(tile[0:FULL, slot, :],
                             arr[0:FULL * COLS].rearrange("(p t) -> p t", t=COLS)).then_inc(s_key_in, 16)
                sp.dma_start(tile[FULL:FULL + 1, slot, 0:REST],
                             arr[FULL * COLS:E].rearrange("(p t) -> p t", p=1)).then_inc(s_key_in, 16)
            sp.dma_start(attr_s[0:FULL, :, :],
                         attr[0:FULL * COLS, :].rearrange("(p t) g -> p t g", t=COLS)).then_inc(s_attr_in, 16)
            sp.dma_start(attr_s[FULL:FULL + 1, 0:REST, :],
                         attr[FULL * COLS:E, :].rearrange("(p t) g -> p t g", p=1)).then_inc(s_attr_in, 16)
            sp.dma_start(wf1_s[:, :], wf1).then_inc(s_w_in, 16)
            for tile, w in ((wf2_s, wf2), (wu1_s, wu1), (wu2_s, wu2), (theta_n, theta_w), (phi_n, phi_w)):
                sp.dma_start(tile[:, :, :], w.rearrange("(c p) d -> p c d", p=P)).then_inc(s_w_in, 16)
            for j, b in enumerate((bf1, bf2, bu1, theta_b, phi_b)):
                sp.dma_start(cols[:, j, :], b.rearrange("(c p) -> p c", p=P),
                             allow_slow_non_contiguous=True).then_inc(s_w_in, 16)
            for j, b in enumerate((bu2, gamma, beta)):
                sp.dma_start(rows_b[:, j, :],
                             b.rearrange("(a d) -> a d", a=1).to_broadcast([P, D])).then_inc(s_w_in, 16)
            sp.wait_ge(s_const, 8)
            sp.dma_start(sorted0[EP:EP + 1, :], pad_row[:, :]).then_inc(s_pad_row, 16)
            sp.dma_start(sorted1[EP:EP + 1, :], pad_row[:, 0:W1]).then_inc(s_pad_row, 16)
            sp.wait_ge(s_zero, 1)
            with sp.Fori(0, NN) as t:
                sp.dma_start(node_tiles(d_tab)[t], node_d[:, 0, :, :]).then_inc(s_fill, 16)
            sp.dma_start(d_tab[NN * P * R:N, :], node_d[0:TAIL, 0, 0, :]).then_inc(s_fill, 16)

            def load_edges(a, ly):
                def body(t):
                    s = t.slot(4)
                    wait(sp, ly["key_bank"], t.n - 3)
                    wait(sp, ly["tails"], t.n - 3)
                    if a == 0:
                        wait(sp, ly["attr_bank"], t.n - 3)
                    wait(sp, ly["ends"], t.n - 3)
                    if t.k is None and t.c == 0:
                        for i in range(2):
                            sp.wait_ge(sort_s[a]["scattered"][i], 16 * SUB * ((NT + 1 - i) // 2))
                        sp.wait_ge(s_pad_row, 32)
                    sp.dma_start(edge[:, s, :, 0:WT[a]], sorted_rows[a][t.n]).then_inc(ly["edges_in"][s], 16)
                    sp.dma_start(next_key[:, s, :], next_rows[a][t.n][:, :, KEY[a]],
                                 allow_slow_non_contiguous=True).then_inc(ly["edges_in"][s], 16)
                return body

            pipeline(sp, NT, 4, [(0, load_edges(0, l0))])

            def load_nodes(t):
                s = t.slot(2)
                wait(sp, nd_out[s], t.turn(2) * 32)
                sp.dma_start(node_x[:, s, :, :], node_tiles(x)[t.n]).then_inc(nd_in[s], 16)
                sp.dma_start(node_d[:, s, :, :], node_tiles(d_tab)[t.n]).then_inc(nd_in[s], 16)

            def store_nodes(t):
                s = t.slot(2)
                sp.wait_ge(nd["rows"], (t.n + 1) * 1)
                sp.dma_start(node_tiles(x1_tab)[t.n], node_d[:, s, :, :]).then_inc(nd_out[s], 16)
                sp.dma_start(node_tiles(out)[t.n], node_x[:, s, :, :]).then_inc(nd_out[s], 16)

            sp.wait_ge(s_fill, 16 * (NN + 1))
            for i in range(2):
                sp.wait_ge(l0["scattered"][i], 16 * SUB * ((NT + 1 - i) // 2))
            pipeline(sp, NN, 2, [(0, load_nodes), (1, store_nodes)])
            s = NN % 2
            sp.wait_ge(nd_out[s], (NN // 2) * 32)
            sp.dma_start(node_x[0:TAIL, s, 0, :], x[NN * P * R:N, :]).then_inc(nd_in[s], 16)
            sp.dma_start(node_d[0:TAIL, s, 0, :], d_tab[NN * P * R:N, :]).then_inc(nd_in[s], 16)
            sp.wait_ge(nd["rows"], NN + 1)
            sp.dma_start(x1_tab[NN * P * R:N, :], node_d[0:TAIL, s, 0, :]).then_inc(nd_out[s], 16)
            sp.dma_start(out[NN * P * R:N, :], node_x[0:TAIL, s, 0, :]).then_inc(nd_out[s], 16)
            pipeline(sp, NT, 4, [(0, load_edges(1, l1))])

        @block.gpsimd
        def _(pool):
            pool.memset(ones[:, :], 1.0).then_inc(s_const, 1)
            pool.memset(ident[:, :], 0.0).then_inc(s_const, 1)
            pool.memset(before[:, :], 1.0).then_inc(s_const, 1)
            pool.memset(pad_row[:, :], SKIP).then_inc(s_const, 1)
            pool.iota(iota_f[:, :], pattern=[[1, LO]], base=0, channel_multiplier=0,
                      allow_small_or_imprecise_dtypes=True).then_inc(s_const, 1)
            pool.iota(row_id[:, :], pattern=[[P, 2]], base=0, channel_multiplier=1,
                      allow_small_or_imprecise_dtypes=True).then_inc(s_const, 1)
            pool.wait_ge(s_const, 6)
            pool.affine_select(out=ident[:, :], in_=ident[:, :], compare_op=ALU.not_equal, fill=1.0, base=0,
                               pattern=[[-1, P]], channel_multiplier=1).then_inc(s_const, 1)
            pool.affine_select(out=before[:, :], in_=before[:, :], compare_op=ALU.is_gt, fill=0.0, base=0,
                               pattern=[[1, P]], channel_multiplier=-1).then_inc(s_const, 1)

            def scatter_payload(a, so, table):
                def body(t):
                    s = t.slot(2)
                    pool.wait_ge(so["pay_ready"], t.n + 1)
                    pool.wait_ge(so["place_ready"], t.n + 1)
                    pool.nop(nofuse=True)
                    for g in range(SUB):
                        pool.indirect_dma_start(
                            out=table, out_offset=bass.IndirectOffsetOnAxis(
                                ap=place_i[:, s, g:g + 1].bitcast(U32), axis=0),
                            in_=pay_t[:, s, g, 0:WT[a]], in_offset=None).then_inc(so["scattered"][s], 16)
                return body

            def gather(idx, table, to, done):
                for g in range(SUB):
                    pool.indirect_dma_start(
                        out=to[:, g, :], out_offset=None, in_=table,
                        in_offset=bass.IndirectOffsetOnAxis(ap=idx[g], axis=0)).then_inc(done, 16)

            def scatter_tails(table, ready, rows, sems):
                def body(t):
                    s = t.slot(2)
                    pool.wait_ge(ready[0], ready[1] * (t.n + 1))
                    pool.nop(nofuse=True)
                    for g in range(SUB):
                        pool.indirect_dma_start(
                            out=table, out_offset=bass.IndirectOffsetOnAxis(
                                ap=tail_i[:, t.slot(4), g:g + 1].bitcast(U32), axis=0),
                            in_=rows[:, s, g, :], in_offset=None, bounds_check=N - 1,
                            oob_is_err=False).then_inc(sems[s], 16)
                return body

            pipeline(pool, NT, 2, [(0, scatter_payload(0, sort_s[0], sorted0))])

            def gather0(t):
                s = t.slot(2)
                wait(pool, l0["xt_bank"], 2 * (t.n - 1))
                pool.wait_ge(l0["ends"], t.n + 1)
                pool.nop(nofuse=True)
                gather([ends_i[:, t.slot(4), 0, g:g + 1].bitcast(U32) for g in range(SUB)], x,
                       gathered[:, s], l0["gathered"][s])

            pool.wait_ge(s_fill, 16 * (NN + 1))
            pipeline(pool, NT, 4, [(0, gather0), (3, scatter_tails(d_tab, (l0["d"], 2), d_rows, l0["scattered"]))])
            pipeline(pool, NT, 2, [(0, scatter_payload(1, sort_s[1], sorted1))])

            def gather1(t):
                s = t.slot(2)
                wait(pool, l1["xt_bank"], 2 * (t.n - 1))
                wait(pool, l1["sum"], 2 * (t.n - 3))
                pool.wait_ge(l1["ends"], t.n + 1)
                pool.nop(nofuse=True)
                q = t.slot(4)
                gather([ends_i[:, q, 0, g:g + 1].bitcast(U32) for g in range(SUB)], x1_tab,
                       gathered[:, s], l1["gathered"][s])
                gather([ends_i[:, q, 1, g:g + 1].bitcast(U32) for g in range(SUB)], x1_tab,
                       gathered2[:, q], l1["gathered"][s])

            for s in range(2):
                pool.wait_ge(nd_out[s], 32 * ((NN + 1 + 1 - s) // 2))
            pipeline(pool, NT, 4, [(0, gather1), (3, scatter_tails(out, (l1["rows"], 1), sq, l1["scattered"]))])
            for i in range(2):
                pool.wait_ge(l1["scattered"][i], 16 * SUB * ((NT + 1 - i) // 2))

        tab_bank = bank[0]
        off_bank = bank[3]
        high_bank = [bank[1 + i][:, 0:TE // 2].bitcast(BF16) for i in range(2)]

        @block.tensor
        def _(pe):
            def sort(a, so):
                pe.matmul(tab_bank[:, :], zeros_b[:, 0:P], zeros_b[:, :], start=True, stop=False, skip_group_check=True)

                def add_counts(s, last_sem):
                    for g in range(SUB):
                        for c in range(2):
                            mm = pe.matmul(tab_bank[:, c * LO:(c + 1) * LO], hot_hi[:, s, g, c * P:(c + 1) * P],
                                           hot_lo[:, s, g, :], start=False, stop=(g == SUB - 1 and c == 1),
                                           skip_group_check=True)
                    mm.then_inc(last_sem, 1)

                def count(t):
                    pe.wait_ge(so["hot_c"], t.n + 1)
                    add_counts(t.slot(2), so["counted"])

                pipeline(pe, NT, 2, [(0, count)])
                pe.wait_ge(so["prefix"], 4)
                pe.matmul(off_bank[:, 0:2], before[:, :], tot[:, :], start=True, stop=False, skip_group_check=True)
                pe.matmul(off_bank[:, 1:2], ones[:, 0:P], tot[:, 0:1], start=False, stop=True,
                          skip_group_check=True).then_inc(so["offset"], 1)
                pe.wait_ge(so["prefix"], 7)
                pe.matmul(tab_bank[:, 0:LO], ident[:, :], base[:, 0, :], start=True, stop=False, skip_group_check=True)
                pe.matmul(tab_bank[:, LO:2 * LO], ident[:, :], base[:, 1, :], start=False, stop=False,
                          skip_group_check=True).then_inc(so["base_in"], 1)

                def high_rows(t):
                    wait(pe, so["high_ready"], t.n - 1)
                    for g in range(SUB):
                        mm = pe.transpose(high_bank[t.slot(2)][:, g * P:(g + 1) * P],
                                          high_b[:, bass.ds(t.n * SUB + g, 1)].to_broadcast([P, P]), ident_b[:, :])
                    mm.then_inc(so["high_bank"], 1)

                def look_up(t):
                    s = t.slot(2)
                    pe.wait_ge(so["tab_ready"], t.n + 1)
                    pe.wait_ge(so["hot_s"], t.n + 1)
                    add_counts(s, so["added"])
                    pe.wait_ge(so["ready"], t.n + 1)
                    wait(pe, so["place_found"], t.n - 1)
                    for g in range(SUB):
                        to = bank[4 + 2 * s + g // 2][:, (g % 2) * LO:(g % 2 + 1) * LO]
                        for c in range(2):
                            hot = hot_hi_t[:, s, c, g * P:(g + 1) * P]
                            pe.matmul(to, hot, tab_hi[:, s, c * LO:(c + 1) * LO], start=(c == 0), stop=False)
                            pe.matmul(to, hot, tab_lo[:, s, c * LO:(c + 1) * LO], start=False, stop=False)
                        for e in range(g + 1):
                            mm = pe.matmul(to, earlier[:, s, e, g * P:(g + 1) * P], hot_lo[:, s, e, :],
                                           start=False, stop=(e == g))
                    mm.then_inc(so["looked_up"], 1)

                pipeline(pe, NT, 2, [(0, high_rows), (1, look_up)])

            pe.wait_ge(s_const, 8)
            pe.wait_ge(s_const_v, 5)
            pe.wait_ge(s_w_in, 16 * 14)
            pe.wait_ge(s_w2, 1)
            for j, w in enumerate((theta_n, phi_n)):
                for c in range(KC):
                    for o in range(KC):
                        mm = pe.transpose(bank[1 + 2 * j + c][:, o * P:(o + 1) * P], w[:, o, c * P:(c + 1) * P],
                                          ident[:, :])
            mm.then_inc(s_wt, 1)
            pe.wait_ge(s_z0, 1)
            for c in range(KC):
                mm = pe.matmul(bank[5][:, 0:D], z0_wide[:, c, :], wu2_s[:, c, :], start=(c == 0), stop=(c == KC - 1))
            mm.then_inc(s_h0, 1)
            pe.wait_ge(s_wt_used, 4)
            pe.wait_ge(s_h0_v, 2)
            sort(0, sort_s[0])
            pe.wait_ge(sort_s[0]["place_found"], NT)

            L = l0

            def keys_attrs(t):
                wait(pe, L["msg"], 2 * (t.n - 1))
                wait(pe, L["key_row"], t.n)
                pe.wait_ge(L["edges_in"][t.slot(4)], 32 * t.turn(4) + 32)
                for g in range(SUB):
                    mm = pe.transpose(bank[4][:, g * P:(g + 1) * P],
                                      edge[:, t.slot(4), g, KEY0:KEY0 + 1].to_broadcast([P, P]), ident[:, :])
                mm.then_inc(L["key_bank"], 1)
                wait(pe, L["attr_t"], t.n)
                for g in range(SUB):
                    mm = pe.transpose(bank[5][0:G, g * P:(g + 1) * P], edge[:, t.slot(4), g, 0:G], ident[:, :])
                mm.then_inc(L["attr_bank"], 1)

            def update_in(t):
                s = t.slot(2)
                pe.wait_ge(L["agg"], 2 * (t.n + 1))
                for o in range(KC):
                    wait(pe, L["z"], 2 * (t.n - 1) + o + 1)
                    if o == 0:
                        wait(pe, L["h1"], 2 * (t.n + 2), 2 * NT)
                    else:
                        pe.wait_ge(L["xt"], 2 * t.n + 1)
                    for c in range(KC):
                        mm = pe.matmul(bank[o][:, :], wu1_s[:, c, o * P:(o + 1) * P], agg[:, s, c, :],
                                       start=(c == 0), stop=(c == KC - 1))
                    mm.then_inc(L["z_bank"], 1)

            def update_out(t):
                s = t.slot(2)
                pe.wait_ge(L["z"], 2 * (t.n + 1))
                for j in range(2):
                    wait(pe, L["d"], 2 * (t.n - 1) + j + 1)
                    if j == 0:
                        wait(pe, L["xt"], 2 * (t.n + 2), 2 * NT)
                    else:
                        wait(pe, L["msg"], 2 * (t.n + 1) + 1, 2 * NT)
                    for g in range(2 * j, 2 * j + 2):
                        for c in range(KC):
                            mm = pe.matmul(bank[2 + j][:, (g % 2) * D:(g % 2 + 1) * D],
                                           zt[:, s, c, g * P:(g + 1) * P], wu2_s[:, c, :],
                                           start=(c == 0), stop=(c == KC - 1))
                    mm.then_inc(L["h_bank"], 1)

            def filter_in(t):
                pe.wait_ge(L["attr_t"], t.n + 1)
                for o in range(KC):
                    if o == 0:
                        wait(pe, L["h1"], 2 * (t.n - 1) + 1)
                    else:
                        wait(pe, L["z"], 2 * (t.n - 2) + 1)
                    pe.matmul(bank[6 if o == 0 else 0][:, :], wf1_s[:, o * P:(o + 1) * P], attr_t[:, :],
                              start=True, stop=True).then_inc(L["h1_bank"], 1)

            def filter_out(t):
                s = t.slot(2)
                pe.wait_ge(L["gathered"][s], 64 * t.turn(2) + 64)
                for c in range(KC):
                    if c == 0:
                        wait(pe, L["z"], 2 * t.n)
                    else:
                        wait(pe, L["d"], 2 * (t.n - 2) + 1)
                    for g in range(SUB):
                        mm = pe.transpose(bank[1 + c][:, g * P:(g + 1) * P],
                                          gathered[:, s, g, c * P:(c + 1) * P], ident[:, :])
                    mm.then_inc(L["xt_bank"], 1)
                pe.wait_ge(L["h1"], 2 * (t.n + 1))
                for o in range(KC):
                    if o == 0:
                        wait(pe, L["d"], 2 * (t.n - 1))
                    else:
                        wait(pe, L["key_row"], t.n + 2, NT)
                    for c in range(KC):
                        mm = pe.matmul(bank[3 + o][:, :], wf2_s[:, c, o * P:(o + 1) * P], h1[:, s, c, :],
                                       start=(c == 0), stop=(c == KC - 1))
                    mm.then_inc(L["filt_bank"], 1)

            pipeline(pe, NT, 4, [(0, keys_attrs), (2, update_in), (3, update_out), (0, filter_in), (1, filter_out)])

            pe.wait_ge(L["stats"], NT)
            for j, acc in enumerate((acc_d, acc_q)):
                for g in range(SUB):
                    mm = pe.matmul(bank[7][:, j * D:(j + 1) * D], ones[:, 0:P], acc[:, g, :],
                                   start=(g == 0), stop=(g == SUB - 1))
            mm.then_inc(s_sum, 1)
            pe.wait_ge(s_bn, 1)
            sort(1, sort_s[1])
            pe.wait_ge(sort_s[1]["place_found"], NT)

            M = l1

            def edge_rows(t):
                s = t.slot(2)
                pe.wait_ge(M["gathered"][s], 128 * t.turn(2) + 128)
                for c in range(KC):
                    wait(pe, M["xt"], 2 * (t.n - 1) + c + 1)
                    for g in range(SUB):
                        mm = pe.transpose(bank[1 + c][:, g * P:(g + 1) * P],
                                          gathered[:, s, g, c * P:(c + 1) * P], ident[:, :])
                    mm.then_inc(M["xt_bank"], 1)
                for c in range(KC):
                    wait(pe, M["xt2"], 2 * (t.n - 1) + c + 1)
                    for g in range(SUB):
                        mm = pe.transpose(bank[3 + c][:, g * P:(g + 1) * P],
                                          gathered2[:, t.slot(4), g, c * P:(c + 1) * P], ident[:, :])
                    mm.then_inc(M["xt2_bank"], 1)
                wait(pe, M["sum"], 2 * (t.n - 2) + 1)
                wait(pe, M["key_row"], t.n)
                for g in range(SUB):
                    mm = pe.transpose(bank[7][:, g * P:(g + 1) * P],
                                      edge[:, t.slot(4), g, KEY1:KEY1 + 1].to_broadcast([P, P]), ident[:, :])
                mm.then_inc(M["key_bank"], 1)

            def edge_mlp(t):
                s = t.slot(2)
                pe.wait_ge(M["xt"], 2 * (t.n + 1))
                pe.wait_ge(M["xt2"], 2 * (t.n + 1))
                for o in range(KC):
                    wait(pe, M["e"], 2 * (t.n - 1) + o + 1)
                    for c in range(KC):
                        pe.matmul(bank[5 + o][:, :], w_dst[:, c, o * P:(o + 1) * P], xt2[:, s, c, :],
                                  start=(c == 0), stop=False)
                        mm = pe.matmul(bank[5 + o][:, :], w_src[:, c, o * P:(o + 1) * P], xt[:, s, c, :],
                                       start=False, stop=(c == KC - 1))
                    mm.then_inc(M["e_bank"], 1)

            def best_rows(t):
                s = t.slot(2)
                pe.wait_ge(M["best"], 2 * (t.n + 1))
                for j in range(2):
                    wait(pe, M["sum"], 2 * (t.n - 1) + j + 1)
                    if j == 0:
                        wait(pe, M["key_row"], t.n + 2, NT)
                    for g in range(2 * j, 2 * j + 2):
                        for c in range(KC):
                            mm = pe.transpose(bank[7 if j == 0 else 0][:, (g % 2) * D + c * P:(g % 2) * D + (c + 1) * P],
                                              agg[:, s, c, g * P:(g + 1) * P], ident[:, :])
                    mm.then_inc(M["best_bank"], 1)

            pipeline(pe, NT, 4, [(2, best_rows), (0, edge_rows), (1, edge_mlp)])

        @block.scalar
        def _(act):
            act.wait_ge(s_w_in, 16 * 14)
            act.wait_ge(s_const, 8)
            for c in range(KC):
                mm = act.activation(z0_wide[:, c, :], before[:, :], ACT.Silu, scale=0.0, bias=cols[:, 2, c:c + 1])
            mm.then_inc(s_z0, 1)
            act.wait_ge(s_wt, 1)
            for j, w in enumerate((w_dst, w_src)):
                for c in range(KC):
                    act.copy(w[:, c, :], bank[1 + 2 * j + c][:, 0:D]).then_inc(s_wt_used, 1)
            act.wait_ge(s_attr_in, 32)
            act.copy(pay0[:, :, 0:G], attr_s[:, :, :]).then_inc(s_pay, 1)

            def sort(a, so, pay):
                def high_copy(t):
                    s = t.slot(2)
                    act.wait_ge(so["high_bank"], t.n + 1)
                    wait(act, so["ready"], t.n - 1)
                    act.copy(high_row[:, s, :], high_bank[s]).then_inc(so["high_ready"], 1)

                def lay_out(t):
                    s = t.slot(2)
                    wait(act, so["scattered"][s], 64 * t.turn(2))
                    act.copy(pay_t[:, s, :, 0:WT[a]],
                             pay[:, bass.ds(t.n * SUB, SUB), :]).then_inc(so["pay_ready"], 1)

                act.wait_ge(so["pay_all"], 3)
                pipeline(act, NT, 2, [(0, high_copy), (1, lay_out)])

            act.wait_ge(s_pay, 1)
            sort(0, sort_s[0], pay0)

            L = l0

            def keys_attrs(t):
                s = t.slot(2)
                wait(act, L["same"], t.n - 1)
                if not (t.k is None and t.c == 0):
                    act.wait_ge(L["key_row"], t.n)
                    act.copy(key_row[:, s, 0:1], key_row[:, 1 - s, TE:TE + 1])
                act.wait_ge(L["key_bank"], t.n + 1)
                act.copy(key_row[:, s, 1:TE + 1], bank[4][:, :]).then_inc(L["key_row"], 1)
                act.wait_ge(L["attr_bank"], t.n + 1)
                act.copy(attr_t[:, :], bank[5][0:G, :]).then_inc(L["attr_t"], 1)

            def silu_z(t):
                s = t.slot(2)
                wait(act, L["h_bank"], 2 * (t.n - 1))
                for o in range(KC):
                    act.wait_ge(L["z_bank"], 2 * t.n + o + 1)
                    act.activation(zt[:, s, o, :], bank[o][:, :], ACT.Silu, bias=cols[:, 2, o:o + 1]).then_inc(L["z"], 1)

            def squares(t):
                s = t.slot(2)
                wait(act, L["stats"], t.n - 1)
                for g in range(SUB):
                    if g % 2 == 0:
                        act.wait_ge(L["d"], 2 * t.n + g // 2 + 1)
                    act.activation(sq[:, s, g, :], d_rows[:, s, g, :], ACT.Square,
                                   scale=is_last[:, t.slot(4), g:g + 1]).then_inc(L["sq"], 1)

            def silu_h1(t):
                s = t.slot(2)
                wait(act, L["filt_bank"], 2 * (t.n - 1))
                for o in range(KC):
                    act.wait_ge(L["h1_bank"], 2 * t.n + o + 1)
                    act.activation(h1[:, s, o, :], bank[6 if o == 0 else 0][:, :], ACT.Silu,
                                   bias=cols[:, 0, o:o + 1]).then_inc(L["h1"], 1)

            def copy_xt(t):
                s = t.slot(2)
                wait(act, L["msg"], 2 * (t.n - 1))
                for c in range(KC):
                    act.wait_ge(L["xt_bank"], 2 * t.n + c + 1)
                    act.copy(xt[:, s, c, :], bank[1 + c][:, :]).then_inc(L["xt"], 1)

            pipeline(act, NT, 4, [(0, keys_attrs), (2, silu_z), (3, squares), (0, silu_h1), (1, copy_xt)])

            act.wait_ge(s_bn_v, 1)
            act.activation(bn_tmp[:, :], bn_tmp[:, :], ACT.Sqrt).then_inc(s_bn_sd, 1)

            def roots(t, rows=P, r=R):
                s = t.slot(2)
                act.wait_ge(nd["spread"], t.n + 1)
                act.activation(sd[0:rows, s, :, 0:r], spread[0:rows, s, :, 0:r], ACT.Sqrt).then_inc(nd["sd"], 1)

            def norm_rows(t, rows=P, r=R):
                s = t.slot(2)
                act.wait_ge(nd["neg"], t.n + 1)
                for j in range(r):
                    act.activation(node_x[0:rows, s, j, :], node_d[0:rows, s, j, :], ACT.Identity,
                                   scale=inv[0:rows, s, 1, j:j + 1], bias=neg[0:rows, s, 1, j:j + 1])
                for j in range(r):
                    mm = act.activation(node_d[0:rows, s, j, :], node_d[0:rows, s, j, :], ACT.Identity,
                                        scale=inv[0:rows, s, 0, j:j + 1], bias=neg[0:rows, s, 0, j:j + 1])
                mm.then_inc(nd["rows"], 1)

            pipeline(act, NN, 2, [(0, roots), (0, norm_rows)])
            roots(Tile(NN), TAIL, 1)
            norm_rows(Tile(NN), TAIL, 1)
            sort(1, sort_s[1], pay1)

            M = l1

            def best_norm(t):
                s = t.slot(2)
                act.wait_ge(M["spread"], t.n + 1)
                act.activation(sd[:, s, 0, 0:SUB], spread[:, s, 0, 0:SUB], ACT.Sqrt).then_inc(M["sd"], 1)
                act.wait_ge(M["neg"], t.n + 1)
                wait(act, M["scattered"][s], 64 * t.turn(2))
                for g in range(SUB):
                    mm = act.activation(sq[:, s, g, :], d_rows[:, s, g, :], ACT.Identity,
                                        scale=inv[:, s, 0, g:g + 1], bias=neg[:, s, 0, g:g + 1])
                mm.then_inc(M["rows"], 1)

            def copies(t):
                s = t.slot(2)
                wait(act, M["e_bank"], 2 * (t.n - 1))
                for c in range(KC):
                    act.wait_ge(M["xt_bank"], 2 * t.n + c + 1)
                    act.copy(xt[:, s, c, :], bank[1 + c][:, :]).then_inc(M["xt"], 1)
                for c in range(KC):
                    act.wait_ge(M["xt2_bank"], 2 * t.n + c + 1)
                    act.copy(xt2[:, s, c, :], bank[3 + c][:, :]).then_inc(M["xt2"], 1)
                wait(act, M["same"], t.n - 1)
                if not (t.k is None and t.c == 0):
                    act.wait_ge(M["key_row"], t.n)
                    act.copy(key_row[:, s, 0:1], key_row[:, 1 - s, TE:TE + 1])
                act.wait_ge(M["key_bank"], t.n + 1)
                act.copy(key_row[:, s, 1:TE + 1], bank[7][:, :]).then_inc(M["key_row"], 1)

            def relu_e(t):
                s = t.slot(2)
                wait(act, M["best"], 2 * (t.n - 1))
                for o in range(KC):
                    act.wait_ge(M["e_bank"], 2 * t.n + o + 1)
                    act.activation(zt[:, s, o, :], bank[5 + o][:, :], ACT.Relu, bias=cols[:, 5, o:o + 1]).then_inc(M["e"], 1)

            pipeline(act, NT, 4, [(0, copies), (2, best_norm), (1, relu_e)])

        @block.vector
        def _(dve):
            dve.memset(key_i[:, :, :], PAD_KEY)
            dve.memset(attr_s[:, :, :], 0.0)
            dve.memset(other_i[:, :, :], 0).then_inc(s_pad, 1)
            dve.memset(node_d[:, 0, :, :], 0.0).then_inc(s_zero, 1)
            dve.memset(zeros_b[:, :], 0.0).then_inc(s_const_v, 1)
            dve.memset(acc_d[:, :, :], 0.0)
            dve.memset(acc_q[:, :, :], 0.0)
            dve.memset(pay0[:, :, G:W0], 0.0)
            dve.memset(key_row[:, 0, 0:1], -1.0).then_inc(s_prep, 1)
            dve.wait_ge(s_const, 8)
            dve.tensor_copy(iota_b[:, :], iota_f[:, :]).then_inc(s_const_v, 1)
            dve.tensor_copy(ident_b[:, :], ident[:, :]).then_inc(s_const_v, 1)
            dve.tensor_copy(before_b[:, :], before[:, :]).then_inc(s_const_v, 1)
            dve.wait_ge(s_key_in, 16 * 8)
            dve.memset(pay1[:, :, :], 0.0).then_inc(s_const_v, 1)
            dve.wait_ge(s_const_v, 5)
            dve.wait_ge(s_prep, 1)

            def split(a, so, pay, w):
                dve.tensor_scalar(part_i[:, 0, :], key_i[:, a, :], 8, None, ALU.logical_shift_right)
                dve.tensor_scalar(part_i[:, 1, :], key_i[:, a, :], LO - 1, None, ALU.bitwise_and).then_inc(so["split"], 1)
                dve.wait_ge(so["split"], 1)
                dve.tensor_copy(part_f[:, :, 0, :], halves(0))
                dve.tensor_copy(high_b[:, :], part_i[:, 0, :])
                dve.tensor_copy(part_f[:, :, 1, :], halves(1)).then_inc(so["split"], 1)
                dve.tensor_copy(pay[:, :, KEY[a]], key_i[:, a, :]).then_inc(so["pay_all"], 1)
                dve.tensor_copy(pay[:, :, OTHER[a]], other_i[:, a, :]).then_inc(so["pay_all"], 1)
                if a == 1:
                    dve.tensor_copy(pay[:, :, OTHER[a] + 1], other_i[:, 0, :]).then_inc(so["pay_all"], 1)
                else:
                    dve.tensor_copy(pay[:, :, W0 - 1], key_i[:, a, :]).then_inc(so["pay_all"], 1)
                dve.wait_ge(so["split"], 2)

            def one_hots(t, so, parts_sem, hot_sem):
                s = t.slot(2)
                dve.tensor_copy(parts[:, s, :, :], part_f[:, bass.ds(t.n, 1), :, :].rearrange(
                    "p a c s -> p (a c) s")).then_inc(so[parts_sem], 1)
                dve.wait_ge(so[parts_sem], t.n + 1)
                for g in range(SUB):
                    dve.tensor_scalar(hot_hi[:, s, g, :], iota_b[:, :], parts[:, s, 0, g:g + 1], None, ALU.is_equal)
                    mm = dve.tensor_scalar(hot_lo[:, s, g, :], iota_b[:, :], parts[:, s, 1, g:g + 1], None, ALU.is_equal)
                mm.then_inc(so[hot_sem], 1)

            def sort(a, so):
                def count(t):
                    wait(dve, so["counted"], t.n - 1)
                    one_hots(t, so, "parts_c", "hot_c")

                pipeline(dve, NT, 2, [(0, count)])
                dve.wait_ge(so["counted"], NT)
                dve.tensor_copy(cnt_s[:, :, :], tab_bank[:, :].rearrange("p (c k) -> p c k", c=2)).then_inc(so["prefix"], 1)
                dve.wait_ge(so["prefix"], 1)
                for c in range(2):
                    mm = dve.tensor_tensor_scan(incl[:, c, :], ones[:, :], cnt_s[:, c, :], 0.0, ALU.mult, ALU.add)
                mm.then_inc(so["prefix"], 1)
                dve.wait_ge(so["prefix"], 2)
                dve.tensor_tensor(base[:, :, :], incl[:, :, :], cnt_s[:, :, :], ALU.subtract).then_inc(so["prefix"], 1)
                dve.tensor_copy(tot[:, :], incl[:, :, LO - 1]).then_inc(so["prefix"], 1)
                dve.wait_ge(so["offset"], 1)
                dve.tensor_copy(off[:, :], off_bank[:, 0:2]).then_inc(so["prefix"], 1)
                dve.wait_ge(so["prefix"], 5)
                for c in range(2):
                    dve.tensor_scalar(base[:, c, :], base[:, c, :], off[:, c:c + 1], None, ALU.add).then_inc(so["prefix"], 1)

                def prepare(t):
                    s = t.slot(2)
                    wait(dve, so["looked_up"], t.n - 1)
                    one_hots(t, so, "parts_s", "hot_s")
                    dve.wait_ge(so["high_ready"], t.n + 1)
                    for c in range(2):
                        dve.tensor_scalar(hot_hi_t[:, s, c, :], high_row[:, s, :], row_id[:, c:c + 1], None, ALU.is_equal)
                    for e in range(SUB):
                        mm = dve.scalar_tensor_tensor(
                            out=earlier[:, s, e, e * P:(e + 1) * P], in0=high_row[:, s, e * P:(e + 1) * P],
                            scalar=parts[:, s, 0, e:e + 1], in1=before_b[:, :], op0=ALU.is_equal, op1=ALU.mult)
                        if e < SUB - 1:
                            mm = dve.tensor_scalar(earlier[:, s, e, (e + 1) * P:TE], high_row[:, s, (e + 1) * P:TE],
                                                   parts[:, s, 0, e:e + 1], None, ALU.is_equal)
                    mm.then_inc(so["ready"], 1)

                def read_table(t):
                    s = t.slot(2)
                    if t.k is None and t.c == 0:
                        dve.wait_ge(so["base_in"], 1)
                    else:
                        dve.wait_ge(so["added"], t.n)
                    wait(dve, so["looked_up"], t.n - 1)
                    dve.tensor_scalar(tab_hi[:, s, :], tab_bank[:, :], ROUND, ROUND, ALU.add,
                                      ALU.subtract).then_inc(so["tab_hi_ready"], 1)
                    dve.wait_ge(so["tab_hi_ready"], t.n + 1)
                    dve.tensor_tensor(tab_lo[:, s, :], tab_bank[:, :], tab_hi[:, s, :],
                                      ALU.subtract).then_inc(so["tab_ready"], 1)

                def find_place(t):
                    s = t.slot(2)
                    dve.wait_ge(so["looked_up"], t.n + 1)
                    for g in range(SUB):
                        mm = dve.tensor_tensor_reduce(
                            out=picked[:, g, :], in0=bank[4 + 2 * s + g // 2][:, (g % 2) * LO:(g % 2 + 1) * LO],
                            in1=hot_lo[:, s, g, :], scale=1.0, scalar=0.0, op0=ALU.mult, op1=ALU.add,
                            accum_out=place_f[:, s, g:g + 1])
                    mm.then_inc(so["place_found"], 1)
                    dve.wait_ge(so["place_found"], t.n + 1)
                    wait(dve, so["scattered"][s], 64 * t.turn(2))
                    dve.tensor_copy(place_i[:, s, :], place_f[:, s, :]).then_inc(so["place_ready"], 1)

                pipeline(dve, NT, 2, [(1, read_table), (2, find_place), (0, prepare)])

            split(0, sort_s[0], pay0, W0)
            dve.wait_ge(s_w_in, 16 * 14)
            dve.tensor_tensor(phi_n[:, :, :], phi_n[:, :, :], theta_n[:, :, :], ALU.subtract).then_inc(s_w2, 1)
            dve.tensor_tensor(cols[:, 5, :], cols[:, 3, :], cols[:, 4, :], ALU.add)
            dve.wait_ge(s_h0, 1)
            dve.tensor_tensor(h0[:, :], bank[5][:, 0:D], rows_b[:, 0, :], ALU.add).then_inc(s_h0_v, 1)
            dve.wait_ge(s_h0_v, 1)
            dve.tensor_tensor(shift[:, :], rows_b[:, 0, :], h0[:, :], ALU.subtract).then_inc(s_h0_v, 1)
            sort(0, sort_s[0])

            def ends(t, L, other, n):
                q = t.slot(4)
                wait(dve, L["gathered"][t.slot(2)], 64 * n * (t.turn(2) - 1))
                dve.wait_ge(L["edges_in"][q], 32 * t.turn(4) + 32)
                dve.tensor_copy(ends_i[:, q, 0:n, :], edge[:, q, :, other:other + n].rearrange("p g n -> p n g")).then_inc(L["ends"], 1)

            def tails(t, L, key):
                q = t.slot(4)
                wait(dve, L["scattered"][t.slot(2)], 64 * (t.turn(2) - 1))
                dve.wait_ge(L["edges_in"][q], 32 * t.turn(4) + 32)
                dve.tensor_tensor(goes_on[:, :], edge[:, q, :, key], next_key[:, q, :], ALU.is_equal).then_inc(L["tail_step"], 1)
                dve.wait_ge(L["tail_step"], 2 * t.n + 1)
                dve.scalar_tensor_tensor(out=tail_f[:, q, :], in0=goes_on[:, :], scalar=SKIP, in1=edge[:, q, :, key],
                                         op0=ALU.mult, op1=ALU.add).then_inc(L["tail_step"], 1)
                dve.wait_ge(L["tail_step"], 2 * t.n + 2)
                dve.tensor_scalar(is_last[:, q, :], tail_f[:, q, :], N - 0.5, None, ALU.is_lt)
                dve.tensor_copy(tail_i[:, q, :], tail_f[:, q, :]).then_inc(L["tails"], 1)

            def compare_keys(t, L):
                s = t.slot(2)
                dve.wait_ge(L["key_row"], t.n + 1)
                dve.tensor_tensor(same[:, s, :], key_row[:, s, 1:TE + 1], key_row[:, s, 0:TE], ALU.is_equal).then_inc(L["same"], 1)

            L = l0

            def d_and_stats(t):
                s, q = t.slot(2), t.slot(4)
                wait(dve, L["scattered"][s], 64 * t.turn(2))
                wait(dve, L["sq"], 4 * (t.n - 1))
                for j in range(2):
                    dve.wait_ge(L["h_bank"], 2 * t.n + j + 1)
                    dve.tensor_tensor(d_rows[:, s, 2 * j:2 * j + 2, :],
                                      bank[2 + j][:, :].rearrange("p (g d) -> p g d", g=2),
                                      shift[:, :].rearrange("p (a d) -> p a d", a=1).to_broadcast([P, 2, D]),
                                      ALU.add).then_inc(L["d"], 1)
                wait(dve, L["stats"], t.n)
                for g in range(SUB):
                    if g % 2 == 0:
                        dve.wait_ge(L["d"], 2 * t.n + g // 2 + 1)
                    dve.scalar_tensor_tensor(out=acc_d[:, g, :], in0=d_rows[:, s, g, :], scalar=is_last[:, q, g:g + 1],
                                             in1=acc_d[:, g, :], op0=ALU.mult, op1=ALU.add)
                dve.wait_ge(L["sq"], 4 * (t.n + 1))
                dve.tensor_tensor(acc_q[:, :, :], acc_q[:, :, :], sq[:, s, :, :], ALU.add).then_inc(L["stats"], 1)

            def keys0(t):
                tails(t, L, KEY0)
                compare_keys(t, L)

            def sum_messages(t):
                s = t.slot(2)
                wait(dve, L["z_bank"], 2 * (t.n - 1))
                for c in range(KC):
                    dve.wait_ge(L["filt_bank"], 2 * t.n + c + 1)
                    dve.wait_ge(L["xt"], 2 * t.n + c + 1)
                    dve.scalar_tensor_tensor(out=msg[:, c, :], in0=bank[3 + c][:, :], scalar=cols[:, 1, c:c + 1],
                                             in1=xt[:, s, c, :], op0=ALU.add, op1=ALU.mult).then_inc(L["msg"], 1)
                if not (t.k is None and t.c == 0):
                    dve.wait_ge(L["agg"], 2 * t.n)
                dve.wait_ge(L["same"], t.n + 1)
                for c in range(KC):
                    dve.wait_ge(L["msg"], 2 * t.n + c + 1)
                    first = 0.0 if t.k is None and t.c == 0 else agg[:, 1 - s, c, TE - 1:TE]
                    dve.tensor_tensor_scan(agg[:, s, c, :], same[:, s, :], msg[:, c, :], first, ALU.mult,
                                           ALU.add).then_inc(L["agg"], 1)

            pipeline(dve, NT, 4, [(0, lambda t: ends(t, L, OTHER0, 1)), (4, d_and_stats), (1, keys0), (2, sum_messages)])

            steps = [0]

            def bn(ins):
                steps[0] += 1
                ins.then_inc(s_bn, 1)
                dve.wait_ge(s_bn, steps[0])

            dve.wait_ge(s_sum, 1)
            bn(dve.tensor_scalar(bn_sum[:, :, :], bank[7][:, :].rearrange("p (j d) -> p j d", j=2), 1.0 / N, None, ALU.mult))
            bn(dve.tensor_tensor(bn_mean[:, :], bn_sum[:, 0, :], bn_sum[:, 0, :], ALU.mult))
            bn(dve.tensor_tensor(bn_mean[:, :], bn_sum[:, 1, :], bn_mean[:, :], ALU.subtract))
            bn(dve.tensor_scalar(bn_mean[:, :], bn_mean[:, :], 0.0, EPS, ALU.max, ALU.add))
            dve.tensor_copy(bn_tmp[:, :], bn_mean[:, :]).then_inc(s_bn_v, 1)
            dve.wait_ge(s_bn_sd, 1)
            bn(dve.reciprocal(bn_tmp[:, :], bn_tmp[:, :]))
            bn(dve.tensor_tensor(bn_scale[:, :], bn_tmp[:, :], rows_b[:, 1, :], ALU.mult))
            bn(dve.tensor_tensor(bn_tmp[:, :], bn_sum[:, 0, :], bn_scale[:, :], ALU.mult))
            bn(dve.tensor_tensor(bn_shift[:, :], rows_b[:, 2, :], bn_tmp[:, :], ALU.subtract))

            def moments(sem_of, t, rows, r):
                s = t.slot(2)
                st = stats[0:rows, s, 0:r, :].rearrange("p r k -> p k r")
                mo = moment[0:rows, s, :, 0:r]
                dve.wait_ge(sem_of["stats"], t.n + 1)
                dve.tensor_tensor(mo[:, 0, :], st[:, 1, :], st[:, 4, :], ALU.add)
                dve.tensor_tensor(mo[:, 1, :], st[:, 1, :], st[:, 4, :], ALU.subtract)
                dve.tensor_tensor(mo[:, 2, :], st[:, 2, :], st[:, 5, :], ALU.add).then_inc(sem_of["mv"], 1)
                dve.wait_ge(sem_of["mv"], 3 * t.n + 1)
                dve.scalar_tensor_tensor(out=mo[:, 3, :], in0=mo[:, 1, :], scalar=0.25, in1=mo[:, 1, :],
                                         op0=ALU.mult, op1=ALU.mult).then_inc(sem_of["mv"], 1)
                dve.wait_ge(sem_of["mv"], 3 * t.n + 2)
                dve.scalar_tensor_tensor(out=mo[:, 4, :], in0=mo[:, 2, :], scalar=1.0 / D, in1=mo[:, 3, :],
                                         op0=ALU.mult, op1=ALU.add).then_inc(sem_of["mv"], 1)
                dve.wait_ge(sem_of["mv"], 3 * t.n + 3)

            def node(t, rows=P, r=R):
                s = t.slot(2)
                xr, dr = node_x[0:rows, s, 0:r, :], node_d[0:rows, s, 0:r, :]

                def wide(v):
                    return v[0:rows, :].rearrange("p (a d) -> p a d", a=1).to_broadcast([rows, r, D])

                dve.wait_ge(nd_in[s], 32 * t.turn(2) + 32)
                dve.tensor_tensor(dr, dr, wide(bn_scale), ALU.mult).then_inc(nd["step"], 1)
                dve.wait_ge(nd["step"], 3 * t.n + 1)
                dve.scalar_tensor_tensor(out=dr, in0=xr, scalar=2.0, in1=dr, op0=ALU.mult, op1=ALU.add).then_inc(nd["step"], 1)
                dve.wait_ge(nd["step"], 3 * t.n + 2)
                dve.tensor_tensor(dr, dr, wide(bn_shift), ALU.add).then_inc(nd["step"], 1)
                dve.wait_ge(nd["step"], 3 * t.n + 3)
                for j in range(r):
                    mm = dve.bn_stats(stats[0:rows, s, j, :], node_d[0:rows, s, j, :])
                mm.then_inc(nd["stats"], 1)
                moments(nd, t, rows, r)
                dve.tensor_scalar(spread[0:rows, s, 0, 0:r], moment[0:rows, s, 4, 0:r], EPS, None, ALU.add)
                dve.tensor_scalar(spread[0:rows, s, 1, 0:r], moment[0:rows, s, 4, 0:r], 1.0 + EPS, EPS * EPS,
                                  ALU.mult, ALU.add).then_inc(nd["spread"], 1)

            def node_scales(t, rows=P, r=R):
                s = t.slot(2)
                dve.wait_ge(nd["sd"], t.n + 1)
                dve.reciprocal(inv[0:rows, s, :, 0:r], sd[0:rows, s, :, 0:r]).then_inc(nd["inv"], 1)
                dve.wait_ge(nd["inv"], t.n + 1)
                for j in range(2):
                    mm = dve.scalar_tensor_tensor(out=neg[0:rows, s, j, 0:r], in0=moment[0:rows, s, 0, 0:r], scalar=-0.5,
                                                  in1=inv[0:rows, s, j, 0:r], op0=ALU.mult, op1=ALU.mult)
                mm.then_inc(nd["neg"], 1)

            pipeline(dve, NN, 2, [(0, node), (0, node_scales)])
            node(Tile(NN), TAIL, 1)
            node_scales(Tile(NN), TAIL, 1)

            split(1, sort_s[1], pay1, W1)
            sort(1, sort_s[1])

            M = l1
            dve.memset(key_row[:, 0, 0:1], -1.0).then_inc(s_prep, 1)
            dve.wait_ge(s_prep, 2)

            def last_rows(t):
                s = t.slot(2)
                wait(dve, M["rows"], t.n - 1)
                for j in range(2):
                    dve.wait_ge(M["best_bank"], 2 * t.n + j + 1)
                    dve.tensor_tensor(d_rows[:, s, 2 * j:2 * j + 2, :],
                                      bank[7 if j == 0 else 0][:, :].rearrange("p (g d) -> p g d", g=2),
                                      gathered2[:, t.slot(4), 2 * j:2 * j + 2, :], ALU.add).then_inc(M["sum"], 1)
                for g in range(SUB):
                    dve.wait_ge(M["sum"], 2 * t.n + g // 2 + 1)
                    mm = dve.bn_stats(stats[:, s, g, :], d_rows[:, s, g, :])
                mm.then_inc(M["stats"], 1)
                moments(M, t, P, SUB)
                dve.tensor_scalar(spread[:, s, 0, 0:SUB], moment[:, s, 4, 0:SUB], EPS, None, ALU.add).then_inc(M["spread"], 1)
                dve.wait_ge(M["sd"], t.n + 1)
                dve.reciprocal(inv[:, s, 0, 0:SUB], sd[:, s, 0, 0:SUB]).then_inc(M["inv"], 1)
                dve.wait_ge(M["inv"], t.n + 1)
                dve.scalar_tensor_tensor(out=neg[:, s, 0, 0:SUB], in0=moment[:, s, 0, 0:SUB], scalar=-0.5,
                                         in1=inv[:, s, 0, 0:SUB], op0=ALU.mult, op1=ALU.mult).then_inc(M["neg"], 1)

            def keys1(t):
                tails(t, M, KEY1)
                compare_keys(t, M)

            def max_edges(t):
                s = t.slot(2)
                wait(dve, M["best_bank"], 2 * (t.n - 1))
                dve.wait_ge(M["same"], t.n + 1)
                if not (t.k is None and t.c == 0):
                    dve.wait_ge(M["best"], 2 * t.n)
                for o in range(KC):
                    dve.wait_ge(M["e"], 2 * t.n + o + 1)
                    first = 0.0 if t.k is None and t.c == 0 else agg[:, 1 - s, o, TE - 1:TE]
                    dve.tensor_tensor_scan(agg[:, s, o, :], same[:, s, :], zt[:, s, o, :], first, ALU.mult,
                                           ALU.max).then_inc(M["best"], 1)

            pipeline(dve, NT, 4, [(0, lambda t: ends(t, M, OTHER1, 2)), (3, last_rows), (1, keys1), (2, max_edges)])


_INS = ['x', 'src', 'dst', 'edge_attr_20', 'L0_gnn_Wf1', 'L0_gnn_bf1', 'L0_gnn_Wf2', 'L0_gnn_bf2', 'L0_gnn_Wu1',
        'L0_gnn_bu1', 'L0_gnn_Wu2', 'L0_gnn_bu2', 'L0_gnn_gamma', 'L0_gnn_beta', 'L1_gnn_theta_w', 'L1_gnn_theta_b',
        'L1_gnn_phi_w', 'L1_gnn_phi_b']
_OUTS = [((50000, 256), 'float32')]


def kernel(**inputs):
    import numpy as _np
    import concourse.bacc as _bacc
    from concourse import mybir as _mybir
    from concourse.bass_utils import run_bass_kernel_spmd as _run

    nc = _bacc.Bacc("TRN2", target_bir_lowering=False, num_devices=1)
    arrays, args = {}, []
    for name in _INS:
        a = _np.ascontiguousarray(inputs[name])
        arrays[f"in_{name}_dram"] = a
        args.append(nc.dram_tensor(f"in_{name}_dram", a.shape, _mybir.dt.from_np(a.dtype), kind="ExternalInput").ap())
    for i, (shape, dtype) in enumerate(_OUTS):
        dt = _mybir.dt.from_np(_np.dtype(dtype))
        args.append(nc.dram_tensor(f"out_{i}_dram", shape, dt, kind="ExternalOutput").ap())
    build(nc, *args)
    r = _run(nc, [arrays], core_ids=[0])
    return r.results[0]["out_0_dram"]
```

```python
from contextlib import ExitStack

import concourse.bass as bass
from concourse import mybir

F32 = mybir.dt.float32
BF16 = mybir.dt.bfloat16
I32 = mybir.dt.int32
U32 = mybir.dt.uint32
ALU = mybir.AluOpType
ACT = mybir.ActivationFunctionType

P = 128
SUB = 4
TE = SUB * P
LO = 256
ROUND = 1.5 * 2.0 ** 31
SKIP = 65536.0
EPS = 1e-5


class Tile:

    def __init__(self, c, unroll=1, k=None):
        self.c, self.unroll, self.k = c, unroll, k
        self.n = c if k is None else k * unroll + c

    def slot(self, m):
        return self.c % m

    def turn(self, m):
        return self.c // m if self.k is None else self.k * (self.unroll // m) + self.c // m


def pipeline(eng, count, unroll, stages):
    lags = max(lag for lag, _ in stages)

    def step(c, k=None):
        for lag, body in stages:
            if k is not None or 0 <= c - lag < count:
                body(Tile(c - lag, unroll, k))

    first = lags + max(unroll, 2)
    rounds = (count - first) // unroll
    for c in range(first):
        step(c)
    with eng.Fori(0, rounds) as k:
        for j in range(unroll):
            step(first + j, k)
    for c in range(first + rounds * unroll, count + lags):
        step(c)


def wait(eng, sem, value, most=None):
    if isinstance(value, int):
        if most is not None:
            value = min(value, most)
        if value <= 0:
            return
    eng.wait_ge(sem, value)


def build(nc, x, src, dst, attr, wf1, bf1, wf2, bf2, wu1, bu1, wu2, bu2, gamma, beta,
          theta_w, theta_b, phi_w, phi_b, out):
    N, D = x.shape
    E, G = attr.shape
    KC = D // P
    NT = -(-E // TE)
    COLS = NT * SUB
    EP = NT * TE
    PAD_KEY = N + 47
    assert N <= PAD_KEY < LO * LO and KC == 2 and D == LO
    W0 = 24
    OTHER0, KEY0 = G, G + 2
    W1 = 4
    OTHER1, KEY1 = 0, 2
    R = 5
    SLOTS = 6
    NN = N // (P * R)
    TAIL = N - NN * P * R
    ZR = 2 * R
    NZ = N // (P * ZR)
    assert TAIL <= P and N - NZ * P * ZR == TAIL

    ctx = ExitStack()
    with ctx:
        def sb(name, shape, dt=F32):
            return ctx.enter_context(nc.sbuf_tensor(name, shape, dt))

        def ps(name, shape, dt=F32):
            return ctx.enter_context(nc.psum_tensor(name, shape, dt))

        def sem(name):
            return ctx.enter_context(nc.semaphore(name))

        sorted0 = nc.dram_tensor("sorted0", (EP + 1, W0), F32).ap()
        sorted1 = nc.dram_tensor("sorted1", (EP + 1, W1), F32).ap()
        d_tab = nc.dram_tensor("d_tab", (N, D), F32).ap()
        x1_tab = nc.dram_tensor("x1_tab", (N, D), F32).ap()

        iota_f = sb("iota_f", [P, LO])
        iota_b = sb("iota_b", [P, LO], BF16)
        row_id = sb("row_id", [P, 2])
        ident = sb("ident", [P, P])
        ident_b = sb("ident_b", [P, P], BF16)
        before = sb("before", [P, P])
        before_b = sb("before_b", [P, P], BF16)
        ones = sb("ones", [P, LO])
        zeros_b = sb("zeros_b", [P, TE], BF16)
        pad_row = sb("pad_row", [1, W0])

        wf1_s = sb("wf1_s", [G, D])
        wf2_s = sb("wf2_s", [P, KC, D])
        wu1_s = sb("wu1_s", [P, KC, D])
        wu2_s = sb("wu2_s", [P, KC, D])
        theta_n = sb("theta_n", [P, KC, D])
        phi_n = sb("phi_n", [P, KC, D])
        w_dst = sb("w_dst", [P, KC, D])
        w_src = sb("w_src", [P, KC, D])
        cols = sb("cols", [P, 6, KC])
        rows_b = sb("rows_b", [P, 3, D])
        z0_wide = sb("z0_wide", [P, KC, P])
        h0 = sb("h0", [P, D])
        shift = sb("shift", [P, D])
        bn_scale = sb("bn_scale", [P, D])
        bn_shift = sb("bn_shift", [P, D])
        bn_mean = sb("bn_mean", [P, D])
        bn_tmp = sb("bn_tmp", [P, D])
        bn_sum = sb("bn_sum", [P, 2, D])

        key_i = sb("key_i", [P, 2, COLS], I32)
        other_i = sb("other_i", [P, 2, COLS], I32)
        next_dst = sb("next_dst", [P, COLS], I32)
        inversions = sb("inversions", [P, COLS])
        out_of_order = sb("out_of_order", [P, 2])
        out_of_order_i = sb("out_of_order_i", [P, 2], I32)
        part_i = sb("part_i", [P, 2, COLS], I32)
        part_f = sb("part_f", [P, NT, 2, SUB])
        high_b = sb("high_b", [P, COLS], BF16)
        pay1 = sb("pay1", [P, COLS, W1])
        parts = sb("parts", [P, 2, 2, SUB])
        hot_hi = sb("hot_hi", [P, 2, SUB, LO], BF16)
        hot_lo = sb("hot_lo", [P, 2, SUB, LO], BF16)
        high_row = sb("high_row", [P, 2, TE], BF16)
        hot_hi_t = sb("hot_hi_t", [P, 2, 2, TE], BF16)
        earlier = sb("earlier", [P, 2, SUB, TE], BF16)
        tab_hi = sb("tab_hi", [P, 2, 2 * LO], BF16)
        tab_lo = sb("tab_lo", [P, 2, 2 * LO], BF16)
        cnt_s = sb("cnt_s", [P, 2, LO])
        incl = sb("incl", [P, 2, LO])
        tot = sb("tot", [P, 2])
        off = sb("off", [P, 2])
        base = sb("base", [P, 2, LO])
        place_f = sb("place_f", [P, 2, SUB])
        place_i = sb("place_i", [P, 2, SUB], I32)
        picked = sb("picked", [P, SUB, LO], BF16)
        pay_t = sb("pay_t", [P, 2, SUB, W0])

        edge = sb("edge", [P, 4, SUB, W0])
        ends_i = sb("ends_i", [P, 4, 2, SUB], I32)
        next_key = sb("next_key", [P, 4, SUB])
        tail_f = sb("tail_f", [P, 4, SUB])
        tail_i = sb("tail_i", [P, 4, SUB], I32)
        is_last = sb("is_last", [P, 4, SUB])
        goes_on = sb("goes_on", [P, SUB])
        key_row = sb("key_row", [P, 2, TE + 1])
        same = sb("same", [P, 2, TE])
        attr_t = sb("attr_t", [G, TE])
        gathered = sb("gathered", [P, 2, SUB, D])
        h1_xt = sb("h1_xt", [P, 4 * KC * TE])
        h1 = h1_xt[:, 0:2 * KC * TE].rearrange("p (s c e) -> p s c e", s=2, c=KC)
        xt = h1_xt[:, 2 * KC * TE:4 * KC * TE].rearrange("p (s c e) -> p s c e", s=2, c=KC)
        xt2 = h1
        attr_s = h1_xt[:, 0:COLS * G].rearrange("p (t g) -> p t g", g=G)
        msg = sb("msg", [P, KC, TE])
        layer_all = sb("layer_all", [P, 8 * KC * TE])
        agg, zt = (layer_all[:, 2 * i * KC * TE:2 * (i + 1) * KC * TE].rearrange("p (s c e) -> p s c e", s=2, c=KC)
                   for i in range(2))
        d_rows, sq = (layer_all[:, 2 * i * KC * TE:2 * (i + 1) * KC * TE].rearrange("p (s g d) -> p s g d", s=2, g=SUB)
                      for i in range(2, 4))
        acc_d = sb("acc_d", [P, SUB, D])
        acc_q = sb("acc_q", [P, SUB, D])
        node_x_all = sb("node_x_all", [P, SLOTS * R * D])
        node_d_all = layer_all[:, 0:SLOTS * R * D]
        node_x = node_x_all[:, :].rearrange("p (s r d) -> p s r d", s=SLOTS, r=R)
        node_d = node_d_all.rearrange("p (s r d) -> p s r d", s=SLOTS, r=R)
        pay0 = node_x_all[:, 0:COLS * W0].rearrange("p (t w) -> p t w", w=W0)
        gathered2 = node_x_all[:, 0:4 * SUB * D].rearrange("p (s g d) -> p s g d", s=4, g=SUB)
        stats = sb("stats", [P, SLOTS, R, 6])
        moment = sb("moment", [P, SLOTS, 5, R])
        spread = sb("spread", [P, SLOTS, 2, R])
        sd = sb("sd", [P, SLOTS, 2, R])
        inv = sb("inv", [P, SLOTS, 2, R])
        neg = sb("neg", [P, SLOTS, 2, R])

        bank = [ps(f"bank{i}", [P, TE]) for i in range(8)]

        s_pad = sem("padding_set")
        s_const = sem("constants_made")
        s_const_v = sem("constants_cast")
        s_key_in = sem("keys_loaded")
        s_attr_in = sem("attributes_loaded")
        s_w_in = sem("weights_loaded")
        s_zero = sem("zeros_made")
        s_fill = sem("d_tab_filled")
        s_prep = sem("vector_setup_step")
        s_w2 = sem("phi_minus_theta")
        s_wt = sem("weights_transposed")
        s_wt_used = sem("weights_copied")
        s_z0 = sem("z0_ready")
        s_h0 = sem("h0_in_psum")
        s_h0_v = sem("h0_step")
        s_pay0 = sem("payload0_laid_out")
        s_pay1 = sem("payload1_laid_out")

        def sort_sems(a):
            return {k: sem(f"{k}{a}") for k in (
                "split", "parts_c", "hot_c", "counted", "prefix", "offset", "base_in", "parts_s", "hot_s",
                "high_bank", "high_ready", "ready", "tab_hi_ready", "tab_ready", "added", "looked_up",
                "place_found", "place_ready", "pay_ready")} | {
                    "scattered": [sem(f"scattered{a}_{i}") for i in range(2)]}

        sort_s = [sort_sems(0), sort_sems(1)]

        def layer_sems(a, names):
            return {k: sem(f"{k}{a}") for k in names} | {
                "edges_in": [sem(f"edges_in{a}_{i}") for i in range(4)],
                "gathered": [sem(f"gathered{a}_{i}") for i in range(2)],
                "scattered": [sem(f"rows_scattered{a}_{i}") for i in range(2)]}

        l0 = layer_sems(0, ("key_bank", "key_row", "attr_bank", "attr_t", "h1_bank", "h1", "xt_bank", "xt",
                            "filt_bank", "msg", "same", "agg", "z_bank", "z", "h_bank", "d", "sq", "stats",
                            "tails", "tail_step", "ends"))
        l1 = layer_sems(1, ("key_bank", "key_row", "xt_bank", "xt", "xt2_bank", "xt2", "e_bank", "e", "same",
                            "best", "best_bank", "sum", "stats", "sums", "square", "variance", "spread", "sd", "inv", "neg", "rows",
                            "tails", "tail_step", "ends"))
        s_sum = sem("column_sums")
        s_bn = sem("batch_norm_step")
        s_bn_sd = sem("batch_norm_sd")
        s_bn_v = sem("batch_norm_variance")
        nd = {k: sem(f"node_{k}") for k in ("scaled", "summed", "z", "stats", "sums", "square", "variance", "spread", "sd",
                                            "inv", "neg", "rows")}
        nd_in = [sem(f"node_in_{i}") for i in range(SLOTS)]
        nd_out = [sem(f"node_out_{i}") for i in range(SLOTS)]
        s_pad_row = sem("pad_rows_written")
        s_order = sem("order_step")
        s_order_pe = sem("inversions_summed")
        s_in_order = sem("edges_stored_in_order")
        s_placed1 = sem("sorted1_complete")

        sorted_rows = [t[0:EP, :].rearrange("(t s p) w -> t p s w", s=SUB, p=P) for t in (sorted0, sorted1)]
        next_rows = [t[1:EP + 1, :].rearrange("(t s p) w -> t p s w", s=SUB, p=P) for t in (sorted0, sorted1)]

        def node_tiles(t):
            return t[0:NN * P * R, :].rearrange("(t p r) d -> t p r d", p=P, r=R)

        WT = [W0, W1]
        KEY = [KEY0, KEY1]
        OTHER = [OTHER0, OTHER1]
        FULL = E // COLS
        REST = E - FULL * COLS

        def halves(a):
            return part_i[:, a, :].rearrange("p (t s) -> p t s", s=SUB)

        block = ctx.enter_context(nc.Block())

        @block.sync
        def _(sp):
            sp.wait_ge(s_pad, 1)
            for tile, slot, arr in ((key_i, 0, src), (key_i, 1, dst), (other_i, 0, dst), (other_i, 1, src)):
                sp.dma_start(tile[0:FULL, slot, :],
                             arr[0:FULL * COLS].rearrange("(p t) -> p t", t=COLS)).then_inc(s_key_in, 16)
                sp.dma_start(tile[FULL:FULL + 1, slot, 0:REST],
                             arr[FULL * COLS:E].rearrange("(p t) -> p t", p=1)).then_inc(s_key_in, 16)
            sp.dma_start(next_dst[0:FULL, :],
                         dst[1:FULL * COLS + 1].rearrange("(p t) -> p t", t=COLS)).then_inc(s_key_in, 16)
            sp.dma_start(next_dst[FULL:FULL + 1, 0:REST - 1],
                         dst[FULL * COLS + 1:E].rearrange("(p t) -> p t", p=1)).then_inc(s_key_in, 16)
            sp.dma_start(attr_s[0:FULL, :, :],
                         attr[0:FULL * COLS, :].rearrange("(p t) g -> p t g", t=COLS)).then_inc(s_attr_in, 16)
            sp.dma_start(attr_s[FULL:FULL + 1, 0:REST, :],
                         attr[FULL * COLS:E, :].rearrange("(p t) g -> p t g", p=1)).then_inc(s_attr_in, 16)
            sp.dma_start(wf1_s[:, :], wf1).then_inc(s_w_in, 16)
            for tile, w in ((wf2_s, wf2), (wu1_s, wu1), (wu2_s, wu2), (theta_n, theta_w), (phi_n, phi_w)):
                sp.dma_start(tile[:, :, :], w.rearrange("(c p) d -> p c d", p=P)).then_inc(s_w_in, 16)
            for j, b in enumerate((bf1, bf2, bu1, theta_b, phi_b)):
                sp.dma_start(cols[:, j, :], b.rearrange("(c p) -> p c", p=P),
                             allow_slow_non_contiguous=True).then_inc(s_w_in, 16)
            for j, b in enumerate((bu2, gamma, beta)):
                sp.dma_start(rows_b[:, j, :],
                             b.rearrange("(a d) -> a d", a=1).to_broadcast([P, D])).then_inc(s_w_in, 16)
            sp.wait_ge(s_const, 8)
            sp.dma_start(sorted0[EP:EP + 1, :], pad_row[:, :]).then_inc(s_pad_row, 16)
            sp.dma_start(sorted1[EP:EP + 1, :], pad_row[:, 0:W1]).then_inc(s_pad_row, 16)
            sp.wait_ge(s_pay1, 1)
            sp.wait_ge(s_order, 3)
            sp.dma_start(sorted1[0:EP, :].rearrange("(p t) w -> p (t w)", p=P),
                         pay1[:, :, :].rearrange("p t w -> p (t w)")).then_inc(s_in_order, 16)
            sp.wait_ge(s_zero, 1)
            zero_tiles = d_tab[0:NZ * P * ZR, :].rearrange("(t p r) d -> t p (r d)", p=P, r=ZR)
            with sp.Fori(0, NZ) as t:
                sp.dma_start(zero_tiles[t], node_d_all[:, 0:ZR * D]).then_inc(s_fill, 16)
            sp.dma_start(d_tab[NZ * P * ZR:N, :], node_d_all[0:TAIL, 0:D]).then_inc(s_fill, 16)

            def load_edges(a, ly):
                def body(t):
                    s = t.slot(4)
                    wait(sp, ly["key_bank"], t.n - 3)
                    wait(sp, ly["tails"], t.n - 3)
                    if a == 0:
                        wait(sp, ly["attr_bank"], t.n - 3)
                    wait(sp, ly["ends"], t.n - 3)
                    if t.k is None and t.c == 0:
                        for i in range(2 * (a == 0)):
                            sp.wait_ge(sort_s[a]["scattered"][i], 16 * SUB * ((NT + 1 - i) // 2))
                        sp.wait_ge(s_pad_row, 32)
                    sp.dma_start(edge[:, s, :, 0:WT[a]], sorted_rows[a][t.n]).then_inc(ly["edges_in"][s], 16)
                    sp.dma_start(next_key[:, s, :], next_rows[a][t.n][:, :, KEY[a]],
                                 allow_slow_non_contiguous=True).then_inc(ly["edges_in"][s], 16)
                return body

            pipeline(sp, NT, 4, [(0, load_edges(0, l0))])

            def load_nodes(t):
                s = t.slot(SLOTS)
                wait(sp, nd_out[s], t.turn(SLOTS) * 32)
                sp.dma_start(node_x[:, s, :, :], node_tiles(x)[t.n]).then_inc(nd_in[s], 16)
                sp.dma_start(node_d[:, s, :, :], node_tiles(d_tab)[t.n]).then_inc(nd_in[s], 16)

            sp.wait_ge(s_fill, 16 * (NZ + 1))
            sp.wait_ge(l0["stats"], NT)
            for i in range(2):
                sp.wait_ge(l0["scattered"][i], 16 * SUB * ((NT + 1 - i) // 2))
            pipeline(sp, NN, SLOTS, [(0, load_nodes)])
            s = NN % SLOTS
            sp.wait_ge(nd_out[s], (NN // SLOTS) * 32)
            sp.dma_start(node_x[0:TAIL, s, 0, :], x[NN * P * R:N, :]).then_inc(nd_in[s], 16)
            sp.dma_start(node_d[0:TAIL, s, 0, :], d_tab[NN * P * R:N, :]).then_inc(nd_in[s], 16)
            sp.wait_ge(s_placed1, 1)
            pipeline(sp, NT, 4, [(0, load_edges(1, l1))])

        @block.gpsimd
        def _(pool):
            pool.memset(ones[:, :], 1.0).then_inc(s_const, 1)
            pool.memset(ident[:, :], 0.0).then_inc(s_const, 1)
            pool.memset(before[:, :], 1.0).then_inc(s_const, 1)
            pool.memset(pad_row[:, :], SKIP).then_inc(s_const, 1)
            pool.iota(iota_f[:, :], pattern=[[1, LO]], base=0, channel_multiplier=0,
                      allow_small_or_imprecise_dtypes=True).then_inc(s_const, 1)
            pool.iota(row_id[:, :], pattern=[[P, 2]], base=0, channel_multiplier=1,
                      allow_small_or_imprecise_dtypes=True).then_inc(s_const, 1)
            pool.wait_ge(s_const, 6)
            pool.affine_select(out=ident[:, :], in_=ident[:, :], compare_op=ALU.not_equal, fill=1.0, base=0,
                               pattern=[[-1, P]], channel_multiplier=1).then_inc(s_const, 1)
            pool.affine_select(out=before[:, :], in_=before[:, :], compare_op=ALU.is_gt, fill=0.0, base=0,
                               pattern=[[1, P]], channel_multiplier=-1).then_inc(s_const, 1)

            def scatter_payload(a, so, table):
                def body(t):
                    s = t.slot(2)
                    pool.wait_ge(so["pay_ready"], t.n + 1)
                    pool.wait_ge(so["place_ready"], t.n + 1)
                    pool.nop(nofuse=True)
                    for g in range(SUB):
                        pool.indirect_dma_start(
                            out=table, out_offset=bass.IndirectOffsetOnAxis(
                                ap=place_i[:, s, g:g + 1].bitcast(U32), axis=0),
                            in_=pay_t[:, s, g, 0:WT[a]], in_offset=None).then_inc(so["scattered"][s], 16)
                return body

            def gather(idx, table, to, done):
                for g in range(SUB):
                    pool.indirect_dma_start(
                        out=to[:, g, :], out_offset=None, in_=table,
                        in_offset=bass.IndirectOffsetOnAxis(ap=idx[g], axis=0)).then_inc(done, 16)

            def scatter_tails(table, ready, rows, sems):
                def body(t):
                    s = t.slot(2)
                    pool.wait_ge(ready[0], ready[1] * (t.n + 1))
                    pool.nop(nofuse=True)
                    for g in range(SUB):
                        pool.indirect_dma_start(
                            out=table, out_offset=bass.IndirectOffsetOnAxis(
                                ap=tail_i[:, t.slot(4), g:g + 1].bitcast(U32), axis=0),
                            in_=rows[:, s, g, :], in_offset=None, bounds_check=N - 1,
                            oob_is_err=False).then_inc(sems[s], 16)
                return body

            pipeline(pool, NT, 2, [(0, scatter_payload(0, sort_s[0], sorted0))])

            def gather0(t):
                s = t.slot(2)
                wait(pool, l0["xt_bank"], 2 * (t.n - 1))
                pool.wait_ge(l0["ends"], t.n + 1)
                pool.nop(nofuse=True)
                gather([ends_i[:, t.slot(4), 0, g:g + 1].bitcast(U32) for g in range(SUB)], x,
                       gathered[:, s], l0["gathered"][s])

            pool.wait_ge(s_fill, 16 * (NZ + 1))
            pipeline(pool, NT, 4, [(0, gather0), (3, scatter_tails(d_tab, (l0["d"], 2), d_rows, l0["scattered"]))])
            pool.wait_ge(s_in_order, 16)
            with pool.If(pool.value_load(out_of_order_i[0:1, 0:1]) > 0):
                pipeline(pool, NT, 2, [(0, scatter_payload(1, sort_s[1], sorted1))])
                for i in range(2):
                    pool.wait_ge(sort_s[1]["scattered"][i], 16 * SUB * ((NT + 1 - i) // 2))
            pool.sem_inc(s_placed1, 1)

            def gather1(t):
                s = t.slot(2)
                wait(pool, l1["xt_bank"], 2 * (t.n - 1))
                wait(pool, l1["sum"], 2 * (t.n - 3))
                pool.wait_ge(l1["ends"], t.n + 1)
                pool.nop(nofuse=True)
                q = t.slot(4)
                gather([ends_i[:, q, 0, g:g + 1].bitcast(U32) for g in range(SUB)], x1_tab,
                       gathered[:, s], l1["gathered"][s])
                gather([ends_i[:, q, 1, g:g + 1].bitcast(U32) for g in range(SUB)], x1_tab,
                       gathered2[:, q], l1["gathered"][s])

            for s in range(SLOTS):
                pool.wait_ge(nd_out[s], 32 * ((NN + 1 + SLOTS - 1 - s) // SLOTS))
            pipeline(pool, NT, 4, [(0, gather1), (3, scatter_tails(out, (l1["rows"], 1), sq, l1["scattered"]))])
            for i in range(2):
                pool.wait_ge(l1["scattered"][i], 16 * SUB * ((NT + 1 - i) // 2))

        tab_bank = bank[0]
        off_bank = bank[3]
        high_bank = [bank[1 + i][:, 0:TE // 2].bitcast(BF16) for i in range(2)]

        @block.tensor
        def _(pe):
            def sort(a, so):
                pe.matmul(tab_bank[:, :], zeros_b[:, 0:P], zeros_b[:, :], start=True, stop=False, skip_group_check=True)

                def add_counts(s, last_sem):
                    for g in range(SUB):
                        for c in range(2):
                            mm = pe.matmul(tab_bank[:, c * LO:(c + 1) * LO], hot_hi[:, s, g, c * P:(c + 1) * P],
                                           hot_lo[:, s, g, :], start=False, stop=(g == SUB - 1 and c == 1),
                                           skip_group_check=True)
                    mm.then_inc(last_sem, 1)

                def count(t):
                    pe.wait_ge(so["hot_c"], t.n + 1)
                    add_counts(t.slot(2), so["counted"])

                pipeline(pe, NT, 2, [(0, count)])
                pe.wait_ge(so["prefix"], 4)
                pe.matmul(off_bank[:, 0:2], before[:, :], tot[:, :], start=True, stop=False, skip_group_check=True)
                pe.matmul(off_bank[:, 1:2], ones[:, 0:P], tot[:, 0:1], start=False, stop=True,
                          skip_group_check=True).then_inc(so["offset"], 1)
                pe.wait_ge(so["prefix"], 7)
                pe.matmul(tab_bank[:, 0:LO], ident[:, :], base[:, 0, :], start=True, stop=False, skip_group_check=True)
                pe.matmul(tab_bank[:, LO:2 * LO], ident[:, :], base[:, 1, :], start=False, stop=False,
                          skip_group_check=True).then_inc(so["base_in"], 1)

                def high_rows(t):
                    wait(pe, so["high_ready"], t.n - 1)
                    for g in range(SUB):
                        mm = pe.transpose(high_bank[t.slot(2)][:, g * P:(g + 1) * P],
                                          high_b[:, bass.ds(t.n * SUB + g, 1)].to_broadcast([P, P]), ident_b[:, :])
                    mm.then_inc(so["high_bank"], 1)

                def look_up(t):
                    s = t.slot(2)
                    pe.wait_ge(so["tab_ready"], t.n + 1)
                    pe.wait_ge(so["hot_s"], t.n + 1)
                    add_counts(s, so["added"])
                    pe.wait_ge(so["ready"], t.n + 1)
                    wait(pe, so["place_found"], t.n - 1)
                    for g in range(SUB):
                        to = bank[4 + 2 * s + g // 2][:, (g % 2) * LO:(g % 2 + 1) * LO]
                        for c in range(2):
                            hot = hot_hi_t[:, s, c, g * P:(g + 1) * P]
                            pe.matmul(to, hot, tab_hi[:, s, c * LO:(c + 1) * LO], start=(c == 0), stop=False)
                            pe.matmul(to, hot, tab_lo[:, s, c * LO:(c + 1) * LO], start=False, stop=False)
                        for e in range(g + 1):
                            mm = pe.matmul(to, earlier[:, s, e, g * P:(g + 1) * P], hot_lo[:, s, e, :],
                                           start=False, stop=(e == g))
                    mm.then_inc(so["looked_up"], 1)

                pipeline(pe, NT, 2, [(0, high_rows), (1, look_up)])

            pe.wait_ge(s_const, 8)
            pe.wait_ge(s_const_v, 4)
            pe.wait_ge(s_order, 2)
            pe.matmul(bank[7][:, 0:1], ones[:, 0:P], out_of_order[:, 0:1], start=True, stop=True).then_inc(s_order_pe, 1)
            pe.wait_ge(s_w_in, 16 * 14)
            pe.wait_ge(s_w2, 1)
            for j, w in enumerate((theta_n, phi_n)):
                for c in range(KC):
                    for o in range(KC):
                        mm = pe.transpose(bank[1 + 2 * j + c][:, o * P:(o + 1) * P], w[:, o, c * P:(c + 1) * P],
                                          ident[:, :])
            mm.then_inc(s_wt, 1)
            pe.wait_ge(s_z0, 1)
            for c in range(KC):
                mm = pe.matmul(bank[5][:, 0:D], z0_wide[:, c, :], wu2_s[:, c, :], start=(c == 0), stop=(c == KC - 1))
            mm.then_inc(s_h0, 1)
            pe.wait_ge(s_wt_used, 4)
            pe.wait_ge(s_h0_v, 2)
            pe.wait_ge(s_order, 3)
            sort(0, sort_s[0])
            pe.wait_ge(sort_s[0]["place_found"], NT)

            L = l0

            def keys_attrs(t):
                wait(pe, L["msg"], 2 * (t.n - 1))
                wait(pe, L["key_row"], t.n)
                pe.wait_ge(L["edges_in"][t.slot(4)], 32 * t.turn(4) + 32)
                for g in range(SUB):
                    mm = pe.transpose(bank[4][:, g * P:(g + 1) * P],
                                      edge[:, t.slot(4), g, KEY0:KEY0 + 1].to_broadcast([P, P]), ident[:, :])
                mm.then_inc(L["key_bank"], 1)
                wait(pe, L["attr_t"], t.n)
                for g in range(SUB):
                    mm = pe.transpose(bank[5][0:G, g * P:(g + 1) * P], edge[:, t.slot(4), g, 0:G], ident[:, :])
                mm.then_inc(L["attr_bank"], 1)

            def update_in(t):
                s = t.slot(2)
                pe.wait_ge(L["agg"], 2 * (t.n + 1))
                for o in range(KC):
                    wait(pe, L["z"], 2 * (t.n - 1) + o + 1)
                    if o == 0:
                        wait(pe, L["h1"], 2 * (t.n + 2), 2 * NT)
                    else:
                        pe.wait_ge(L["xt"], 2 * t.n + 1)
                    for c in range(KC):
                        mm = pe.matmul(bank[o][:, :], wu1_s[:, c, o * P:(o + 1) * P], agg[:, s, c, :],
                                       start=(c == 0), stop=(c == KC - 1))
                    mm.then_inc(L["z_bank"], 1)

            def update_out(t):
                s = t.slot(2)
                pe.wait_ge(L["z"], 2 * (t.n + 1))
                for j in range(2):
                    wait(pe, L["d"], 2 * (t.n - 1) + j + 1)
                    if j == 0:
                        wait(pe, L["xt"], 2 * (t.n + 2), 2 * NT)
                    else:
                        wait(pe, L["msg"], 2 * (t.n + 1) + 1, 2 * NT)
                    for g in range(2 * j, 2 * j + 2):
                        for c in range(KC):
                            mm = pe.matmul(bank[2 + j][:, (g % 2) * D:(g % 2 + 1) * D],
                                           zt[:, s, c, g * P:(g + 1) * P], wu2_s[:, c, :],
                                           start=(c == 0), stop=(c == KC - 1))
                    mm.then_inc(L["h_bank"], 1)

            def filter_in(t):
                pe.wait_ge(L["attr_t"], t.n + 1)
                for o in range(KC):
                    if o == 0:
                        wait(pe, L["h1"], 2 * (t.n - 1) + 1)
                    else:
                        wait(pe, L["z"], 2 * (t.n - 2) + 1)
                    pe.matmul(bank[6 if o == 0 else 0][:, :], wf1_s[:, o * P:(o + 1) * P], attr_t[:, :],
                              start=True, stop=True).then_inc(L["h1_bank"], 1)

            def filter_out(t):
                s = t.slot(2)
                pe.wait_ge(L["gathered"][s], 64 * t.turn(2) + 64)
                for c in range(KC):
                    if c == 0:
                        wait(pe, L["z"], 2 * t.n)
                    else:
                        wait(pe, L["d"], 2 * (t.n - 2) + 1)
                    for g in range(SUB):
                        mm = pe.transpose(bank[1 + c][:, g * P:(g + 1) * P],
                                          gathered[:, s, g, c * P:(c + 1) * P], ident[:, :])
                    mm.then_inc(L["xt_bank"], 1)
                pe.wait_ge(L["h1"], 2 * (t.n + 1))
                for o in range(KC):
                    if o == 0:
                        wait(pe, L["d"], 2 * (t.n - 1))
                    else:
                        wait(pe, L["key_row"], t.n + 2, NT)
                    for c in range(KC):
                        mm = pe.matmul(bank[3 + o][:, :], wf2_s[:, c, o * P:(o + 1) * P], h1[:, s, c, :],
                                       start=(c == 0), stop=(c == KC - 1))
                    mm.then_inc(L["filt_bank"], 1)

            pipeline(pe, NT, 4, [(0, keys_attrs), (2, update_in), (3, update_out), (0, filter_in), (1, filter_out)])

            pe.wait_ge(L["stats"], NT)
            for j, acc in enumerate((acc_d, acc_q)):
                for g in range(SUB):
                    mm = pe.matmul(bank[7][:, j * D:(j + 1) * D], ones[:, 0:P], acc[:, g, :],
                                   start=(g == 0), stop=(g == SUB - 1))
            mm.then_inc(s_sum, 1)
            pe.wait_ge(s_bn, 1)
            with pe.If(pe.value_load(out_of_order_i[0:1, 0:1]) > 0):
                sort(1, sort_s[1])
                pe.wait_ge(sort_s[1]["place_found"], NT)

            M = l1

            def edge_rows(t):
                s = t.slot(2)
                pe.wait_ge(M["gathered"][s], 128 * t.turn(2) + 128)
                for c in range(KC):
                    wait(pe, M["xt"], 2 * (t.n - 1) + c + 1)
                    for g in range(SUB):
                        mm = pe.transpose(bank[1 + c][:, g * P:(g + 1) * P],
                                          gathered[:, s, g, c * P:(c + 1) * P], ident[:, :])
                    mm.then_inc(M["xt_bank"], 1)
                for c in range(KC):
                    wait(pe, M["xt2"], 2 * (t.n - 1) + c + 1)
                    for g in range(SUB):
                        mm = pe.transpose(bank[3 + c][:, g * P:(g + 1) * P],
                                          gathered2[:, t.slot(4), g, c * P:(c + 1) * P], ident[:, :])
                    mm.then_inc(M["xt2_bank"], 1)
                wait(pe, M["sum"], 2 * (t.n - 2) + 1)
                wait(pe, M["key_row"], t.n)
                for g in range(SUB):
                    mm = pe.transpose(bank[7][:, g * P:(g + 1) * P],
                                      edge[:, t.slot(4), g, KEY1:KEY1 + 1].to_broadcast([P, P]), ident[:, :])
                mm.then_inc(M["key_bank"], 1)

            def edge_mlp(t):
                s = t.slot(2)
                pe.wait_ge(M["xt"], 2 * (t.n + 1))
                pe.wait_ge(M["xt2"], 2 * (t.n + 1))
                for o in range(KC):
                    wait(pe, M["e"], 2 * (t.n - 1) + o + 1)
                    for c in range(KC):
                        pe.matmul(bank[5 + o][:, :], w_dst[:, c, o * P:(o + 1) * P], xt2[:, s, c, :],
                                  start=(c == 0), stop=False)
                        mm = pe.matmul(bank[5 + o][:, :], w_src[:, c, o * P:(o + 1) * P], xt[:, s, c, :],
                                       start=False, stop=(c == KC - 1))
                    mm.then_inc(M["e_bank"], 1)

            def best_rows(t):
                s = t.slot(2)
                pe.wait_ge(M["best"], 2 * (t.n + 1))
                for j in range(2):
                    wait(pe, M["sum"], 2 * (t.n - 1) + j + 1)
                    if j == 0:
                        wait(pe, M["key_row"], t.n + 2, NT)
                    for g in range(2 * j, 2 * j + 2):
                        for c in range(KC):
                            mm = pe.transpose(bank[7 if j == 0 else 0][:, (g % 2) * D + c * P:(g % 2) * D + (c + 1) * P],
                                              agg[:, s, c, g * P:(g + 1) * P], ident[:, :])
                    mm.then_inc(M["best_bank"], 1)

            pipeline(pe, NT, 4, [(2, best_rows), (0, edge_rows), (1, edge_mlp)])

        @block.scalar
        def _(act):
            act.wait_ge(s_w_in, 16 * 14)
            act.wait_ge(s_const, 8)
            for c in range(KC):
                mm = act.activation(z0_wide[:, c, :], before[:, :], ACT.Silu, scale=0.0, bias=cols[:, 2, c:c + 1])
            mm.then_inc(s_z0, 1)
            act.wait_ge(s_wt, 1)
            for j, w in enumerate((w_dst, w_src)):
                for c in range(KC):
                    act.copy(w[:, c, :], bank[1 + 2 * j + c][:, 0:D]).then_inc(s_wt_used, 1)
            act.wait_ge(s_attr_in, 32)
            act.copy(pay0[:, :, 0:G], attr_s[:, :, :]).then_inc(s_pay0, 1)

            def sort(a, so, pay):
                def high_copy(t):
                    s = t.slot(2)
                    act.wait_ge(so["high_bank"], t.n + 1)
                    wait(act, so["ready"], t.n - 1)
                    act.copy(high_row[:, s, :], high_bank[s]).then_inc(so["high_ready"], 1)

                def lay_out(t):
                    s = t.slot(2)
                    wait(act, so["scattered"][s], 64 * t.turn(2))
                    act.copy(pay_t[:, s, :, 0:WT[a]],
                             pay[:, bass.ds(t.n * SUB, SUB), :]).then_inc(so["pay_ready"], 1)

                pipeline(act, NT, 2, [(0, high_copy), (1, lay_out)])

            act.wait_ge(s_pay0, 2)
            act.wait_ge(s_pay1, 1)
            act.wait_ge(s_order, 3)
            sort(0, sort_s[0], pay0)

            L = l0

            def keys_attrs(t):
                s = t.slot(2)
                wait(act, L["same"], t.n - 1)
                if not (t.k is None and t.c == 0):
                    act.wait_ge(L["key_row"], t.n)
                    act.copy(key_row[:, s, 0:1], key_row[:, 1 - s, TE:TE + 1])
                act.wait_ge(L["key_bank"], t.n + 1)
                act.copy(key_row[:, s, 1:TE + 1], bank[4][:, :]).then_inc(L["key_row"], 1)
                act.wait_ge(L["attr_bank"], t.n + 1)
                act.copy(attr_t[:, :], bank[5][0:G, :]).then_inc(L["attr_t"], 1)

            def silu_z(t):
                s = t.slot(2)
                wait(act, L["h_bank"], 2 * (t.n - 1))
                for o in range(KC):
                    act.wait_ge(L["z_bank"], 2 * t.n + o + 1)
                    act.activation(zt[:, s, o, :], bank[o][:, :], ACT.Silu, bias=cols[:, 2, o:o + 1]).then_inc(L["z"], 1)

            def squares(t):
                s = t.slot(2)
                wait(act, L["stats"], t.n - 1)
                for g in range(SUB):
                    if g % 2 == 0:
                        act.wait_ge(L["d"], 2 * t.n + g // 2 + 1)
                    act.activation(sq[:, s, g, :], d_rows[:, s, g, :], ACT.Square,
                                   scale=is_last[:, t.slot(4), g:g + 1]).then_inc(L["sq"], 1)

            def silu_h1(t):
                s = t.slot(2)
                wait(act, L["filt_bank"], 2 * (t.n - 1))
                for o in range(KC):
                    act.wait_ge(L["h1_bank"], 2 * t.n + o + 1)
                    act.activation(h1[:, s, o, :], bank[6 if o == 0 else 0][:, :], ACT.Silu,
                                   bias=cols[:, 0, o:o + 1]).then_inc(L["h1"], 1)

            def copy_xt(t):
                s = t.slot(2)
                wait(act, L["msg"], 2 * (t.n - 1))
                for c in range(KC):
                    act.wait_ge(L["xt_bank"], 2 * t.n + c + 1)
                    act.copy(xt[:, s, c, :], bank[1 + c][:, :]).then_inc(L["xt"], 1)

            pipeline(act, NT, 4, [(0, keys_attrs), (2, silu_z), (3, squares), (0, silu_h1), (1, copy_xt)])

            act.wait_ge(s_bn_v, 1)
            act.activation(bn_tmp[:, :], bn_tmp[:, :], ACT.Sqrt).then_inc(s_bn_sd, 1)

            def roots(t, rows=P, r=R):
                s = t.slot(SLOTS)
                act.wait_ge(nd["spread"], t.n + 1)
                act.activation(sd[0:rows, s, :, 0:r], spread[0:rows, s, :, 0:r], ACT.Sqrt).then_inc(nd["sd"], 1)

            def norm_rows(t, rows=P, r=R):
                s = t.slot(SLOTS)
                act.wait_ge(nd["neg"], t.n + 1)
                for j in range(r):
                    act.activation(node_x[0:rows, s, j, :], node_d[0:rows, s, j, :], ACT.Identity,
                                   scale=inv[0:rows, s, 1, j:j + 1], bias=neg[0:rows, s, 1, j:j + 1])
                for j in range(r):
                    mm = act.activation(node_d[0:rows, s, j, :], node_d[0:rows, s, j, :], ACT.Identity,
                                        scale=inv[0:rows, s, 0, j:j + 1], bias=neg[0:rows, s, 0, j:j + 1])
                mm.then_inc(nd["rows"], 1)

            def store_nodes(t):
                s = t.slot(SLOTS)
                act.wait_ge(nd["rows"], t.n + 1)
                act.dma_start(node_tiles(x1_tab)[t.n], node_d[:, s, :, :]).then_inc(nd_out[s], 16)
                act.dma_start(node_tiles(out)[t.n], node_x[:, s, :, :]).then_inc(nd_out[s], 16)

            pipeline(act, NN, SLOTS, [(0, roots), (1, norm_rows), (2, store_nodes)])
            roots(Tile(NN), TAIL, 1)
            norm_rows(Tile(NN), TAIL, 1)
            s = NN % SLOTS
            act.wait_ge(nd["rows"], NN + 1)
            act.dma_start(x1_tab[NN * P * R:N, :], node_d[0:TAIL, s, 0, :]).then_inc(nd_out[s], 16)
            act.dma_start(out[NN * P * R:N, :], node_x[0:TAIL, s, 0, :]).then_inc(nd_out[s], 16)
            with act.If(act.value_load(out_of_order_i[0:1, 0:1]) > 0):
                sort(1, sort_s[1], pay1)

            M = l1

            def best_norm(t):
                s = t.slot(2)
                act.wait_ge(M["spread"], t.n + 1)
                act.activation(sd[:, s, 0, 0:SUB], spread[:, s, 0, 0:SUB], ACT.Sqrt).then_inc(M["sd"], 1)
                act.wait_ge(M["neg"], t.n + 1)
                wait(act, M["scattered"][s], 64 * t.turn(2))
                for g in range(SUB):
                    mm = act.activation(sq[:, s, g, :], d_rows[:, s, g, :], ACT.Identity,
                                        scale=inv[:, s, 0, g:g + 1], bias=neg[:, s, 0, g:g + 1])
                mm.then_inc(M["rows"], 1)

            def copies(t):
                s = t.slot(2)
                wait(act, M["e_bank"], 2 * (t.n - 1))
                for c in range(KC):
                    act.wait_ge(M["xt_bank"], 2 * t.n + c + 1)
                    act.copy(xt[:, s, c, :], bank[1 + c][:, :]).then_inc(M["xt"], 1)
                for c in range(KC):
                    act.wait_ge(M["xt2_bank"], 2 * t.n + c + 1)
                    act.copy(xt2[:, s, c, :], bank[3 + c][:, :]).then_inc(M["xt2"], 1)
                wait(act, M["same"], t.n - 1)
                if not (t.k is None and t.c == 0):
                    act.wait_ge(M["key_row"], t.n)
                    act.copy(key_row[:, s, 0:1], key_row[:, 1 - s, TE:TE + 1])
                act.wait_ge(M["key_bank"], t.n + 1)
                act.copy(key_row[:, s, 1:TE + 1], bank[7][:, :]).then_inc(M["key_row"], 1)

            def relu_e(t):
                s = t.slot(2)
                wait(act, M["best"], 2 * (t.n - 1))
                for o in range(KC):
                    act.wait_ge(M["e_bank"], 2 * t.n + o + 1)
                    act.activation(zt[:, s, o, :], bank[5 + o][:, :], ACT.Relu, bias=cols[:, 5, o:o + 1]).then_inc(M["e"], 1)

            pipeline(act, NT, 4, [(0, copies), (2, best_norm), (1, relu_e)])

        @block.vector
        def _(dve):
            dve.memset(key_i[:, :, :], PAD_KEY)
            dve.memset(next_dst[:, :], PAD_KEY)
            dve.memset(attr_s[:, :, :], 0.0)
            dve.memset(other_i[:, :, :], 0).then_inc(s_pad, 1)
            dve.memset(node_d_all[:, 0:ZR * D], 0.0).then_inc(s_zero, 1)
            dve.memset(zeros_b[:, :], 0.0).then_inc(s_const_v, 1)
            dve.memset(acc_d[:, :, :], 0.0)
            dve.memset(acc_q[:, :, :], 0.0)
            dve.memset(pay0[:, :, G:W0], 0.0)
            dve.memset(pay1[:, :, :], 0.0)
            dve.memset(key_row[:, 0, 0:1], -1.0).then_inc(s_prep, 1)
            dve.wait_ge(s_const, 8)
            dve.tensor_copy(iota_b[:, :], iota_f[:, :]).then_inc(s_const_v, 1)
            dve.tensor_copy(ident_b[:, :], ident[:, :]).then_inc(s_const_v, 1)
            dve.tensor_copy(before_b[:, :], before[:, :]).then_inc(s_const_v, 1)
            dve.wait_ge(s_key_in, 16 * 10)
            dve.wait_ge(s_const_v, 4)
            dve.wait_ge(s_prep, 1)

            def split(a, so):
                dve.tensor_scalar(part_i[:, 0, :], key_i[:, a, :], 8, None, ALU.logical_shift_right)
                dve.tensor_scalar(part_i[:, 1, :], key_i[:, a, :], LO - 1, None, ALU.bitwise_and).then_inc(so["split"], 1)
                dve.wait_ge(so["split"], 1)
                dve.tensor_copy(part_f[:, :, 0, :], halves(0))
                dve.tensor_copy(high_b[:, :], part_i[:, 0, :])
                dve.tensor_copy(part_f[:, :, 1, :], halves(1)).then_inc(so["split"], 1)
                dve.wait_ge(so["split"], 2)

            def one_hots(t, so, parts_sem, hot_sem):
                s = t.slot(2)
                dve.tensor_copy(parts[:, s, :, :], part_f[:, bass.ds(t.n, 1), :, :].rearrange(
                    "p a c s -> p (a c) s")).then_inc(so[parts_sem], 1)
                dve.wait_ge(so[parts_sem], t.n + 1)
                for g in range(SUB):
                    dve.tensor_scalar(hot_hi[:, s, g, :], iota_b[:, :], parts[:, s, 0, g:g + 1], None, ALU.is_equal)
                    mm = dve.tensor_scalar(hot_lo[:, s, g, :], iota_b[:, :], parts[:, s, 1, g:g + 1], None, ALU.is_equal)
                mm.then_inc(so[hot_sem], 1)

            def sort(a, so):
                def count(t):
                    wait(dve, so["counted"], t.n - 1)
                    one_hots(t, so, "parts_c", "hot_c")

                pipeline(dve, NT, 2, [(0, count)])
                dve.wait_ge(so["counted"], NT)
                dve.tensor_copy(cnt_s[:, :, :], tab_bank[:, :].rearrange("p (c k) -> p c k", c=2)).then_inc(so["prefix"], 1)
                dve.wait_ge(so["prefix"], 1)
                for c in range(2):
                    mm = dve.tensor_tensor_scan(incl[:, c, :], ones[:, :], cnt_s[:, c, :], 0.0, ALU.mult, ALU.add)
                mm.then_inc(so["prefix"], 1)
                dve.wait_ge(so["prefix"], 2)
                dve.tensor_tensor(base[:, :, :], incl[:, :, :], cnt_s[:, :, :], ALU.subtract).then_inc(so["prefix"], 1)
                dve.tensor_copy(tot[:, :], incl[:, :, LO - 1]).then_inc(so["prefix"], 1)
                dve.wait_ge(so["offset"], 1)
                dve.tensor_copy(off[:, :], off_bank[:, 0:2]).then_inc(so["prefix"], 1)
                dve.wait_ge(so["prefix"], 5)
                for c in range(2):
                    dve.tensor_scalar(base[:, c, :], base[:, c, :], off[:, c:c + 1], None, ALU.add).then_inc(so["prefix"], 1)

                def prepare(t):
                    s = t.slot(2)
                    wait(dve, so["looked_up"], t.n - 1)
                    one_hots(t, so, "parts_s", "hot_s")
                    dve.wait_ge(so["high_ready"], t.n + 1)
                    for c in range(2):
                        dve.tensor_scalar(hot_hi_t[:, s, c, :], high_row[:, s, :], row_id[:, c:c + 1], None, ALU.is_equal)
                    for e in range(SUB):
                        mm = dve.scalar_tensor_tensor(
                            out=earlier[:, s, e, e * P:(e + 1) * P], in0=high_row[:, s, e * P:(e + 1) * P],
                            scalar=parts[:, s, 0, e:e + 1], in1=before_b[:, :], op0=ALU.is_equal, op1=ALU.mult)
                        if e < SUB - 1:
                            mm = dve.tensor_scalar(earlier[:, s, e, (e + 1) * P:TE], high_row[:, s, (e + 1) * P:TE],
                                                   parts[:, s, 0, e:e + 1], None, ALU.is_equal)
                    mm.then_inc(so["ready"], 1)

                def read_table(t):
                    s = t.slot(2)
                    if t.k is None and t.c == 0:
                        dve.wait_ge(so["base_in"], 1)
                    else:
                        dve.wait_ge(so["added"], t.n)
                    wait(dve, so["looked_up"], t.n - 1)
                    dve.tensor_scalar(tab_hi[:, s, :], tab_bank[:, :], ROUND, ROUND, ALU.add,
                                      ALU.subtract).then_inc(so["tab_hi_ready"], 1)
                    dve.wait_ge(so["tab_hi_ready"], t.n + 1)
                    dve.tensor_tensor(tab_lo[:, s, :], tab_bank[:, :], tab_hi[:, s, :],
                                      ALU.subtract).then_inc(so["tab_ready"], 1)

                def find_place(t):
                    s = t.slot(2)
                    dve.wait_ge(so["looked_up"], t.n + 1)
                    for g in range(SUB):
                        mm = dve.tensor_tensor_reduce(
                            out=picked[:, g, :], in0=bank[4 + 2 * s + g // 2][:, (g % 2) * LO:(g % 2 + 1) * LO],
                            in1=hot_lo[:, s, g, :], scale=1.0, scalar=0.0, op0=ALU.mult, op1=ALU.add,
                            accum_out=place_f[:, s, g:g + 1])
                    mm.then_inc(so["place_found"], 1)
                    dve.wait_ge(so["place_found"], t.n + 1)
                    wait(dve, so["scattered"][s], 64 * t.turn(2))
                    dve.tensor_copy(place_i[:, s, :], place_f[:, s, :]).then_inc(so["place_ready"], 1)

                pipeline(dve, NT, 2, [(1, read_table), (2, find_place), (0, prepare)])

            dve.tensor_copy(pay0[:, :, KEY0], key_i[:, 0, :])
            dve.tensor_copy(pay0[:, :, OTHER0], other_i[:, 0, :]).then_inc(s_pay0, 1)
            dve.tensor_tensor(inversions[:, :], key_i[:, 1, :], next_dst[:, :], ALU.is_gt).then_inc(s_order, 1)
            dve.wait_ge(s_order, 1)
            dve.tensor_reduce(out_of_order[:, 0:1], inversions[:, :], mybir.AxisListType.X, ALU.add).then_inc(s_order, 1)
            dve.wait_ge(s_order_pe, 1)
            dve.tensor_scalar(out_of_order_i[:, 0:1], bank[7][:, 0:1], 1.0, None, ALU.min).then_inc(s_order, 1)
            dve.tensor_copy(pay1[:, :, KEY1], key_i[:, 1, :])
            dve.tensor_copy(pay1[:, :, OTHER1], other_i[:, 1, :])
            dve.tensor_copy(pay1[:, :, OTHER1 + 1], other_i[:, 0, :]).then_inc(s_pay1, 1)
            split(0, sort_s[0])
            dve.wait_ge(s_w_in, 16 * 14)
            dve.tensor_tensor(phi_n[:, :, :], phi_n[:, :, :], theta_n[:, :, :], ALU.subtract).then_inc(s_w2, 1)
            dve.tensor_tensor(cols[:, 5, :], cols[:, 3, :], cols[:, 4, :], ALU.add)
            dve.wait_ge(s_h0, 1)
            dve.tensor_tensor(h0[:, :], bank[5][:, 0:D], rows_b[:, 0, :], ALU.add).then_inc(s_h0_v, 1)
            dve.wait_ge(s_h0_v, 1)
            dve.tensor_tensor(shift[:, :], rows_b[:, 0, :], h0[:, :], ALU.subtract).then_inc(s_h0_v, 1)
            sort(0, sort_s[0])

            def ends(t, L, other, n):
                q = t.slot(4)
                wait(dve, L["gathered"][t.slot(2)], 64 * n * (t.turn(2) - 1))
                dve.wait_ge(L["edges_in"][q], 32 * t.turn(4) + 32)
                dve.tensor_copy(ends_i[:, q, 0:n, :], edge[:, q, :, other:other + n].rearrange("p g n -> p n g")).then_inc(L["ends"], 1)

            def tails(t, L, key):
                q = t.slot(4)
                wait(dve, L["scattered"][t.slot(2)], 64 * (t.turn(2) - 1))
                dve.wait_ge(L["edges_in"][q], 32 * t.turn(4) + 32)
                dve.tensor_tensor(goes_on[:, :], edge[:, q, :, key], next_key[:, q, :], ALU.is_equal).then_inc(L["tail_step"], 1)
                dve.wait_ge(L["tail_step"], 2 * t.n + 1)
                dve.scalar_tensor_tensor(out=tail_f[:, q, :], in0=goes_on[:, :], scalar=SKIP, in1=edge[:, q, :, key],
                                         op0=ALU.mult, op1=ALU.add).then_inc(L["tail_step"], 1)
                dve.wait_ge(L["tail_step"], 2 * t.n + 2)
                dve.tensor_scalar(is_last[:, q, :], tail_f[:, q, :], N - 0.5, None, ALU.is_lt)
                dve.tensor_copy(tail_i[:, q, :], tail_f[:, q, :]).then_inc(L["tails"], 1)

            def compare_keys(t, L):
                s = t.slot(2)
                dve.wait_ge(L["key_row"], t.n + 1)
                dve.tensor_tensor(same[:, s, :], key_row[:, s, 1:TE + 1], key_row[:, s, 0:TE], ALU.is_equal).then_inc(L["same"], 1)

            L = l0
            dve.wait_ge(s_fill, 16 * (NZ + 1))

            def d_and_stats(t):
                s, q = t.slot(2), t.slot(4)
                wait(dve, L["scattered"][s], 64 * t.turn(2))
                wait(dve, L["sq"], 4 * (t.n - 1))
                for j in range(2):
                    dve.wait_ge(L["h_bank"], 2 * t.n + j + 1)
                    dve.tensor_tensor(d_rows[:, s, 2 * j:2 * j + 2, :],
                                      bank[2 + j][:, :].rearrange("p (g d) -> p g d", g=2),
                                      shift[:, :].rearrange("p (a d) -> p a d", a=1).to_broadcast([P, 2, D]),
                                      ALU.add).then_inc(L["d"], 1)
                wait(dve, L["stats"], t.n)
                for g in range(SUB):
                    if g % 2 == 0:
                        dve.wait_ge(L["d"], 2 * t.n + g // 2 + 1)
                    dve.scalar_tensor_tensor(out=acc_d[:, g, :], in0=d_rows[:, s, g, :], scalar=is_last[:, q, g:g + 1],
                                             in1=acc_d[:, g, :], op0=ALU.mult, op1=ALU.add)
                dve.wait_ge(L["sq"], 4 * (t.n + 1))
                dve.tensor_tensor(acc_q[:, :, :], acc_q[:, :, :], sq[:, s, :, :], ALU.add).then_inc(L["stats"], 1)

            def keys0(t):
                tails(t, L, KEY0)
                compare_keys(t, L)

            def sum_messages(t):
                s = t.slot(2)
                wait(dve, L["z_bank"], 2 * (t.n - 1))
                for c in range(KC):
                    dve.wait_ge(L["filt_bank"], 2 * t.n + c + 1)
                    dve.wait_ge(L["xt"], 2 * t.n + c + 1)
                    dve.scalar_tensor_tensor(out=msg[:, c, :], in0=bank[3 + c][:, :], scalar=cols[:, 1, c:c + 1],
                                             in1=xt[:, s, c, :], op0=ALU.add, op1=ALU.mult).then_inc(L["msg"], 1)
                if not (t.k is None and t.c == 0):
                    dve.wait_ge(L["agg"], 2 * t.n)
                dve.wait_ge(L["same"], t.n + 1)
                for c in range(KC):
                    dve.wait_ge(L["msg"], 2 * t.n + c + 1)
                    first = 0.0 if t.k is None and t.c == 0 else agg[:, 1 - s, c, TE - 1:TE]
                    dve.tensor_tensor_scan(agg[:, s, c, :], same[:, s, :], msg[:, c, :], first, ALU.mult,
                                           ALU.add).then_inc(L["agg"], 1)

            pipeline(dve, NT, 4, [(0, lambda t: ends(t, L, OTHER0, 1)), (4, d_and_stats), (1, keys0), (2, sum_messages)])

            steps = [0]

            def bn(ins):
                steps[0] += 1
                ins.then_inc(s_bn, 1)
                dve.wait_ge(s_bn, steps[0])

            dve.wait_ge(s_sum, 1)
            bn(dve.tensor_scalar(bn_sum[:, :, :], bank[7][:, :].rearrange("p (j d) -> p j d", j=2), 1.0 / N, None, ALU.mult))
            bn(dve.tensor_tensor(bn_mean[:, :], bn_sum[:, 0, :], bn_sum[:, 0, :], ALU.mult))
            bn(dve.tensor_tensor(bn_mean[:, :], bn_sum[:, 1, :], bn_mean[:, :], ALU.subtract))
            bn(dve.tensor_scalar(bn_mean[:, :], bn_mean[:, :], 0.0, EPS, ALU.max, ALU.add))
            dve.tensor_copy(bn_tmp[:, :], bn_mean[:, :]).then_inc(s_bn_v, 1)
            dve.wait_ge(s_bn_sd, 1)
            bn(dve.reciprocal(bn_tmp[:, :], bn_tmp[:, :]))
            bn(dve.tensor_tensor(bn_scale[:, :], bn_tmp[:, :], rows_b[:, 1, :], ALU.mult))
            bn(dve.tensor_tensor(bn_tmp[:, :], bn_sum[:, 0, :], bn_scale[:, :], ALU.mult))
            bn(dve.tensor_tensor(bn_shift[:, :], rows_b[:, 2, :], bn_tmp[:, :], ALU.subtract))

            def row_sums(of, t, s, rows=P, r=R):
                st = stats[0:rows, s, 0:r, :].rearrange("p r k -> p k r")
                mo = moment[0:rows, s, :, 0:r]
                dve.wait_ge(of["stats"], t.n + 1)
                dve.tensor_tensor(mo[:, 0, :], st[:, 1, :], st[:, 4, :], ALU.add)
                dve.tensor_tensor(mo[:, 1, :], st[:, 1, :], st[:, 4, :], ALU.subtract)
                dve.tensor_tensor(mo[:, 2, :], st[:, 2, :], st[:, 5, :], ALU.add).then_inc(of["sums"], 1)

            def row_square(of, t, s, rows=P, r=R):
                mo = moment[0:rows, s, :, 0:r]
                dve.wait_ge(of["sums"], t.n + 1)
                dve.scalar_tensor_tensor(out=mo[:, 3, :], in0=mo[:, 1, :], scalar=0.25, in1=mo[:, 1, :],
                                         op0=ALU.mult, op1=ALU.mult).then_inc(of["square"], 1)

            def row_variance(of, t, s, rows=P, r=R):
                mo = moment[0:rows, s, :, 0:r]
                dve.wait_ge(of["square"], t.n + 1)
                dve.scalar_tensor_tensor(out=mo[:, 4, :], in0=mo[:, 2, :], scalar=1.0 / D, in1=mo[:, 3, :],
                                         op0=ALU.mult, op1=ALU.add).then_inc(of["variance"], 1)

            def wide(v, rows, r):
                return v[0:rows, :].rearrange("p (a d) -> p a d", a=1).to_broadcast([rows, r, D])

            def node_scale(t, rows=P, r=R):
                s = t.slot(SLOTS)
                dr = node_d[0:rows, s, 0:r, :]
                dve.wait_ge(nd_in[s], 32 * t.turn(SLOTS) + 32)
                dve.tensor_tensor(dr, dr, wide(bn_scale, rows, r), ALU.mult).then_inc(nd["scaled"], 1)

            def node_sum(t, rows=P, r=R):
                s = t.slot(SLOTS)
                xr, dr = node_x[0:rows, s, 0:r, :], node_d[0:rows, s, 0:r, :]
                dve.wait_ge(nd["scaled"], t.n + 1)
                dve.scalar_tensor_tensor(out=dr, in0=xr, scalar=2.0, in1=dr, op0=ALU.mult, op1=ALU.add).then_inc(nd["summed"], 1)

            def node_shift(t, rows=P, r=R):
                s = t.slot(SLOTS)
                dr = node_d[0:rows, s, 0:r, :]
                dve.wait_ge(nd["summed"], t.n + 1)
                dve.tensor_tensor(dr, dr, wide(bn_shift, rows, r), ALU.add).then_inc(nd["z"], 1)

            def node_stats(t, rows=P, r=R):
                s = t.slot(SLOTS)
                dve.wait_ge(nd["z"], t.n + 1)
                for j in range(r):
                    mm = dve.bn_stats(stats[0:rows, s, j, :], node_d[0:rows, s, j, :])
                mm.then_inc(nd["stats"], 1)

            def node_spread(t, rows=P, r=R):
                s = t.slot(SLOTS)
                dve.wait_ge(nd["variance"], t.n + 1)
                dve.tensor_scalar(spread[0:rows, s, 0, 0:r], moment[0:rows, s, 4, 0:r], EPS, None, ALU.add)
                dve.tensor_scalar(spread[0:rows, s, 1, 0:r], moment[0:rows, s, 4, 0:r], 1.0 + EPS, EPS * EPS,
                                  ALU.mult, ALU.add).then_inc(nd["spread"], 1)

            def node_inverse(t, rows=P, r=R):
                s = t.slot(SLOTS)
                dve.wait_ge(nd["sd"], t.n + 1)
                dve.reciprocal(inv[0:rows, s, :, 0:r], sd[0:rows, s, :, 0:r]).then_inc(nd["inv"], 1)

            def node_negative(t, rows=P, r=R):
                s = t.slot(SLOTS)
                dve.wait_ge(nd["inv"], t.n + 1)
                for j in range(2):
                    mm = dve.scalar_tensor_tensor(out=neg[0:rows, s, j, 0:r], in0=moment[0:rows, s, 0, 0:r], scalar=-0.5,
                                                  in1=inv[0:rows, s, j, 0:r], op0=ALU.mult, op1=ALU.mult)
                mm.then_inc(nd["neg"], 1)

            def of_nodes(stage):
                return lambda t, rows=P, r=R: stage(nd, t, t.slot(SLOTS), rows, r)

            stages = [(0, node_scale), (1, of_nodes(row_sums)), (2, node_inverse), (0, node_sum), (1, of_nodes(row_square)),
                      (2, node_negative), (0, node_shift), (1, of_nodes(row_variance)), (0, node_stats), (1, node_spread)]
            pipeline(dve, NN, SLOTS, stages)
            for stage in (node_scale, node_sum, node_shift, node_stats, of_nodes(row_sums), of_nodes(row_square),
                          of_nodes(row_variance), node_spread, node_inverse, node_negative):
                stage(Tile(NN), TAIL, 1)

            with dve.If(dve.value_load(out_of_order_i[0:1, 0:1]) > 0):
                split(1, sort_s[1])
                sort(1, sort_s[1])

            M = l1
            dve.memset(key_row[:, 0, 0:1], -1.0).then_inc(s_prep, 1)
            dve.wait_ge(s_prep, 2)

            def last_rows(t):
                s = t.slot(2)
                wait(dve, M["rows"], t.n - 1)
                for j in range(2):
                    dve.wait_ge(M["best_bank"], 2 * t.n + j + 1)
                    dve.tensor_tensor(d_rows[:, s, 2 * j:2 * j + 2, :],
                                      bank[7 if j == 0 else 0][:, :].rearrange("p (g d) -> p g d", g=2),
                                      gathered2[:, t.slot(4), 2 * j:2 * j + 2, :], ALU.add).then_inc(M["sum"], 1)
                for g in range(SUB):
                    dve.wait_ge(M["sum"], 2 * t.n + g // 2 + 1)
                    mm = dve.bn_stats(stats[:, s, g, :], d_rows[:, s, g, :])
                mm.then_inc(M["stats"], 1)
                row_sums(M, t, s, P, SUB)
                row_square(M, t, s, P, SUB)
                row_variance(M, t, s, P, SUB)
                dve.wait_ge(M["variance"], t.n + 1)
                dve.tensor_scalar(spread[:, s, 0, 0:SUB], moment[:, s, 4, 0:SUB], EPS, None, ALU.add).then_inc(M["spread"], 1)
                dve.wait_ge(M["sd"], t.n + 1)
                dve.reciprocal(inv[:, s, 0, 0:SUB], sd[:, s, 0, 0:SUB]).then_inc(M["inv"], 1)
                dve.wait_ge(M["inv"], t.n + 1)
                dve.scalar_tensor_tensor(out=neg[:, s, 0, 0:SUB], in0=moment[:, s, 0, 0:SUB], scalar=-0.5,
                                         in1=inv[:, s, 0, 0:SUB], op0=ALU.mult, op1=ALU.mult).then_inc(M["neg"], 1)

            def keys1(t):
                tails(t, M, KEY1)
                compare_keys(t, M)

            def max_edges(t):
                s = t.slot(2)
                wait(dve, M["best_bank"], 2 * (t.n - 1))
                dve.wait_ge(M["same"], t.n + 1)
                if not (t.k is None and t.c == 0):
                    dve.wait_ge(M["best"], 2 * t.n)
                for o in range(KC):
                    dve.wait_ge(M["e"], 2 * t.n + o + 1)
                    first = 0.0 if t.k is None and t.c == 0 else agg[:, 1 - s, o, TE - 1:TE]
                    dve.tensor_tensor_scan(agg[:, s, o, :], same[:, s, :], zt[:, s, o, :], first, ALU.mult,
                                           ALU.max).then_inc(M["best"], 1)

            pipeline(dve, NT, 4, [(0, lambda t: ends(t, M, OTHER1, 2)), (3, last_rows), (1, keys1), (2, max_edges)])


_INS = ['x', 'src', 'dst', 'edge_attr_20', 'L0_gnn_Wf1', 'L0_gnn_bf1', 'L0_gnn_Wf2', 'L0_gnn_bf2', 'L0_gnn_Wu1',
        'L0_gnn_bu1', 'L0_gnn_Wu2', 'L0_gnn_bu2', 'L0_gnn_gamma', 'L0_gnn_beta', 'L1_gnn_theta_w', 'L1_gnn_theta_b',
        'L1_gnn_phi_w', 'L1_gnn_phi_b']
_OUTS = [((50000, 256), 'float32')]


def kernel(**inputs):
    import numpy as _np
    import concourse.bacc as _bacc
    from concourse import mybir as _mybir
    from concourse.bass_utils import run_bass_kernel_spmd as _run

    nc = _bacc.Bacc("TRN2", target_bir_lowering=False, num_devices=1)
    arrays, args = {}, []
    for name in _INS:
        a = _np.ascontiguousarray(inputs[name])
        arrays[f"in_{name}_dram"] = a
        args.append(nc.dram_tensor(f"in_{name}_dram", a.shape, _mybir.dt.from_np(a.dtype), kind="ExternalInput").ap())
    for i, (shape, dtype) in enumerate(_OUTS):
        dt = _mybir.dt.from_np(_np.dtype(dtype))
        args.append(nc.dram_tensor(f"out_{i}_dram", shape, dt, kind="ExternalOutput").ap())
    build(nc, *args)
    r = _run(nc, [arrays], core_ids=[0])
    return r.results[0]["out_0_dram"]
```

```python
from contextlib import ExitStack

import concourse.bass as bass
from concourse import mybir

F32 = mybir.dt.float32
BF16 = mybir.dt.bfloat16
I32 = mybir.dt.int32
U32 = mybir.dt.uint32
ALU = mybir.AluOpType
ACT = mybir.ActivationFunctionType

P = 128
SUB = 4
TE = SUB * P
LO = 256
ROUND = 1.5 * 2.0 ** 31
SKIP = 65536.0
EPS = 1e-5
PAIRS = ((0, 0), (0, 1), (0, 2), (1, 0), (1, 1), (2, 0))


class Tile:

    def __init__(self, c, unroll=1, k=None):
        self.c, self.unroll, self.k = c, unroll, k
        self.n = c if k is None else k * unroll + c

    def slot(self, m):
        return self.c % m

    def turn(self, m):
        return self.c // m if self.k is None else self.k * (self.unroll // m) + self.c // m


def pipeline(eng, count, unroll, stages):
    lags = max(lag for lag, _ in stages)

    def step(c, k=None):
        for lag, body in stages:
            if k is not None or 0 <= c - lag < count:
                body(Tile(c - lag, unroll, k))

    first = lags + max(unroll, 2)
    rounds = (count - 1 - first) // unroll
    for c in range(first):
        step(c)
    with eng.Fori(0, rounds) as k:
        for j in range(unroll):
            step(first + j, k)
    for c in range(first + rounds * unroll, count + lags):
        step(c)


def wait(eng, sem, value, most=None):
    if isinstance(value, int):
        if most is not None:
            value = min(value, most)
        if value <= 0:
            return
    eng.wait_ge(sem, value)


def build(nc, x, src, dst, attr, wf1, bf1, wf2, bf2, wu1, bu1, wu2, bu2, gamma, beta,
          theta_w, theta_b, phi_w, phi_b, out):
    N, D = x.shape
    E, G = attr.shape
    KC = D // P
    NT = -(-E // TE)
    COLS = NT * SUB
    EP = NT * TE
    PAD_KEY = N + 47
    assert G * len(PAIRS) <= P
    HI = PAD_KEY // LO + 1
    assert EP < SKIP - 1 and P < HI
    assert N <= PAD_KEY < LO * LO and KC == 2 and D == LO
    W1 = 4
    W0 = D + W1
    AT = [D, 0]
    OTHER0, KEY0 = AT[0], AT[0] + 2
    OTHER1, KEY1 = AT[1], AT[1] + 2
    R = 5
    SLOTS = 6
    NN = N // (P * R)
    TAIL = N - NN * P * R
    AHEAD = SLOTS - 1
    NR = NN * R + (TAIL > 0)
    assert 0 < TAIL <= P and NR <= KC * D

    ctx = ExitStack()
    with ctx:
        def sb(name, shape, dt=F32):
            return ctx.enter_context(nc.sbuf_tensor(name, shape, dt))

        def ps(name, shape, dt=F32):
            return ctx.enter_context(nc.psum_tensor(name, shape, dt))

        def sem(name):
            return ctx.enter_context(nc.semaphore(name))

        sorted0 = nc.dram_tensor("sorted0", (EP + 1, W0), F32).ap()
        sorted1 = nc.dram_tensor("sorted1", (EP + 1, W1), F32).ap()
        d_sorted = nc.dram_tensor("d_sorted", (EP, D), F32).ap()
        last_edges = nc.dram_tensor("last_edges", (LO * LO,), F32).ap()
        x1_tab = nc.dram_tensor("x1_tab", (N, D), F32).ap()

        iota_f = sb("iota_f", [P, LO])
        iota_b = sb("iota_b", [P, LO], BF16)
        row_id = sb("row_id", [P, 2])
        ident = sb("ident", [P, P])
        ident_b = sb("ident_b", [P, P], BF16)
        before = sb("before", [P, P])
        before_b = sb("before_b", [P, P], BF16)
        ones = sb("ones", [P, LO])
        zeros_b = sb("zeros_b", [P, TE], BF16)
        pad_row = sb("pad_row", [1, W0])

        wf1_s = sb("wf1_s", [P, D], BF16)
        wf2_s = sb("wf2_s", [P, KC, D])
        wu1_s = sb("wu1_s", [P, KC, D])
        wu2_s = sb("wu2_s", [P, KC, D])
        theta_n = sb("theta_n", [P, KC, D])
        phi_n = sb("phi_n", [P, KC, D])
        node_row = phi_n[:, :, :].rearrange("p c d -> p (c d)")[:, 0:NR].bitcast(I32)
        w_dst = sb("w_dst", [P, KC, D])
        w_src = sb("w_src", [P, KC, D])
        cols = sb("cols", [P, 5, KC])
        rows_b = sb("rows_b", [P, 4, D])
        shift = sb("shift", [P, D])
        bn_scale = sb("bn_scale", [P, D])
        bn_shift = sb("bn_shift", [P, D])
        bn_mean = sb("bn_mean", [P, D])
        bn_tmp = sb("bn_tmp", [P, D])
        z0_wide = bn_mean[:, :].rearrange("p (c o) -> p c o", c=KC)
        h0 = bn_tmp
        bn_sum = sb("bn_sum", [P, 2, D])

        key_i = sb("key_i", [P, 2, COLS], I32)
        other_i = sb("other_i", [P, 2, COLS], I32)
        next_dst = sb("next_dst", [P, COLS], I32)
        inversions = sb("inversions", [P, COLS])
        out_of_order = sb("out_of_order", [P, 2])
        out_of_order_i = sb("out_of_order_i", [P, 2], I32)
        part_i = sb("part_i", [P, 2, COLS], I32)
        part_f = sb("part_f", [P, NT, 2, SUB])
        high_b = sb("high_b", [P, COLS], BF16)
        pay = sb("pay", [P, 2, COLS, W1])
        parts = sb("parts", [P, 2, 2, SUB])
        msg_hot = sb("msg_hot", [P, KC * TE])
        msg = msg_hot[:, :].rearrange("p (c e) -> p c e", c=KC)
        hot_hi = msg_hot[:, :].bitcast(BF16).rearrange("p (s g k) -> p s g k", s=2, g=SUB)
        hot_lo = sb("hot_lo", [P, 2, SUB, LO], BF16)
        high_row = sb("high_row", [P, 2, TE], BF16)
        hot_hi_t = sb("hot_hi_t", [P, 2, 2, TE], BF16)
        acc_earlier = sb("acc_earlier", [P, 2 * SUB * D])
        acc_d, acc_q = (acc_earlier[:, i * SUB * D:(i + 1) * SUB * D].rearrange("p (g d) -> p g d", g=SUB)
                        for i in range(2))
        earlier = acc_earlier[:, :].bitcast(BF16).rearrange("p (s g e) -> p s g e", s=2, g=SUB)
        tab_hi = sb("tab_hi", [P, 2, 2 * LO], BF16)
        tab_lo = sb("tab_lo", [P, 2, 2 * LO], BF16)
        cnt_s = sb("cnt_s", [P, 2, LO])
        incl = sb("incl", [P, 2, LO])
        tot = sb("tot", [P, 2])
        off = sb("off", [P, 2])
        base = sb("base", [P, 2, LO])
        place_f = sb("place_f", [P, 2, SUB])
        place_i = sb("place_i", [P, 2, SUB], I32)
        picked = sb("picked", [P, SUB, LO], BF16)
        pay_t = sb("pay_t", [P, 2, SUB, W0])

        edge = sb("edge", [P, 4, SUB, W0])
        ends_i = sb("ends_i", [P, 4, 2, SUB], I32)
        next_key = sb("next_key", [P, 4, SUB])
        tail_f = sb("tail_f", [P, 4, SUB])
        tail_i = sb("tail_i", [P, 4, SUB], I32)
        is_last = sb("is_last", [P, 4, SUB])
        goes_on = sb("goes_on", [P, 4, SUB], BF16)
        same_row = sb("same_row", [P, 2, TE + 1])
        attr_c = sb("attr_c", [P, 2, SUB, P], BF16)
        attr_left = sb("attr_left", [P, 3, SUB, G])
        attr_t = sb("attr_t", [P, TE], BF16)
        gathered_all = sb("gathered_all", [P, 2 * SUB * D])
        gathered = gathered_all[:, :].rearrange("p (s g d) -> p s g d", s=2, g=SUB)
        wf1_left = gathered_all[0:G, 0:3 * D].rearrange("p (j d) -> p j d", j=3)
        filt_parts = gathered_all[0:G, 3 * D:6 * D].bitcast(BF16)[:, 0:3 * D].rearrange("p (j d) -> p j d", j=3)
        h1_xt = sb("h1_xt", [P, 4 * KC * TE])
        h1 = h1_xt[:, 0:2 * KC * TE].rearrange("p (s c e) -> p s c e", s=2, c=KC)
        xt = h1_xt[:, 2 * KC * TE:4 * KC * TE].rearrange("p (s c e) -> p s c e", s=2, c=KC)
        xt2 = h1
        layer_all = sb("layer_all", [P, 8 * KC * TE])
        agg, zt = (layer_all[:, 2 * i * KC * TE:2 * (i + 1) * KC * TE].rearrange("p (s c e) -> p s c e", s=2, c=KC)
                   for i in range(2))
        d_rows, sq = (layer_all[:, 2 * i * KC * TE:2 * (i + 1) * KC * TE].rearrange("p (s g d) -> p s g d", s=2, g=SUB)
                      for i in range(2, 4))
        node_x_all = sb("node_x_all", [P, SLOTS * R * D])
        node_d_all = layer_all[:, 0:SLOTS * R * D]
        node_x = node_x_all[:, :].rearrange("p (s r d) -> p s r d", s=SLOTS, r=R)
        node_d = node_d_all.rearrange("p (s r d) -> p s r d", s=SLOTS, r=R)
        attr_s = node_x_all[:, 0:COLS * G].rearrange("p (t g) -> p t g", g=G)
        gathered2 = node_x_all[:, 0:4 * SUB * D].rearrange("p (s g d) -> p s g d", s=4, g=SUB)
        last_edge = sb("last_edge", [P, NR])
        node_i = sb("node_i", [P, SLOTS, R], I32)
        stats = sb("stats", [P, SLOTS, R, 6])
        moment = sb("moment", [P, SLOTS, 5, R])
        spread = sb("spread", [P, SLOTS, 2, R])
        sd = sb("sd", [P, SLOTS, 2, R])
        inv = sb("inv", [P, SLOTS, 2, R])
        neg = sb("neg", [P, SLOTS, 2, R])

        bank = [ps(f"bank{i}", [P, TE]) for i in range(8)]

        s_pad = sem("padding_set")
        s_const = sem("constants_made")
        FILLS, MASKS, ATTR_ZERO, WF1_ZERO, LAST_ZERO, PARTS_ZERO = 6, 8, 9, 10, 11, 13
        s_const_v = sem("constants_cast")
        s_key_in = sem("keys_loaded")
        s_attr_in = sem("attributes_loaded")
        s_w_in = sem("weights_loaded")
        s_filt_in = sem("filter_weights_loaded")
        s_filt_parts = sem("filter_weights_split")
        s_filt_w = sem("filter_weight_parts_placed")
        s_last = sem("last_edges_in_node_order")
        s_w2 = sem("phi_minus_theta")
        s_wt = sem("weights_transposed")
        s_wt_used = sem("weights_copied")
        s_z0 = sem("z0_ready")
        s_h0 = sem("h0_in_psum")
        s_vector = sem("vector_step")
        s_pay = sem("payload_words_laid_out")

        def sort_sems(a):
            return {k: sem(f"{k}{a}") for k in (
                "split", "parts_c", "hot_c", "counted", "prefix", "offset", "base_in", "parts_s", "hot_s",
                "high_bank", "high_ready", "ready", "tab_hi_ready", "tab_ready", "added", "looked_up",
                "place_found", "place_ready", "pay_ready") + (
                "attr_part", "attr_c", "attr_bank", "attr_t", "h1_bank", "h1", "filt_bank", "filt") * (a == 0)} | {
                    "scattered": [sem(f"scattered{a}_{i}") for i in range(2)]}

        sort_s = [sort_sems(0), sort_sems(1)]

        def layer_sems(a, names):
            return {k: sem(f"{k}{a}") for k in names} | {
                "edges_in": [sem(f"edges_in{a}_{i}") for i in range(4)],
                "gathered": [sem(f"gathered{a}_{i}") for i in range(2)],
                "stored": [sem(f"rows_stored{a}_{i}") for i in range(2)]}

        l0 = layer_sems(0, ("same_bank", "same_row", "msg", "msg_bank", "agg", "z_bank", "z", "h_bank", "d", "sq", "stats",
                            "tails", "tail_step", "ends"))
        l1 = layer_sems(1, ("same_bank", "same_row", "xt_bank", "xt", "xt2_bank", "xt2", "e_bank", "e",
                            "best", "best_bank", "sum", "stats", "moments", "spread", "sd", "inv", "neg", "rows",
                            "tails", "tail_step", "ends"))
        s_sum = sem("column_sums")
        s_bn = sem("batch_norm_step")
        s_bn_sd = sem("batch_norm_sd")
        nd = {k: sem(f"node_{k}") for k in ("index", "cleared", "z", "stats", "moments", "spread", "sd",
                                            "inv", "neg", "rows")}
        nd_in = [sem(f"node_in_{i}") for i in range(SLOTS)]
        nd_gathered = [sem(f"node_gathered_{i}") for i in range(SLOTS)]
        nd_out = [sem(f"node_out_{i}") for i in range(SLOTS)]
        s_pad_row = sem("pad_rows_written")
        s_order = sem("order_step")
        s_order_pe = sem("inversions_summed")
        s_in_order = sem("edges_stored_in_order")
        s_placed1 = sem("sorted1_complete")

        sorted_rows = [t[0:EP, :].rearrange("(t s p) w -> t p s w", s=SUB, p=P) for t in (sorted0, sorted1)]
        next_rows = [t[1:EP + 1, :].rearrange("(t s p) w -> t p s w", s=SUB, p=P) for t in (sorted0, sorted1)]

        def node_tiles(t):
            return t[0:NN * P * R, :].rearrange("(p t r) d -> t p r d", p=P, r=R)

        def node_stage(stage):
            return lambda t: stage(t, TAIL, 1) if t.k is None and t.c == NN else stage(t)

        WT = [W0, W1]
        KEY = [KEY0, KEY1]
        FULL = E // COLS
        REST = E - FULL * COLS

        def halves(a):
            return part_i[:, a, :].rearrange("p (t s) -> p t s", s=SUB)

        block = ctx.enter_context(nc.Block())

        @block.sync
        def _(sp):
            sp.wait_ge(s_pad, 1)
            for tile, slot, arr in ((key_i, 0, src), (key_i, 1, dst), (other_i, 0, dst), (other_i, 1, src)):
                sp.dma_start(tile[0:FULL, slot, :],
                             arr[0:FULL * COLS].rearrange("(p t) -> p t", t=COLS)).then_inc(s_key_in, 16)
                sp.dma_start(tile[FULL:FULL + 1, slot, 0:REST],
                             arr[FULL * COLS:E].rearrange("(p t) -> p t", p=1)).then_inc(s_key_in, 16)
            sp.dma_start(next_dst[0:FULL, :],
                         dst[1:FULL * COLS + 1].rearrange("(p t) -> p t", t=COLS)).then_inc(s_key_in, 16)
            sp.dma_start(next_dst[FULL:FULL + 1, 0:REST - 1],
                         dst[FULL * COLS + 1:E].rearrange("(p t) -> p t", p=1)).then_inc(s_key_in, 16)
            sp.dma_start(wf1_left[0:G, 0, :], wf1).then_inc(s_filt_in, 16)
            for tile, w in ((wf2_s, wf2), (wu1_s, wu1), (wu2_s, wu2), (theta_n, theta_w), (phi_n, phi_w)):
                sp.dma_start(tile[:, :, :], w.rearrange("(c p) d -> p c d", p=P)).then_inc(s_w_in, 16)
            for j, b in enumerate((bf1, bu1, theta_b, phi_b)):
                sp.dma_start(cols[:, j, :], b.rearrange("(c p) -> p c", p=P),
                             allow_slow_non_contiguous=True).then_inc(s_w_in, 16)
            for j, b in enumerate((bu2, gamma, beta, bf2)):
                sp.dma_start(rows_b[:, j, :],
                             b.rearrange("(a d) -> a d", a=1).to_broadcast([P, D])).then_inc(s_w_in, 16)
            sp.wait_ge(s_const, ATTR_ZERO)
            sp.dma_start(attr_s[0:FULL, :, :],
                         attr[0:FULL * COLS, :].rearrange("(p t) g -> p t g", t=COLS)).then_inc(s_attr_in, 16)
            sp.dma_start(attr_s[FULL:FULL + 1, 0:REST, :],
                         attr[FULL * COLS:E, :].rearrange("(p t) g -> p t g", p=1)).then_inc(s_attr_in, 16)
            sp.wait_ge(s_const, WF1_ZERO)
            sp.wait_ge(s_filt_parts, 5)
            for k, (_, j) in enumerate(PAIRS):
                sp.dma_start(wf1_s[k * G:(k + 1) * G, :], filt_parts[0:G, j, :]).then_inc(s_filt_w, 16)
            sp.wait_ge(s_const, MASKS)
            sp.dma_start(sorted0[EP:EP + 1, :], pad_row[:, :]).then_inc(s_pad_row, 16)
            sp.dma_start(sorted1[EP:EP + 1, :], pad_row[:, 0:W1]).then_inc(s_pad_row, 16)
            sp.wait_ge(s_pay, 1)
            sp.dma_start(sorted1[0:EP, :].rearrange("(p t) w -> p (t w)", p=P),
                         pay[:, 1, :, :].rearrange("p t w -> p (t w)")).then_inc(s_in_order, 16)
            sp.wait_ge(s_vector, 5)
            sp.dma_start(last_edges.rearrange("(c p k) -> p c k", p=P, k=LO), cnt_s[:, :, :]).then_inc(s_last, 16)
            sp.wait_ge(s_last, 16)
            sp.wait_ge(s_const, LAST_ZERO)
            sp.dma_start(last_edge[:, 0:NN * R],
                         last_edges[0:NN * P * R].rearrange("(p j) -> p j", p=P)).then_inc(s_last, 16)
            sp.dma_start(last_edge[0:TAIL, NN * R:NR],
                         last_edges[NN * P * R:N].rearrange("(p j) -> p j", j=1)).then_inc(s_last, 16)

            def load_edges(a, ly):
                def body(t):
                    s = t.slot(4)
                    wait(sp, ly["tails"], t.n - 3)
                    if a == 0:
                        wait(sp, ly["msg"], t.n - 3)
                    wait(sp, ly["ends"], t.n - 3)
                    if t.k is None and t.c == 0:
                        for i in range(2 * (a == 0)):
                            sp.wait_ge(sort_s[a]["scattered"][i], 16 * SUB * ((NT + 1 - i) // 2))
                        sp.wait_ge(s_pad_row, 32)
                    sp.dma_start(edge[:, s, :, 0:WT[a]], sorted_rows[a][t.n]).then_inc(ly["edges_in"][s], 16)
                    sp.dma_start(next_key[:, s, :], next_rows[a][t.n][:, :, KEY[a]],
                                 allow_slow_non_contiguous=True).then_inc(ly["edges_in"][s], 16)
                return body

            pipeline(sp, NT, 4, [(0, load_edges(0, l0))])

            def load_nodes(t, rows=P, r=R):
                s = t.slot(SLOTS)
                wait(sp, nd_out[s], t.turn(SLOTS) * 32)
                from_x = node_tiles(x)[t.n] if r == R else x[NN * P * R:N, :].rearrange("(p r) d -> p r d", r=1)
                sp.dma_start(node_x[0:rows, s, 0:r, :], from_x).then_inc(nd_in[s], 16)

            pipeline(sp, NN + 1, SLOTS, [(0, node_stage(load_nodes))])
            sp.wait_ge(s_placed1, 1)
            pipeline(sp, NT, 4, [(0, load_edges(1, l1))])

        @block.gpsimd
        def _(pool):
            pool.memset(ones[:, :], 1.0).then_inc(s_const, 1)
            pool.memset(ident[:, :], 0.0).then_inc(s_const, 1)
            pool.memset(before[:, :], 1.0).then_inc(s_const, 1)
            pool.memset(pad_row[:, :], SKIP).then_inc(s_const, 1)
            pool.iota(iota_f[:, :], pattern=[[1, LO]], base=0, channel_multiplier=0,
                      allow_small_or_imprecise_dtypes=True).then_inc(s_const, 1)
            pool.iota(row_id[:, :], pattern=[[P, 2]], base=0, channel_multiplier=1,
                      allow_small_or_imprecise_dtypes=True).then_inc(s_const, 1)
            pool.wait_ge(s_const, FILLS)
            pool.affine_select(out=ident[:, :], in_=ident[:, :], compare_op=ALU.not_equal, fill=1.0, base=0,
                               pattern=[[-1, P]], channel_multiplier=1).then_inc(s_const, 1)
            pool.affine_select(out=before[:, :], in_=before[:, :], compare_op=ALU.is_gt, fill=0.0, base=0,
                               pattern=[[1, P]], channel_multiplier=-1).then_inc(s_const, 1)
            pool.memset(attr_s, 0.0).then_inc(s_const, 1)
            pool.memset(wf1_s[:, :], 0.0).then_inc(s_const, 1)
            pool.memset(last_edge[:, :], 0.0).then_inc(s_const, 1)
            pool.memset(pay[:, :, :, :], 0.0).then_inc(s_const, 1)

            pool.wait_ge(s_filt_in, 16)
            for j in range(3):
                pool.tensor_copy(filt_parts[:, j, :], wf1_left[:, j, :]).then_inc(s_filt_parts, 1)
                if j < 2:
                    pool.wait_ge(s_filt_parts, 2 * j + 1)
                    pool.tensor_tensor(wf1_left[:, j + 1, :], wf1_left[:, j, :], filt_parts[:, j, :],
                                       ALU.subtract).then_inc(s_filt_parts, 1)
                    pool.wait_ge(s_filt_parts, 2 * j + 2)
            pool.wait_ge(s_w_in, 16 * 13)
            pool.tensor_tensor(phi_n[:, :, :], phi_n[:, :, :], theta_n[:, :, :], ALU.subtract).then_inc(s_w2, 1)
            pool.tensor_tensor(cols[:, 4, :], cols[:, 2, :], cols[:, 3, :], ALU.add).then_inc(s_w2, 1)
            pool.memset(attr_c[:, :, :, :], 0.0).then_inc(s_const, 1)
            pool.wait_ge(s_const, PARTS_ZERO)
            pool.wait_ge(s_key_in, 16 * 10)
            pool.tensor_copy(pay[:, 1, :, 1], other_i[:, 0, :])
            for a in range(2):
                pool.tensor_copy(pay[:, a, :, 2], key_i[:, a, :])
                mm = pool.tensor_copy(pay[:, a, :, 0], other_i[:, a, :])
            mm.then_inc(s_pay, 1)
            pool.wait_ge(s_attr_in, 32)

            def attr_parts(t):
                s, so = t.slot(2), sort_s[0]
                parts_of = attr_c[:, s, :, 0:G * len(PAIRS)].rearrange("p s (k g) -> p s k g", g=G)
                wait(pool, so["attr_bank"], t.n - 1)
                pool.nop(nofuse=True)
                pool.tensor_copy(attr_left[:, 0, :, :], attr_s[:, bass.ds(t.n * SUB, SUB), :]).then_inc(so["attr_part"], 1)
                first = 0
                for j in range(3):
                    pool.wait_ge(so["attr_part"], 5 * t.n + 2 * j + 1)
                    pool.nop(nofuse=True)
                    times = sum(i == j for i, _ in PAIRS)
                    mm = pool.tensor_copy(parts_of[:, :, first:first + times, :], attr_left[:, j, :, :].rearrange(
                        "p s (k g) -> p s k g", k=1).to_broadcast([P, SUB, times, G]))
                    if j == 2:
                        mm.then_inc(so["attr_c"], 1)
                        break
                    mm.then_inc(so["attr_part"], 1)
                    pool.wait_ge(so["attr_part"], 5 * t.n + 2 * j + 2)
                    pool.nop(nofuse=True)
                    pool.tensor_tensor(attr_left[:, j + 1, :, :], attr_left[:, j, :, :], parts_of[:, :, first, :],
                                       ALU.subtract).then_inc(so["attr_part"], 1)
                    first += times

            def scatter_payload(a, so, table):
                def body(t):
                    s = t.slot(2)
                    pool.wait_ge(so["pay_ready"], t.n + 1)
                    if a == 0:
                        pool.wait_ge(so["filt"], 2 * t.n + 2)
                    pool.wait_ge(so["place_ready"], t.n + 1)
                    pool.nop(nofuse=True)
                    for g in range(SUB):
                        pool.indirect_dma_start(
                            out=table, out_offset=bass.IndirectOffsetOnAxis(
                                ap=place_i[:, s, g:g + 1].bitcast(U32), axis=0),
                            in_=pay_t[:, s, g, 0:WT[a]], in_offset=None).then_inc(so["scattered"][s], 16)
                return body

            def gather(idx, table, to, done):
                for g in range(SUB):
                    pool.indirect_dma_start(
                        out=to[:, g, :], out_offset=None, in_=table,
                        in_offset=bass.IndirectOffsetOnAxis(ap=idx[g], axis=0)).then_inc(done, 16)

            def scatter_tails(t):
                s = t.slot(2)
                pool.wait_ge(l1["rows"], t.n + 1)
                pool.nop(nofuse=True)
                for g in range(SUB):
                    pool.indirect_dma_start(
                        out=out, out_offset=bass.IndirectOffsetOnAxis(
                            ap=tail_i[:, t.slot(4), g:g + 1].bitcast(U32), axis=0),
                        in_=sq[:, s, g, :], in_offset=None, bounds_check=N - 1,
                        oob_is_err=False).then_inc(l1["stored"][s], 16)

            pipeline(pool, NT, 2, [(0, attr_parts), (3, scatter_payload(0, sort_s[0], sorted0))])

            def gather0(t):
                s = t.slot(2)
                wait(pool, l0["msg_bank"], 2 * (t.n - 1))
                pool.wait_ge(l0["ends"], t.n + 1)
                pool.nop(nofuse=True)
                gather([ends_i[:, t.slot(4), 0, g:g + 1].bitcast(U32) for g in range(SUB)], x,
                       gathered[:, s], l0["gathered"][s])

            pipeline(pool, NT, 4, [(0, gather0)])

            def gather_nodes(t, rows=P, r=R):
                s = t.slot(SLOTS)
                wait(pool, nd_out[s], 32 * t.turn(SLOTS))
                pool.nop(nofuse=True)
                pool.memset(node_d[0:rows, s, 0:r, :], 0.0).then_inc(nd["cleared"], 1)
                pool.wait_ge(nd["cleared"], t.n + 1)
                pool.wait_ge(nd["index"], t.n + 1)
                pool.nop(nofuse=True)
                for j in range(r):
                    pool.indirect_dma_start(
                        out=node_d[0:rows, s, j, :], out_offset=None, in_=d_sorted,
                        in_offset=bass.IndirectOffsetOnAxis(ap=node_i[0:rows, s, j:j + 1].bitcast(U32), axis=0),
                        bounds_check=EP - 1, oob_is_err=False).then_inc(nd_gathered[s], 16)

            pool.wait_ge(l0["stats"], NT)
            for i in range(2):
                pool.wait_ge(l0["stored"][i], 16 * ((NT + 1 - i) // 2))
            pipeline(pool, NN + 1, SLOTS, [(0, node_stage(gather_nodes))])
            pool.wait_ge(s_in_order, 16)
            pool.wait_ge(s_order, 3)
            with pool.If(pool.value_load(out_of_order_i[0:1, 0:1]) > 0):
                pipeline(pool, NT, 2, [(0, scatter_payload(1, sort_s[1], sorted1))])
                for i in range(2):
                    pool.wait_ge(sort_s[1]["scattered"][i], 16 * SUB * ((NT + 1 - i) // 2))
            pool.sem_inc(s_placed1, 1)

            def gather1(t):
                s = t.slot(2)
                wait(pool, l1["xt_bank"], 2 * (t.n - 1))
                wait(pool, l1["sum"], 2 * (t.n - 3))
                pool.wait_ge(l1["ends"], t.n + 1)
                pool.nop(nofuse=True)
                q = t.slot(4)
                gather([ends_i[:, q, 0, g:g + 1].bitcast(U32) for g in range(SUB)], x1_tab,
                       gathered[:, s], l1["gathered"][s])
                gather([ends_i[:, q, 1, g:g + 1].bitcast(U32) for g in range(SUB)], x1_tab,
                       gathered2[:, q], l1["gathered"][s])

            for s in range(SLOTS):
                pool.wait_ge(nd_out[s], 32 * ((NN + 1 + SLOTS - 1 - s) // SLOTS))
            pipeline(pool, NT, 4, [(0, gather1), (3, scatter_tails)])
            for i in range(2):
                pool.wait_ge(l1["stored"][i], 16 * SUB * ((NT + 1 - i) // 2))

        tab_bank = bank[0]
        high_bank = bank[1][:, 0:TE // 2].bitcast(BF16)
        place_bank = [bank[2], bank[3]]
        off_bank = bank[2]
        attr_bank = bank[4][:, 0:TE // 2].bitcast(BF16)
        h1_bank = [bank[5], bank[6]]
        same_bank0, same_bank1 = (bank[i][:, 0:TE // 2].bitcast(BF16) for i in (4, 7))
        filt_bank = [bank[7], bank[4]]

        @block.tensor
        def _(pe):
            def add_counts(s, last_sem):
                for g in range(SUB):
                    for c in range(2):
                        mm = pe.matmul(tab_bank[0:min(P, HI - c * P), c * LO:(c + 1) * LO],
                                       hot_hi[:, s, g, c * P:min((c + 1) * P, HI)],
                                       hot_lo[:, s, g, :], start=False, stop=(g == SUB - 1 and c == 1),
                                       skip_group_check=True)
                mm.then_inc(last_sem, 1)

            def count_edges(a, so):
                pe.matmul(tab_bank[:, :], zeros_b[:, 0:P], zeros_b[:, :], start=True, stop=False, skip_group_check=True)

                def count(t):
                    pe.wait_ge(so["hot_c"], t.n + 1)
                    add_counts(t.slot(2), so["counted"])

                pipeline(pe, NT, 2, [(0, count)])

            def place_edges(a, so):
                pe.wait_ge(so["prefix"], 4)
                pe.matmul(off_bank[:, 0:2], before[:, :], tot[:, :], start=True, stop=False, skip_group_check=True)
                pe.matmul(off_bank[:, 1:2], ones[:, 0:P], tot[:, 0:1], start=False, stop=True,
                          skip_group_check=True).then_inc(so["offset"], 1)
                pe.wait_ge(so["prefix"], 7)
                pe.matmul(tab_bank[:, 0:LO], ident[:, :], base[:, 0, :], start=True, stop=False, skip_group_check=True)
                pe.matmul(tab_bank[:, LO:2 * LO], ident[:, :], base[:, 1, :], start=False, stop=False,
                          skip_group_check=True).then_inc(so["base_in"], 1)

                def high_rows(t):
                    wait(pe, so["high_ready"], t.n)
                    for g in range(SUB):
                        mm = pe.transpose(high_bank[:, g * P:(g + 1) * P],
                                          high_b[:, bass.ds(t.n * SUB + g, 1)].to_broadcast([P, P]), ident_b[:, :])
                    mm.then_inc(so["high_bank"], 1)

                def attr_rows(t):
                    pe.wait_ge(so["attr_c"], t.n + 1)
                    wait(pe, so["attr_t"], t.n)
                    wait(pe, so["filt"], 2 * (t.n - 1))
                    for g in range(SUB):
                        mm = pe.transpose(attr_bank[:, g * P:(g + 1) * P], attr_c[:, t.slot(2), g, :], ident_b[:, :])
                    mm.then_inc(so["attr_bank"], 1)

                def filter_in(t):
                    pe.wait_ge(so["attr_t"], t.n + 1)
                    for o in range(KC):
                        wait(pe, so["h1"], 2 * (t.n - 1) + o + 1)
                        pe.matmul(h1_bank[o][:, :], wf1_s[:, o * P:(o + 1) * P], attr_t[:, :],
                                  start=True, stop=True).then_inc(so["h1_bank"], 1)

                def filter_out(t):
                    pe.wait_ge(so["h1"], 2 * (t.n + 1))
                    for j in range(2):
                        wait(pe, so["filt"], 2 * (t.n - 1) + j + 1)
                        if j == 1:
                            wait(pe, so["attr_t"], t.n + 2, NT)
                        for g in range(2 * j, 2 * j + 2):
                            for c in range(KC):
                                mm = pe.matmul(filt_bank[j][:, (g % 2) * D:(g % 2 + 1) * D],
                                               h1[:, t.slot(2), c, g * P:(g + 1) * P], wf2_s[:, c, :],
                                               start=(c == 0), stop=(c == KC - 1))
                        mm.then_inc(so["filt_bank"], 1)

                def update_table(t):
                    pe.wait_ge(so["tab_ready"], t.n + 1)
                    pe.wait_ge(so["hot_s"], t.n + 1)
                    add_counts(t.slot(2), so["added"])

                def look_up(t):
                    s = t.slot(2)
                    pe.wait_ge(so["ready"], t.n + 1)
                    for g in range(SUB):
                        if g % 2 == 0:
                            wait(pe, so["place_found"], 2 * (t.n - 1) + g // 2 + 1)
                        to = place_bank[g // 2][:, (g % 2) * LO:(g % 2 + 1) * LO]
                        for c in range(2):
                            hot = hot_hi_t[:, s, c, g * P:(g + 1) * P]
                            pe.matmul(to, hot, tab_hi[:, s, c * LO:(c + 1) * LO], start=(c == 0), stop=False)
                            pe.matmul(to, hot, tab_lo[:, s, c * LO:(c + 1) * LO], start=False, stop=False)
                        for e in range(g + 1):
                            mm = pe.matmul(to, earlier[:, s, e, g * P:(g + 1) * P], hot_lo[:, s, e, :],
                                           start=False, stop=(e == g))
                        if g % 2:
                            mm.then_inc(so["looked_up"], 1)

                if a == 0:
                    pipeline(pe, NT, 2, [(2, filter_out), (1, filter_in), (2, update_table), (2, look_up), (0, high_rows),
                                         (0, attr_rows)])
                else:
                    pipeline(pe, NT, 2, [(2, update_table), (2, look_up), (0, high_rows)])

            pe.wait_ge(s_const, MASKS)
            pe.wait_ge(s_const_v, 5)
            count_edges(0, sort_s[0])
            pe.wait_ge(s_w_in, 16 * 13)
            pe.wait_ge(s_w2, 1)
            for j, w in enumerate((theta_n, phi_n)):
                for c in range(KC):
                    for o in range(KC):
                        mm = pe.transpose(bank[1 + 2 * j + c][:, o * P:(o + 1) * P], w[:, o, c * P:(c + 1) * P],
                                          ident[:, :])
            mm.then_inc(s_wt, 1)
            pe.wait_ge(s_z0, 1)
            for c in range(KC):
                mm = pe.matmul(bank[5][:, 0:D], z0_wide[:, c, :], wu2_s[:, c, :], start=(c == 0), stop=(c == KC - 1))
            mm.then_inc(s_h0, 1)
            pe.wait_ge(s_wt_used, 4)
            pe.wait_ge(s_vector, 2)
            pe.wait_ge(s_filt_w, 16 * len(PAIRS))
            place_edges(0, sort_s[0])
            pe.wait_ge(sort_s[0]["place_found"], 2 * NT)
            pe.wait_ge(sort_s[0]["filt"], 2 * NT)
            pe.wait_ge(s_order, 2)
            pe.matmul(bank[7][:, 0:1], ones[:, 0:P], out_of_order[:, 0:1], start=True, stop=True).then_inc(s_order_pe, 1)

            L = l0

            def same_rows(ly, bank):
                def body(t):
                    wait(pe, ly["same_row"], t.n)
                    pe.wait_ge(ly["tails"], t.n + 1)
                    for g in range(SUB):
                        mm = pe.transpose(bank[:, g * P:(g + 1) * P],
                                          goes_on[:, t.slot(4), g:g + 1].to_broadcast([P, P]), ident_b[:, :])
                    mm.then_inc(ly["same_bank"], 1)
                return body

            def update_in(t):
                s = t.slot(2)
                pe.wait_ge(L["agg"], 2 * (t.n + 1))
                for o in range(KC):
                    wait(pe, L["z"], 2 * (t.n - 1) + o + 1)
                    for c in range(KC):
                        mm = pe.matmul(bank[o][:, :], wu1_s[:, c, o * P:(o + 1) * P], agg[:, s, c, :],
                                       start=(c == 0), stop=(c == KC - 1))
                    mm.then_inc(L["z_bank"], 1)

            def update_out(t):
                s = t.slot(2)
                pe.wait_ge(L["z"], 2 * (t.n + 1))
                for j in range(2):
                    wait(pe, L["d"], 2 * (t.n - 1) + j + 1)
                    for g in range(2 * j, 2 * j + 2):
                        for c in range(KC):
                            mm = pe.matmul(bank[2 + j][:, (g % 2) * D:(g % 2 + 1) * D],
                                           zt[:, s, c, g * P:(g + 1) * P], wu2_s[:, c, :],
                                           start=(c == 0), stop=(c == KC - 1))
                    mm.then_inc(L["h_bank"], 1)

            def messages(t):
                s = t.slot(2)
                pe.wait_ge(L["msg"], t.n + 1)
                for c in range(KC):
                    wait(pe, L["agg"], 2 * (t.n - 1) + c + 1)
                    for g in range(SUB):
                        mm = pe.transpose(bank[5 + c][:, g * P:(g + 1) * P],
                                          gathered[:, s, g, c * P:(c + 1) * P], ident[:, :])
                    mm.then_inc(L["msg_bank"], 1)

            pipeline(pe, NT, 4, [(3, update_in), (1, messages), (3, update_out), (1, same_rows(L, same_bank0))])

            pe.wait_ge(L["stats"], NT)
            pe.wait_ge(s_order, 3)
            for j, acc in enumerate((acc_d, acc_q)):
                for g in range(SUB):
                    mm = pe.matmul(bank[7][:, j * D:(j + 1) * D], ones[:, 0:P], acc[:, g, :],
                                   start=(g == 0), stop=(g == SUB - 1))
            mm.then_inc(s_sum, 1)
            pe.wait_ge(s_bn, 1)
            with pe.If(pe.value_load(out_of_order_i[0:1, 0:1]) > 0):
                count_edges(1, sort_s[1])
                place_edges(1, sort_s[1])
                pe.wait_ge(sort_s[1]["place_found"], 2 * NT)

            M = l1

            def edge_rows(t):
                s = t.slot(2)
                pe.wait_ge(M["gathered"][s], 128 * t.turn(2) + 128)
                for c in range(KC):
                    wait(pe, M["xt"], 2 * (t.n - 1) + c + 1)
                    for g in range(SUB):
                        mm = pe.transpose(bank[1 + c][:, g * P:(g + 1) * P],
                                          gathered[:, s, g, c * P:(c + 1) * P], ident[:, :])
                    mm.then_inc(M["xt_bank"], 1)
                for c in range(KC):
                    wait(pe, M["xt2"], 2 * (t.n - 1) + c + 1)
                    for g in range(SUB):
                        mm = pe.transpose(bank[3 + c][:, g * P:(g + 1) * P],
                                          gathered2[:, t.slot(4), g, c * P:(c + 1) * P], ident[:, :])
                    mm.then_inc(M["xt2_bank"], 1)
                wait(pe, M["sum"], 2 * (t.n - 2) + 1)
                same_rows(M, same_bank1)(t)

            def edge_mlp(t):
                s = t.slot(2)
                pe.wait_ge(M["xt"], 2 * (t.n + 1))
                pe.wait_ge(M["xt2"], 2 * (t.n + 1))
                for o in range(KC):
                    wait(pe, M["e"], 2 * (t.n - 1) + o + 1)
                    for c in range(KC):
                        pe.matmul(bank[5 + o][:, :], w_dst[:, c, o * P:(o + 1) * P], xt2[:, s, c, :],
                                  start=(c == 0), stop=False)
                        mm = pe.matmul(bank[5 + o][:, :], w_src[:, c, o * P:(o + 1) * P], xt[:, s, c, :],
                                       start=False, stop=(c == KC - 1))
                    mm.then_inc(M["e_bank"], 1)

            def best_rows(t):
                s = t.slot(2)
                pe.wait_ge(M["best"], 2 * (t.n + 1))
                for j in range(2):
                    wait(pe, M["sum"], 2 * (t.n - 1) + j + 1)
                    if j == 0:
                        wait(pe, M["same_row"], t.n + 2, NT)
                    for g in range(2 * j, 2 * j + 2):
                        for c in range(KC):
                            mm = pe.transpose(bank[7 if j == 0 else 0][:, (g % 2) * D + c * P:(g % 2) * D + (c + 1) * P],
                                              agg[:, s, c, g * P:(g + 1) * P], ident[:, :])
                    mm.then_inc(M["best_bank"], 1)

            pipeline(pe, NT, 4, [(2, best_rows), (0, edge_rows), (1, edge_mlp)])

        @block.scalar
        def _(act):
            act.wait_ge(s_w_in, 16 * 13)
            act.wait_ge(s_const, MASKS)
            for c in range(KC):
                mm = act.activation(z0_wide[:, c, :], before[:, :], ACT.Silu, scale=0.0, bias=cols[:, 1, c:c + 1])
            mm.then_inc(s_z0, 1)
            act.wait_ge(s_wt, 1)
            for j, w in enumerate((w_dst, w_src)):
                for c in range(KC):
                    act.copy(w[:, c, :], bank[1 + 2 * j + c][:, 0:D]).then_inc(s_wt_used, 1)

            def sort(a, so):
                def high_copy(t):
                    s = t.slot(2)
                    act.wait_ge(so["high_bank"], t.n + 1)
                    wait(act, so["ready"], t.n - 1)
                    act.copy(high_row[:, s, :], high_bank).then_inc(so["high_ready"], 1)

                def attr_copy(t):
                    act.wait_ge(so["attr_bank"], t.n + 1)
                    act.copy(attr_t[:, :], attr_bank).then_inc(so["attr_t"], 1)

                def silu_h1(t):
                    s = t.slot(2)
                    wait(act, so["filt_bank"], 2 * (t.n - 1))
                    for o in range(KC):
                        act.wait_ge(so["h1_bank"], 2 * t.n + o + 1)
                        act.activation(h1[:, s, o, :], h1_bank[o][:, :], ACT.Silu,
                                       bias=cols[:, 0, o:o + 1]).then_inc(so["h1"], 1)

                def lay_out(t):
                    s = t.slot(2)
                    wait(act, so["scattered"][s], 64 * t.turn(2))
                    act.copy(pay_t[:, s, :, AT[a]:AT[a] + W1],
                             pay[:, a, bass.ds(t.n * SUB, SUB), :]).then_inc(so["pay_ready"], 1)

                if a == 0:
                    pipeline(act, NT, 2, [(2, lay_out), (1, silu_h1), (0, high_copy), (0, attr_copy)])
                else:
                    pipeline(act, NT, 2, [(0, high_copy), (1, lay_out)])

            act.wait_ge(s_pay, 1)
            sort(0, sort_s[0])

            L = l0

            def same_copy(ly, bank, used):
                def body(t):
                    s = t.slot(2)
                    wait(act, used, 2 * (t.n - 1))
                    if not (t.k is None and t.c == 0):
                        act.wait_ge(ly["same_row"], t.n)
                        act.copy(same_row[:, s, 0:1], same_row[:, 1 - s, TE:TE + 1])
                    act.wait_ge(ly["same_bank"], t.n + 1)
                    act.copy(same_row[:, s, 1:TE + 1], bank).then_inc(ly["same_row"], 1)
                return body

            def silu_z(t):
                s = t.slot(2)
                wait(act, L["h_bank"], 2 * (t.n - 1))
                for o in range(KC):
                    act.wait_ge(L["z_bank"], 2 * t.n + o + 1)
                    act.activation(zt[:, s, o, :], bank[o][:, :], ACT.Silu, bias=cols[:, 1, o:o + 1]).then_inc(L["z"], 1)

            def squares(t):
                s = t.slot(2)
                wait(act, L["stats"], t.n - 1)
                for g in range(SUB):
                    if g % 2 == 0:
                        act.wait_ge(L["d"], 2 * t.n + g // 2 + 1)
                    act.activation(sq[:, s, g, :], d_rows[:, s, g, :], ACT.Square,
                                   scale=is_last[:, t.slot(4), g:g + 1]).then_inc(L["sq"], 1)

            def store_rows(t):
                s = t.slot(2)
                act.wait_ge(L["d"], 2 * (t.n + 1))
                act.dma_start(d_sorted.rearrange("(t g p) d -> t p g d", g=SUB, p=P)[t.n],
                              d_rows[:, s, :, :]).then_inc(L["stored"][s], 16)

            pipeline(act, NT, 4, [(3, silu_z), (4, squares), (4, store_rows), (1, same_copy(L, same_bank0, L["agg"]))])

            act.wait_ge(s_vector, 7)
            act.activation(bn_tmp[:, :], bn_tmp[:, :], ACT.Sqrt).then_inc(s_bn_sd, 1)

            def roots(t, rows=P, r=R):
                s = t.slot(SLOTS)
                act.wait_ge(nd["spread"], t.n + 1)
                act.activation(sd[0:rows, s, :, 0:r], spread[0:rows, s, :, 0:r], ACT.Sqrt).then_inc(nd["sd"], 1)

            def norm_rows(t, rows=P, r=R):
                s = t.slot(SLOTS)
                act.wait_ge(nd["neg"], t.n + 1)
                for j in range(r):
                    act.activation(node_x[0:rows, s, j, :], node_d[0:rows, s, j, :], ACT.Identity,
                                   scale=inv[0:rows, s, 1, j:j + 1], bias=neg[0:rows, s, 1, j:j + 1])
                for j in range(r):
                    mm = act.activation(node_d[0:rows, s, j, :], node_d[0:rows, s, j, :], ACT.Identity,
                                        scale=inv[0:rows, s, 0, j:j + 1], bias=neg[0:rows, s, 0, j:j + 1])
                mm.then_inc(nd["rows"], 1)

            def store_nodes(t, rows=P, r=R):
                s = t.slot(SLOTS)
                act.wait_ge(nd["rows"], t.n + 1)
                for table, norm in ((x1_tab, node_d), (out, node_x)):
                    to = node_tiles(table)[t.n] if r == R else table[NN * P * R:N, :].rearrange("(p r) d -> p r d", r=1)
                    act.dma_start(to, norm[0:rows, s, 0:r, :]).then_inc(nd_out[s], 16)

            pipeline(act, NN + 1, SLOTS, [(0, node_stage(roots)), (1, node_stage(norm_rows)), (2, node_stage(store_nodes))])
            act.wait_ge(s_order, 3)
            with act.If(act.value_load(out_of_order_i[0:1, 0:1]) > 0):
                sort(1, sort_s[1])

            M = l1

            def best_norm(t):
                s = t.slot(2)
                act.wait_ge(M["spread"], t.n + 1)
                act.activation(sd[:, s, 0, 0:SUB], spread[:, s, 0, 0:SUB], ACT.Sqrt).then_inc(M["sd"], 1)
                act.wait_ge(M["neg"], t.n + 1)
                wait(act, M["stored"][s], 64 * t.turn(2))
                for g in range(SUB):
                    mm = act.activation(sq[:, s, g, :], d_rows[:, s, g, :], ACT.Identity,
                                        scale=inv[:, s, 0, g:g + 1], bias=neg[:, s, 0, g:g + 1])
                mm.then_inc(M["rows"], 1)

            def copies(t):
                s = t.slot(2)
                wait(act, M["e_bank"], 2 * (t.n - 1))
                for c in range(KC):
                    act.wait_ge(M["xt_bank"], 2 * t.n + c + 1)
                    act.copy(xt[:, s, c, :], bank[1 + c][:, :]).then_inc(M["xt"], 1)
                for c in range(KC):
                    act.wait_ge(M["xt2_bank"], 2 * t.n + c + 1)
                    act.copy(xt2[:, s, c, :], bank[3 + c][:, :]).then_inc(M["xt2"], 1)
                same_copy(M, same_bank1, M["best"])(t)

            def relu_e(t):
                s = t.slot(2)
                wait(act, M["best"], 2 * (t.n - 1))
                for o in range(KC):
                    act.wait_ge(M["e_bank"], 2 * t.n + o + 1)
                    act.activation(zt[:, s, o, :], bank[5 + o][:, :], ACT.Relu, bias=cols[:, 4, o:o + 1]).then_inc(M["e"], 1)

            pipeline(act, NT, 4, [(0, copies), (2, best_norm), (1, relu_e)])

        @block.vector
        def _(dve):
            dve.memset(key_i[:, :, :], PAD_KEY)
            dve.memset(next_dst[:, :], PAD_KEY)
            dve.memset(other_i[:, :, :], 0).then_inc(s_pad, 1)
            dve.memset(zeros_b[:, :], 0.0).then_inc(s_const_v, 1)
            dve.memset(same_row[:, 0, 0:1], 0.0).then_inc(s_const_v, 1)
            dve.wait_ge(s_const, MASKS)
            dve.tensor_copy(iota_b[:, :], iota_f[:, :]).then_inc(s_const_v, 1)
            dve.tensor_copy(ident_b[:, :], ident[:, :]).then_inc(s_const_v, 1)
            dve.tensor_copy(before_b[:, :], before[:, :]).then_inc(s_const_v, 1)
            dve.wait_ge(s_key_in, 16 * 10)
            dve.wait_ge(s_const_v, 5)

            def split(a, so):
                dve.tensor_scalar(part_i[:, 0, :], key_i[:, a, :], 8, None, ALU.logical_shift_right)
                dve.tensor_scalar(part_i[:, 1, :], key_i[:, a, :], LO - 1, None, ALU.bitwise_and).then_inc(so["split"], 1)
                dve.wait_ge(so["split"], 1)
                dve.tensor_copy(part_f[:, :, 0, :], halves(0))
                dve.tensor_copy(high_b[:, :], part_i[:, 0, :])
                dve.tensor_copy(part_f[:, :, 1, :], halves(1)).then_inc(so["split"], 1)
                dve.wait_ge(so["split"], 2)

            def tile_parts(so, parts_sem, used):
                def body(t):
                    wait(dve, so[used], t.n - 1)
                    dve.tensor_copy(parts[:, t.slot(2), :, :], part_f[:, bass.ds(t.n, 1), :, :].rearrange(
                        "p a c s -> p (a c) s")).then_inc(so[parts_sem], 1)
                return body

            def high_hots(t, so, parts_sem):
                s = t.slot(2)
                dve.wait_ge(so[parts_sem], t.n + 1)
                for g in range(SUB):
                    dve.tensor_scalar(hot_hi[:, s, g, 0:HI], iota_b[:, 0:HI], parts[:, s, 0, g:g + 1], None, ALU.is_equal)

            def low_hots(t, so, hot_sem):
                s = t.slot(2)
                for g in range(SUB):
                    mm = dve.tensor_scalar(hot_lo[:, s, g, :], iota_b[:, :], parts[:, s, 1, g:g + 1], None, ALU.is_equal)
                mm.then_inc(so[hot_sem], 1)

            def sort(a, so):
                def count_high(t):
                    wait(dve, so["counted"], t.n - 1)
                    high_hots(t, so, "parts_c")

                pipeline(dve, NT, 2, [(1, count_high), (0, tile_parts(so, "parts_c", "hot_c")),
                                      (1, lambda t: low_hots(t, so, "hot_c"))])
                dve.wait_ge(so["counted"], NT)
                dve.tensor_copy(cnt_s[:, :, :], tab_bank[:, :].rearrange("p (c k) -> p c k", c=2)).then_inc(so["prefix"], 1)
                dve.wait_ge(so["prefix"], 1)
                for c in range(2):
                    mm = dve.tensor_tensor_scan(incl[:, c, :], ones[:, :], cnt_s[:, c, :], 0.0, ALU.mult, ALU.add)
                mm.then_inc(so["prefix"], 1)
                dve.wait_ge(so["prefix"], 2)
                dve.tensor_tensor(base[:, :, :], incl[:, :, :], cnt_s[:, :, :], ALU.subtract).then_inc(so["prefix"], 1)
                dve.tensor_copy(tot[:, :], incl[:, :, LO - 1]).then_inc(so["prefix"], 1)
                if a == 0:
                    dve.wait_ge(s_h0, 1)
                    dve.tensor_tensor(h0[:, :], bank[5][:, 0:D], rows_b[:, 0, :], ALU.add).then_inc(s_vector, 1)
                    dve.wait_ge(s_vector, 1)
                    dve.tensor_tensor(shift[:, :], rows_b[:, 0, :], h0[:, :], ALU.subtract).then_inc(s_vector, 1)
                dve.wait_ge(so["offset"], 1)
                dve.tensor_copy(off[:, :], off_bank[:, 0:2]).then_inc(so["prefix"], 1)
                dve.wait_ge(so["prefix"], 5)
                for c in range(2):
                    dve.tensor_scalar(base[:, c, :], base[:, c, :], off[:, c:c + 1], None, ALU.add).then_inc(so["prefix"], 1)
                if a == 0:
                    dve.tensor_scalar(incl[:, :, :], cnt_s[:, :, :], 1.0, -SKIP, ALU.min, ALU.mult).then_inc(s_vector, 1)
                    dve.wait_ge(so["prefix"], 7)
                    dve.wait_ge(s_vector, 3)
                    dve.tensor_tensor(cnt_s[:, :, :], cnt_s[:, :, :], base[:, :, :], ALU.add).then_inc(s_vector, 1)
                    dve.wait_ge(s_vector, 4)
                    dve.scalar_tensor_tensor(out=cnt_s[:, :, :], in0=incl[:, :, :], scalar=SKIP - 1, in1=cnt_s[:, :, :],
                                             op0=ALU.add, op1=ALU.add).then_inc(s_vector, 1)

                def prepare_high(t):
                    wait(dve, so["added"], t.n - 1)
                    high_hots(t, so, "parts_s")

                def prepare(t):
                    s = t.slot(2)
                    wait(dve, so["looked_up"], 2 * (t.n - 1))
                    low_hots(t, so, "hot_s")
                    dve.wait_ge(so["high_ready"], t.n + 1)
                    for c in range(2):
                        dve.tensor_scalar(hot_hi_t[:, s, c, :], high_row[:, s, :], row_id[:, c:c + 1], None, ALU.is_equal)
                    for e in range(SUB):
                        mm = dve.scalar_tensor_tensor(
                            out=earlier[:, s, e, e * P:(e + 1) * P], in0=high_row[:, s, e * P:(e + 1) * P],
                            scalar=parts[:, s, 0, e:e + 1], in1=before_b[:, :], op0=ALU.is_equal, op1=ALU.mult)
                        if e < SUB - 1:
                            mm = dve.tensor_scalar(earlier[:, s, e, (e + 1) * P:TE], high_row[:, s, (e + 1) * P:TE],
                                                   parts[:, s, 0, e:e + 1], None, ALU.is_equal)
                    mm.then_inc(so["ready"], 1)

                def read_table(t):
                    s = t.slot(2)
                    if t.k is None and t.c == 0:
                        dve.wait_ge(so["base_in"], 1)
                    else:
                        dve.wait_ge(so["added"], t.n)
                    wait(dve, so["looked_up"], 2 * (t.n - 1))
                    dve.tensor_scalar(tab_hi[:, s, :], tab_bank[:, :], ROUND, ROUND, ALU.add,
                                      ALU.subtract).then_inc(so["tab_hi_ready"], 1)
                    dve.wait_ge(so["tab_hi_ready"], t.n + 1)
                    dve.tensor_tensor(tab_lo[:, s, :], tab_bank[:, :], tab_hi[:, s, :],
                                      ALU.subtract).then_inc(so["tab_ready"], 1)

                def find_place(t):
                    s = t.slot(2)
                    for g in range(SUB):
                        if g % 2 == 0:
                            dve.wait_ge(so["looked_up"], 2 * t.n + g // 2 + 1)
                        mm = dve.tensor_tensor_reduce(
                            out=picked[:, g, :], in0=place_bank[g // 2][:, (g % 2) * LO:(g % 2 + 1) * LO],
                            in1=hot_lo[:, s, g, :], scale=1.0, scalar=0.0, op0=ALU.mult, op1=ALU.add,
                            accum_out=place_f[:, s, g:g + 1])
                        if g % 2:
                            mm.then_inc(so["place_found"], 1)
                    dve.wait_ge(so["place_found"], 2 * t.n + 2)
                    wait(dve, so["scattered"][s], 64 * t.turn(2))
                    dve.tensor_copy(place_i[:, s, :], place_f[:, s, :]).then_inc(so["place_ready"], 1)

                def filter_rows(t):
                    s = t.slot(2)
                    wait(dve, so["scattered"][s], 64 * t.turn(2))
                    for j in range(2):
                        dve.wait_ge(so["filt_bank"], 2 * t.n + j + 1)
                        dve.tensor_tensor(pay_t[:, s, 2 * j:2 * j + 2, 0:D],
                                          filt_bank[j][:, :].rearrange("p (g d) -> p g d", g=2),
                                          rows_b[:, 3:4, :].to_broadcast([P, 2, D]), ALU.add).then_inc(so["filt"], 1)

                pipeline(dve, NT, 2, [(2, read_table), (1, prepare_high), (0, tile_parts(so, "parts_s", "ready")),
                                      (3, find_place), (1, prepare)] + [(2, filter_rows)] * (a == 0))

            split(0, sort_s[0])
            sort(0, sort_s[0])
            dve.tensor_tensor(inversions[:, :], key_i[:, 1, :], next_dst[:, :], ALU.is_gt).then_inc(s_order, 1)
            dve.wait_ge(s_order, 1)
            dve.tensor_reduce(out_of_order[:, 0:1], inversions[:, :], mybir.AxisListType.X, ALU.add).then_inc(s_order, 1)
            dve.wait_ge(s_order_pe, 1)
            dve.tensor_scalar(out_of_order_i[:, 0:1], bank[7][:, 0:1], 1.0, None, ALU.min).then_inc(s_order, 1)

            def ends(t, L, other, n):
                q = t.slot(4)
                wait(dve, L["gathered"][t.slot(2)], 64 * n * (t.turn(2) - 1))
                dve.wait_ge(L["edges_in"][q], 32 * t.turn(4) + 32)
                dve.tensor_copy(ends_i[:, q, 0:n, :],
                                edge[:, q, :, other:other + n].rearrange("p g n -> p n g")).then_inc(L["ends"], 1)

            def tails(t, L, key):
                q = t.slot(4)
                if L is l1:
                    wait(dve, L["stored"][t.slot(2)], 64 * (t.turn(2) - 1))
                dve.wait_ge(L["edges_in"][q], 32 * t.turn(4) + 32)
                dve.tensor_tensor(goes_on[:, q, :], edge[:, q, :, key], next_key[:, q, :],
                                  ALU.is_equal).then_inc(L["tail_step"], 1)
                dve.wait_ge(L["tail_step"], 2 * t.n + 1)
                dve.scalar_tensor_tensor(out=tail_f[:, q, :], in0=goes_on[:, q, :], scalar=SKIP, in1=edge[:, q, :, key],
                                         op0=ALU.mult, op1=ALU.add).then_inc(L["tail_step"], 1)
                dve.wait_ge(L["tail_step"], 2 * t.n + 2)
                dve.tensor_scalar(is_last[:, q, :], tail_f[:, q, :], N - 0.5, None, ALU.is_lt)
                dve.tensor_copy(tail_i[:, q, :], tail_f[:, q, :]).then_inc(L["tails"], 1)

            L = l0
            dve.memset(acc_d[:, :, :], 0.0)
            dve.memset(acc_q[:, :, :], 0.0).then_inc(s_vector, 1)
            dve.wait_ge(s_last, 16 * 3)
            dve.wait_ge(s_wt, 1)
            dve.tensor_copy(node_row, last_edge[:, :])
            dve.wait_ge(s_vector, 6)

            def d_and_stats(t):
                s, q = t.slot(2), t.slot(4)
                wait(dve, L["stored"][s], 16 * t.turn(2))
                wait(dve, L["sq"], 4 * (t.n - 1))
                for j in range(2):
                    dve.wait_ge(L["h_bank"], 2 * t.n + j + 1)
                    dve.tensor_tensor(d_rows[:, s, 2 * j:2 * j + 2, :],
                                      bank[2 + j][:, :].rearrange("p (g d) -> p g d", g=2),
                                      shift[:, :].rearrange("p (a d) -> p a d", a=1).to_broadcast([P, 2, D]),
                                      ALU.add).then_inc(L["d"], 1)
                wait(dve, L["stats"], t.n)
                for g in range(SUB):
                    if g % 2 == 0:
                        dve.wait_ge(L["d"], 2 * t.n + g // 2 + 1)
                    dve.scalar_tensor_tensor(out=acc_d[:, g, :], in0=d_rows[:, s, g, :], scalar=is_last[:, q, g:g + 1],
                                             in1=acc_d[:, g, :], op0=ALU.mult, op1=ALU.add)
                dve.wait_ge(L["sq"], 4 * (t.n + 1))
                dve.tensor_tensor(acc_q[:, :, :], acc_q[:, :, :], sq[:, s, :, :], ALU.add).then_inc(L["stats"], 1)

            def message_rows(t):
                s = t.slot(2)
                dve.wait_ge(L["gathered"][s], 64 * t.turn(2) + 64)
                dve.wait_ge(L["edges_in"][t.slot(4)], 32 * t.turn(4) + 32)
                dve.tensor_tensor(gathered[:, s, :, :], gathered[:, s, :, :], edge[:, t.slot(4), :, 0:D],
                                  ALU.mult).then_inc(L["msg"], 1)

            def sum_messages(t):
                s = t.slot(2)
                wait(dve, L["z_bank"], 2 * (t.n - 1))
                if not (t.k is None and t.c == 0):
                    dve.wait_ge(L["agg"], 2 * t.n)
                dve.wait_ge(L["same_row"], t.n + 1)
                for c in range(KC):
                    dve.wait_ge(L["msg_bank"], 2 * t.n + c + 1)
                    first = 0.0 if t.k is None and t.c == 0 else agg[:, 1 - s, c, TE - 1:TE]
                    dve.tensor_tensor_scan(agg[:, s, c, :], same_row[:, s, 0:TE], bank[5 + c][:, :], first, ALU.mult,
                                           ALU.add).then_inc(L["agg"], 1)

            pipeline(dve, NT, 4, [(0, lambda t: ends(t, L, OTHER0, 1)), (2, sum_messages), (1, message_rows),
                                  (4, d_and_stats), (0, lambda t: tails(t, L, KEY0))])

            def node_index(t, rows=P, r=R):
                dve.tensor_copy(node_i[0:rows, t.slot(SLOTS), 0:r],
                                node_row[0:rows, bass.ds(t.n * R, r)]).then_inc(nd["index"], 1)

            for c in range(AHEAD):
                node_index(Tile(c))

            steps = [0]

            def bn(ins):
                steps[0] += 1
                ins.then_inc(s_bn, 1)
                dve.wait_ge(s_bn, steps[0])

            dve.wait_ge(s_sum, 1)
            bn(dve.tensor_scalar(bn_sum[:, :, :], bank[7][:, :].rearrange("p (j d) -> p j d", j=2), 1.0 / N, None, ALU.mult))
            bn(dve.tensor_tensor(bn_mean[:, :], bn_sum[:, 0, :], bn_sum[:, 0, :], ALU.mult))
            bn(dve.tensor_tensor(bn_mean[:, :], bn_sum[:, 1, :], bn_mean[:, :], ALU.subtract))
            bn(dve.tensor_scalar(bn_mean[:, :], bn_mean[:, :], 0.0, EPS, ALU.max, ALU.add))
            dve.tensor_copy(bn_tmp[:, :], bn_mean[:, :]).then_inc(s_vector, 1)
            dve.wait_ge(s_bn_sd, 1)
            bn(dve.reciprocal(bn_tmp[:, :], bn_tmp[:, :]))
            bn(dve.tensor_tensor(bn_scale[:, :], bn_tmp[:, :], rows_b[:, 1, :], ALU.mult))
            bn(dve.tensor_tensor(bn_tmp[:, :], bn_sum[:, 0, :], bn_scale[:, :], ALU.mult))
            bn(dve.tensor_tensor(bn_shift[:, :], rows_b[:, 2, :], bn_tmp[:, :], ALU.subtract))

            def row_sums(of, t, s, rows=P, r=R):
                st = stats[0:rows, s, 0:r, :].rearrange("p r k -> p k r")
                mo = moment[0:rows, s, :, 0:r]
                dve.wait_ge(of["stats"], t.n + 1)
                dve.tensor_tensor(mo[:, 0, :], st[:, 1, :], st[:, 4, :], ALU.add)
                dve.tensor_tensor(mo[:, 1, :], st[:, 1, :], st[:, 4, :], ALU.subtract)
                dve.tensor_tensor(mo[:, 2, :], st[:, 2, :], st[:, 5, :], ALU.add).then_inc(of["moments"], 1)

            def row_square(of, t, s, rows=P, r=R):
                mo = moment[0:rows, s, :, 0:r]
                dve.wait_ge(of["moments"], 3 * t.n + 1)
                dve.scalar_tensor_tensor(out=mo[:, 3, :], in0=mo[:, 1, :], scalar=0.25, in1=mo[:, 1, :],
                                         op0=ALU.mult, op1=ALU.mult).then_inc(of["moments"], 1)

            def row_variance(of, t, s, rows=P, r=R):
                mo = moment[0:rows, s, :, 0:r]
                dve.wait_ge(of["moments"], 3 * t.n + 2)
                dve.scalar_tensor_tensor(out=mo[:, 4, :], in0=mo[:, 2, :], scalar=1.0 / D, in1=mo[:, 3, :],
                                         op0=ALU.mult, op1=ALU.add).then_inc(of["moments"], 1)

            def wide(v, rows, r):
                return v[0:rows, :].rearrange("p (a d) -> p a d", a=1).to_broadcast([rows, r, D])

            def node_scale(t, rows=P, r=R):
                s = t.slot(SLOTS)
                dr = node_d[0:rows, s, 0:r, :]
                dve.wait_ge(nd_gathered[s], 16 * R * t.turn(SLOTS) + 16 * r)
                dve.tensor_tensor(dr, dr, wide(bn_scale, rows, r), ALU.mult).then_inc(nd["z"], 1)

            def node_sum(t, rows=P, r=R):
                s = t.slot(SLOTS)
                xr, dr = node_x[0:rows, s, 0:r, :], node_d[0:rows, s, 0:r, :]
                dve.wait_ge(nd_in[s], 16 * t.turn(SLOTS) + 16)
                dve.wait_ge(nd["z"], 3 * t.n + 1)
                dve.scalar_tensor_tensor(out=dr, in0=xr, scalar=2.0, in1=dr, op0=ALU.mult, op1=ALU.add).then_inc(nd["z"], 1)

            def node_shift(t, rows=P, r=R):
                s = t.slot(SLOTS)
                dr = node_d[0:rows, s, 0:r, :]
                dve.wait_ge(nd["z"], 3 * t.n + 2)
                dve.tensor_tensor(dr, dr, wide(bn_shift, rows, r), ALU.add).then_inc(nd["z"], 1)

            def node_stats(t, rows=P, r=R):
                s = t.slot(SLOTS)
                dve.wait_ge(nd["z"], 3 * t.n + 3)
                for j in range(r):
                    mm = dve.bn_stats(stats[0:rows, s, j, :], node_d[0:rows, s, j, :])
                mm.then_inc(nd["stats"], 1)

            def node_spread(t, rows=P, r=R):
                s = t.slot(SLOTS)
                dve.wait_ge(nd["moments"], 3 * t.n + 3)
                dve.tensor_scalar(spread[0:rows, s, 0, 0:r], moment[0:rows, s, 4, 0:r], EPS, None, ALU.add)
                dve.tensor_scalar(spread[0:rows, s, 1, 0:r], moment[0:rows, s, 4, 0:r], 1.0 + EPS, EPS * EPS,
                                  ALU.mult, ALU.add).then_inc(nd["spread"], 1)

            def node_inverse(t, rows=P, r=R):
                s = t.slot(SLOTS)
                dve.wait_ge(nd["sd"], t.n + 1)
                dve.reciprocal(inv[0:rows, s, :, 0:r], sd[0:rows, s, :, 0:r]).then_inc(nd["inv"], 1)

            def node_negative(t, rows=P, r=R):
                s = t.slot(SLOTS)
                dve.wait_ge(nd["inv"], t.n + 1)
                for j in range(2):
                    mm = dve.scalar_tensor_tensor(out=neg[0:rows, s, j, 0:r], in0=moment[0:rows, s, 0, 0:r], scalar=-0.5,
                                                  in1=inv[0:rows, s, j, 0:r], op0=ALU.mult, op1=ALU.mult)
                mm.then_inc(nd["neg"], 1)

            def of_nodes(stage):
                return lambda t, rows=P, r=R: stage(nd, t, t.slot(SLOTS), rows, r)

            stages = [(0, lambda t: None if t.k is None and t.c < AHEAD else node_stage(node_index)(t))] + [
                (AHEAD + lag, node_stage(stage)) for lag, stage in (
                    (0, node_scale), (1, of_nodes(row_sums)), (2, node_inverse), (0, node_sum), (1, of_nodes(row_square)),
                    (2, node_negative), (0, node_shift), (1, of_nodes(row_variance)), (0, node_stats), (1, node_spread))]
            pipeline(dve, NN + 1, SLOTS, stages)

            with dve.If(dve.value_load(out_of_order_i[0:1, 0:1]) > 0):
                split(1, sort_s[1])
                sort(1, sort_s[1])

            M = l1
            dve.memset(same_row[:, 0, 0:1], 0.0).then_inc(s_const_v, 1)
            dve.wait_ge(s_const_v, 6)

            def last_rows(t):
                s = t.slot(2)
                wait(dve, M["rows"], t.n - 1)
                for j in range(2):
                    dve.wait_ge(M["best_bank"], 2 * t.n + j + 1)
                    dve.tensor_tensor(d_rows[:, s, 2 * j:2 * j + 2, :],
                                      bank[7 if j == 0 else 0][:, :].rearrange("p (g d) -> p g d", g=2),
                                      gathered2[:, t.slot(4), 2 * j:2 * j + 2, :], ALU.add).then_inc(M["sum"], 1)
                for g in range(SUB):
                    dve.wait_ge(M["sum"], 2 * t.n + g // 2 + 1)
                    mm = dve.bn_stats(stats[:, s, g, :], d_rows[:, s, g, :])
                mm.then_inc(M["stats"], 1)
                row_sums(M, t, s, P, SUB)
                row_square(M, t, s, P, SUB)
                row_variance(M, t, s, P, SUB)
                dve.wait_ge(M["moments"], 3 * t.n + 3)
                dve.tensor_scalar(spread[:, s, 0, 0:SUB], moment[:, s, 4, 0:SUB], EPS, None, ALU.add).then_inc(M["spread"], 1)
                dve.wait_ge(M["sd"], t.n + 1)
                dve.reciprocal(inv[:, s, 0, 0:SUB], sd[:, s, 0, 0:SUB]).then_inc(M["inv"], 1)
                dve.wait_ge(M["inv"], t.n + 1)
                dve.scalar_tensor_tensor(out=neg[:, s, 0, 0:SUB], in0=moment[:, s, 0, 0:SUB], scalar=-0.5,
                                         in1=inv[:, s, 0, 0:SUB], op0=ALU.mult, op1=ALU.mult).then_inc(M["neg"], 1)

            def max_edges(t):
                s = t.slot(2)
                wait(dve, M["best_bank"], 2 * (t.n - 1))
                dve.wait_ge(M["same_row"], t.n + 1)
                if not (t.k is None and t.c == 0):
                    dve.wait_ge(M["best"], 2 * t.n)
                for o in range(KC):
                    dve.wait_ge(M["e"], 2 * t.n + o + 1)
                    first = 0.0 if t.k is None and t.c == 0 else agg[:, 1 - s, o, TE - 1:TE]
                    dve.tensor_tensor_scan(agg[:, s, o, :], same_row[:, s, 0:TE], zt[:, s, o, :], first, ALU.mult,
                                           ALU.max).then_inc(M["best"], 1)

            pipeline(dve, NT, 4, [(0, lambda t: ends(t, M, OTHER1, 2)), (3, last_rows), (2, max_edges),
                                  (0, lambda t: tails(t, M, KEY1))])


_INS = ['x', 'src', 'dst', 'edge_attr_20', 'L0_gnn_Wf1', 'L0_gnn_bf1', 'L0_gnn_Wf2', 'L0_gnn_bf2', 'L0_gnn_Wu1',
        'L0_gnn_bu1', 'L0_gnn_Wu2', 'L0_gnn_bu2', 'L0_gnn_gamma', 'L0_gnn_beta', 'L1_gnn_theta_w', 'L1_gnn_theta_b',
        'L1_gnn_phi_w', 'L1_gnn_phi_b']
_OUTS = [((50000, 256), 'float32')]


def kernel(**inputs):
    import numpy as _np
    import concourse.bacc as _bacc
    from concourse import mybir as _mybir
    from concourse.bass_utils import run_bass_kernel_spmd as _run

    nc = _bacc.Bacc("TRN2", target_bir_lowering=False, num_devices=1)
    arrays, args = {}, []
    for name in _INS:
        a = _np.ascontiguousarray(inputs[name])
        arrays[f"in_{name}_dram"] = a
        args.append(nc.dram_tensor(f"in_{name}_dram", a.shape, _mybir.dt.from_np(a.dtype), kind="ExternalInput").ap())
    for i, (shape, dtype) in enumerate(_OUTS):
        dt = _mybir.dt.from_np(_np.dtype(dtype))
        args.append(nc.dram_tensor(f"out_{i}_dram", shape, dt, kind="ExternalOutput").ap())
    build(nc, *args)
    r = _run(nc, [arrays], core_ids=[0])
    return r.results[0]["out_0_dram"]
```
